# Optimizing a Trainium2 kernel written in Bass

```python
import numpy as np
import jax
import jax.numpy as jnp

def _softmax(x, axis=-1):
    return jax.nn.softmax(x, axis=axis)

def _gelu(x):
    return jax.nn.gelu(x, approximate=True)

def _silu(x):
    return jax.nn.silu(x)

def _sigmoid(x):
    return jax.nn.sigmoid(x)

def _layernorm(x, axis=-1, eps=1e-05):
    m = jnp.mean(x, axis=axis, keepdims=True)
    v = jnp.var(x, axis=axis, keepdims=True)
    return (x - m) / jnp.sqrt(v + eps)

def _scatter_add(tgt, idx, src, axis=0):
    return tgt.at[idx].add(src)

def _segment_sum(src, seg, n):
    return jax.ops.segment_sum(src, seg, n)
kernel_name = 'mk_gnn_ffn_d1_gnn_r8_b80fad'

def setup_inputs(seed: int=0):
    np.random.seed(seed)
    _w = jnp.asarray

    def _rec_inputs():
        import jax
        import jax.numpy as jnp
        _gk = jax.random.key(seed)
        x = -0.0003713 + 1 * jax.random.normal(jax.random.fold_in(_gk, 1), (6250, 256), jnp.float32)
        src = jax.random.randint(jax.random.fold_in(_gk, 2), (100000,), 0, 6250, jnp.int32)
        dst = jnp.minimum((6250 * jax.random.uniform(jax.random.fold_in(_gk, 3), (100000,)) ** 2.0).astype(jnp.int32), 49999)
        _o = jnp.argsort(dst, stable=True)
        src = src[_o]
        dst = dst[_o]
        return (x, src, dst)
    x, src, dst = _rec_inputs()

    def _L0_gnn_setup():
        import jax, jax.numpy as jnp
        import numpy as np
        N_NODES = 6250
        N_EDGES = 200000
        IN_FEATS = 256
        HIDDEN = 512
        OUT_FEATS = 256
        EPS = 0.0
        key = jax.random.key(seed)
        ks = jax.random.split(key, 6)
        x = jax.random.normal(ks[0], (N_NODES, IN_FEATS), dtype=jnp.float32)
        edge_row = jax.random.randint(ks[1], (N_EDGES,), 0, N_NODES, dtype=jnp.int32)
        edge_col = jax.random.randint(ks[2], (N_EDGES,), 0, N_NODES, dtype=jnp.int32)
        W1 = jax.random.uniform(ks[3], (IN_FEATS, HIDDEN), dtype=jnp.float32, minval=-1.0 / np.sqrt(IN_FEATS), maxval=1.0 / np.sqrt(IN_FEATS))
        b1 = jnp.zeros((HIDDEN,), dtype=jnp.float32)
        W2 = jax.random.uniform(ks[4], (HIDDEN, OUT_FEATS), dtype=jnp.float32, minval=-1.0 / np.sqrt(HIDDEN), maxval=1.0 / np.sqrt(HIDDEN))
        b2 = jnp.zeros((OUT_FEATS,), dtype=jnp.float32)
        return {'x': x, 'edge_row': edge_row, 'edge_col': edge_col, 'W1': W1, 'b1': b1, 'W2': W2, 'b2': b2}
    _L0_gnn_all = _L0_gnn_setup()
    _L0_gnn_in = {k: v for k, v in _L0_gnn_all.items() if k in ('W1', 'b1', 'W2', 'b2')}
    del _L0_gnn_all

    def _L0_ffn_setup():
        import jax, jax.numpy as jnp
        import numpy as np
        BN_EPS = 0.001

        def _bn(h, g, b, m, v):
            return g * (h - m) * jax.lax.rsqrt(v + BN_EPS) + b
        key = jax.random.key(seed)
        ks = jax.random.split(key, 8)
        B, F, Df = (256, 64, 256)
        E, H, D = (8, 256, 256)
        s1 = 1.0 / np.sqrt(Df)
        s2 = 1.0 / np.sqrt(H)
        return {'x': jax.random.normal(ks[0], (B, F, Df), jnp.float32), 'Wr': jax.random.normal(ks[1], (Df, E), jnp.float32) * s1, 'br': jnp.zeros((E,), jnp.float32), 'W1': jax.random.normal(ks[2], (E, Df, H), jnp.float32) * s1, 'b1': jnp.zeros((E, H), jnp.float32), 'g1': jnp.ones((E, H), jnp.float32), 'be1': jnp.zeros((E, H), jnp.float32), 'm1': jnp.zeros((E, H), jnp.float32), 'v1': jnp.ones((E, H), jnp.float32), 'W2': jax.random.normal(ks[3], (E, H, H), jnp.float32) * s2, 'b2': jnp.zeros((E, H), jnp.float32), 'g2': jnp.ones((E, H), jnp.float32), 'be2': jnp.zeros((E, H), jnp.float32), 'm2': jnp.zeros((E, H), jnp.float32), 'v2': jnp.ones((E, H), jnp.float32), 'Wo': jax.random.normal(ks[4], (E, H, D), jnp.float32) * s2, 'bo': jnp.zeros((E, D), jnp.float32)}
    _L0_ffn_all = _L0_ffn_setup()
    _L0_ffn_in = {k: v for k, v in _L0_ffn_all.items() if k in ('Wr', 'br', 'W1', 'b1', 'g1', 'be1', 'm1', 'v1', 'W2', 'b2', 'g2', 'be2', 'm2', 'v2', 'Wo', 'bo')}
    del _L0_ffn_all
    return {'x': x, 'src': src, 'dst': dst, 'L0_gnn_W1': _L0_gnn_in['W1'], 'L0_gnn_b1': _L0_gnn_in['b1'], 'L0_gnn_W2': _L0_gnn_in['W2'], 'L0_gnn_b2': _L0_gnn_in['b2'], 'L0_ffn_Wr': _L0_ffn_in['Wr'], 'L0_ffn_br': _L0_ffn_in['br'], 'L0_ffn_W1': _L0_ffn_in['W1'], 'L0_ffn_b1': _L0_ffn_in['b1'], 'L0_ffn_g1': _L0_ffn_in['g1'], 'L0_ffn_be1': _L0_ffn_in['be1'], 'L0_ffn_m1': _L0_ffn_in['m1'], 'L0_ffn_v1': _L0_ffn_in['v1'], 'L0_ffn_W2': _L0_ffn_in['W2'], 'L0_ffn_b2': _L0_ffn_in['b2'], 'L0_ffn_g2': _L0_ffn_in['g2'], 'L0_ffn_be2': _L0_ffn_in['be2'], 'L0_ffn_m2': _L0_ffn_in['m2'], 'L0_ffn_v2': _L0_ffn_in['v2'], 'L0_ffn_Wo': _L0_ffn_in['Wo'], 'L0_ffn_bo': _L0_ffn_in['bo']}

def reference(x, src, dst, L0_gnn_W1, L0_gnn_b1, L0_gnn_W2, L0_gnn_b2, L0_ffn_Wr, L0_ffn_br, L0_ffn_W1, L0_ffn_b1, L0_ffn_g1, L0_ffn_be1, L0_ffn_m1, L0_ffn_v1, L0_ffn_W2, L0_ffn_b2, L0_ffn_g2, L0_ffn_be2, L0_ffn_m2, L0_ffn_v2, L0_ffn_Wo, L0_ffn_bo):
    import jax
    import jax.numpy as jnp

    def _L0_gnn_ref(x, edge_row, edge_col, W1, b1, W2, b2):
        import jax, jax.numpy as jnp
        import numpy as np
        N_NODES = 6250
        N_EDGES = 200000
        IN_FEATS = 256
        HIDDEN = 512
        OUT_FEATS = 256
        EPS = 0.0
        agg = jax.ops.segment_sum(x[edge_col], edge_row, num_segments=N_NODES)
        h = agg + (1.0 + EPS) * x
        h = h @ W1 + b1
        out = h @ W2 + b2
        return out

    def _L0_ffn_ref(x, Wr, br, W1, b1, g1, be1, m1, v1, W2, b2, g2, be2, m2, v2, Wo, bo):
        import jax, jax.numpy as jnp
        import numpy as np
        BN_EPS = 0.001

        def _bn(h, g, b, m, v):
            return g * (h - m) * jax.lax.rsqrt(v + BN_EPS) + b
        feat = jnp.mean(x, axis=0)
        w = jax.nn.softmax(feat @ Wr + br, axis=-1)
        h = jnp.einsum('bfd,edh->bfeh', x, W1) + b1
        h = jax.nn.relu(_bn(h, g1, be1, m1, v1))
        h = jnp.einsum('bfeh,ehk->bfek', h, W2) + b2
        h = jax.nn.relu(_bn(h, g2, be2, m2, v2))
        y = jnp.einsum('bfeh,ehd->bfed', h, Wo) + bo
        return jnp.einsum('bfed,fe->bfd', y, w)
    x = x + _L0_gnn_ref(_layernorm(x, axis=-1), src, dst, L0_gnn_W1, L0_gnn_b1, L0_gnn_W2, L0_gnn_b2)
    x = x + _L0_ffn_ref(_layernorm(x, axis=-1)[None], L0_ffn_Wr, L0_ffn_br, L0_ffn_W1, L0_ffn_b1, L0_ffn_g1, L0_ffn_be1, L0_ffn_m1, L0_ffn_v1, L0_ffn_W2, L0_ffn_b2, L0_ffn_g2, L0_ffn_be2, L0_ffn_m2, L0_ffn_v2, L0_ffn_Wo, L0_ffn_bo)[0]
    return x

_drawn_inputs = setup_inputs


def setup_inputs(seed=0):
    import zlib

    import numpy as np

    out = dict(_drawn_inputs(seed))
    spreads = {'L0_gnn_b1': (0.0, 0.1),
     'L0_gnn_b2': (0.0, 0.1),
     'L0_ffn_br': (0.0, 0.398),
     'L0_ffn_b1': (0.0, 0.536),
     'L0_ffn_g1': (1.0, 0.2),
     'L0_ffn_be1': (0.0, 0.544),
     'L0_ffn_m1': (0.0, 0.526),
     'L0_ffn_v1': (1.0, 0.6),
     'L0_ffn_b2': (0.0, 0.381),
     'L0_ffn_g2': (1.0, 0.2),
     'L0_ffn_be2': (0.0, 0.4),
     'L0_ffn_m2': (0.0, 0.391),
     'L0_ffn_v2': (1.0, 0.6),
     'L0_ffn_bo': (0.0, 0.284)}
    factors = {}
    for name, (base, spread) in spreads.items():
        noise = np.random.default_rng([zlib.crc32(name.encode()), seed]).standard_normal(out[name].shape)
        drawn = base * np.exp(spread * noise) if base else spread * noise
        out[name] = jnp.asarray(drawn.astype(out[name].dtype))
    for name, factor in factors.items():
        out[name] = (out[name] * factor).astype(out[name].dtype)
    return out
```

```python
from contextlib import ExitStack

import concourse.bass as bass
from concourse import mybir

F32 = mybir.dt.float32
F16 = mybir.dt.float16
I32 = mybir.dt.int32
ALU = mybir.AluOpType
ACT = mybir.ActivationFunctionType
AX = mybir.AxisListType
ENG = mybir.EngineType

P = 128
N = 6250
D = 256
KD = D // P
HID = 512
KH = HID // P
E_EDGES = 100000
EX = 8
BINS = -(-N // P)
LAST = N - (BINS - 1) * P
NPAD = BINS * P

EP, EF = 125, 800
SW = 1024
NBLK = SW // P
TILES = -(-E_EDGES // P)
BOUND = TILES + BINS - 1
GT = 4
GROUPS = BINS // GT
EPC = 9
CPG = 8
assert EPC * CPG * BINS >= GT * BOUND and EPC * CPG * GROUPS >= BOUND and BINS == GROUPS * GT + 1
NENT = EPC * CPG * GROUPS
HE = NENT // 2
SLOTS = 2 * EPC
BITS = 13
MASK = (1 << BITS) - 1
KEYBASE = 0x20000000
PADKEY = KEYBASE | (MASK << BITS) | MASK
EPS_LN = 1e-5
EPS_BN = 1e-3
WS = 64.0

BN_NAMES = ["b1", "g1", "be1", "m1", "v1", "b2", "g2", "be2", "m2", "v2"]


def build(nc, x, src, dst, gW1, gb1, gW2, gb2, Wr, br, bn, W1, W2, Wo, bo, out):
    xn_dram = nc.dram_tensor("xn_hilo", (NPAD, 2 * D), F16, kind="Internal").ap()
    xb_dram = nc.dram_tensor("x_plus_bias", (NPAD, D), F32, kind="Internal").ap()
    with ExitStack() as ctx:
        def sb(name, shape, dt):
            return ctx.enter_context(nc.sbuf_tensor(name, shape, dt))

        def ps(name, shape, dt=F32):
            return ctx.enter_context(nc.psum_tensor(name, shape, dt))

        def sem(name):
            return ctx.enter_context(nc.semaphore(name))

        acc = sb("acc", [P, BINS, D], F32)
        accf = acc[:].rearrange("p b d -> p (b d)")
        wsp = [sb(f"wsplit{l}", [P, EX, KD, 2, D], F16) for l in range(3)]
        wrs = sb("wrs", [P, KD, 2, EX], F16)
        gbuf = sb("gbuf", [P, SLOTS, 2 * D], F16)
        onehot = sb("onehot", [P, 2, EPC, P], F16)
        dsti = sb("dsti", [P, NENT], I32)
        khalf = sb("khalf", [P, SW // 2], F32)
        idle = sb("idle", [P, 2], F32)
        idxc = sb("idxc", [P, 2, EPC], I32)
        srel = sb("srel", [P, NENT], F16)
        bofs = sb("bofs", [1, NENT], I32)
        ordi = sb("ordi", [1, 64], I32)
        W12 = sb("W12", [P, KD, D], F32)
        b12 = sb("b12", [P, D], F32)
        bosb = sb("bosb", [EX, D], F32)
        brb = sb("brb", [P, EX], F32)
        bns = sb("bns", [P, 2, 2 * EX], F32)
        bnt = sb("bnt", [P, 2, 2 * EX], F32)
        ident = sb("ident", [P, P], F32)
        iota_row = sb("iota_row", [P, P], F16)
        xt = sb("xt", [P, 2, GT, D], F32)
        hs = sb("hs", [P, GT, D], F32)
        hT = sb("hT", [P, KD, GT * P], F32)
        yT = sb("yT", [P, 2, KD, GT * P], F16)
        zz = sb("zz", [P, 2, 2, GT * P], F32)
        h1 = sb("h1", [P, 2, 2, KD, GT * P], F16)
        h2 = sb("h2", [P, 2, KD, GT * P], F16)
        stat = sb("stat", [P, GT, 6], F32)
        mv = sb("mv", [P, GT, 2], F32)
        sd = sb("sd", [P, GT], F32)
        rstd = sb("rstd", [P, GT], F32)
        nmr = sb("nmr", [P, GT], F32)
        lg = sb("lg", [P, GT, EX], F32)
        mx = sb("mx", [P, GT], F32)
        nmx = sb("nmx", [P, GT], F32)
        ew = sb("ew", [P, GT, EX], F32)
        es = sb("es", [P, GT], F32)
        er = sb("er", [P, GT], F32)
        wn = sb("wn", [P, GT, EX], F32)
        w64 = sb("w64", [P, GT, EX], F32)
        wT = sb("wT", [EX, GT * P], F32)
        wst = sb("wst", [P, 4, KD, D], F32)
        xst = sb("xst", [P, 2, D], F32)
        nst = sb("nst", [P, 4, 2 * D], F16)
        junk = sb("junk", [P, EF], F16)
        cntb = sb("cntb", [P, BINS + 1], F32)
        cnt = sb("cnt", [P, BINS + 1], F32)
        sums = sb("sums", [P, BINS], F32)
        nmean = sb("nmean", [P, BINS], F32)
        sqs = sb("sqs", [P, BINS], F32)
        xsd = sb("xsd", [P, BINS], F32)
        xrs = sb("xrs", [P, BINS], F32)
        xnm = sb("xnm", [P, BINS], F32)
        epsln = sb("epsln", [P, 1], F32)
        epsbn = sb("epsbn", [P, 1], F32)
        ones = sb("ones", [P, P], F32)
        pidx = sb("pidx", [P, 1], I32)
        gray = sb("gray", [P, 10], I32)
        sgn = sb("sgn", [P, 8], F32)
        pcoli = sb("pcoli", [P, NBLK], I32)
        pcol = sb("pcol", [P, NBLK], F32)
        iri = sb("iri", [P, P], I32)
        bcol = sb("bcol", [P, 1], F32)
        prm = sb("prm", [2 * EX, 10, P], F32)
        sm = sb("sm", [BINS, 16], F32)
        smi = sb("smi", [BINS, 8], I32)
        mb = sb("mb", [BINS, BINS], F32)
        Lm = sb("Lm", [BINS, BINS], F32)
        Rm = sb("Rm", [BINS, BINS], F32)
        bbc = sb("bbc", [BINS, P], F32)
        dbc = sb("dbc", [BINS, P], F32)
        br1 = sb("br1", [1, EX], F32)
        b2r = sb("b2r", [1, D], F32)
        b1c = sb("b1c", [P, KH], F32)
        dsg = hs[:].rearrange("p a d -> p (a d)")[:, 0:7 * P].rearrange("p (j q) -> p j q", q=P)
        keyf = [zz[:, i].rearrange("p h n -> p (h n)") for i in range(2)]
        keyi = [k.bitcast(I32) for k in keyf]
        edges = h1[:].rearrange("p a b k n -> p (a b k n)").bitcast(I32)[:, 0:2 * EF].rearrange("p (s n) -> p s n", s=2)
        srcf = wsp[2][:].rearrange("p e k h d -> p (e k h d)").bitcast(F32)[:, 0:EF]
        gb32 = gbuf[:].rearrange("p s d -> p (s d)").bitcast(F32)
        iotk = gb32[:, 0:NENT]
        tk = gb32[:, NENT:2 * NENT]
        bk = gb32[:, 2 * NENT:3 * NENT]
        Mm = gb32[:, 3 * NENT:4 * NENT]
        prw = gb32[0:2 * EX, 4 * NENT:4 * NENT + 8 * P].rearrange("p (l q n) -> p l q n", l=2, q=4)
        yt32 = yT[:].rearrange("p a k n -> p (a k n)").bitcast(F32)
        pat = yt32[:, 0:NENT]
        h132 = h1[:].rearrange("p a b k n -> p (a b k n)").bitcast(F32)
        Pm = [h132[:, i * NENT:(i + 1) * NENT] for i in range(2)]
        xt32 = xt[:].rearrange("p a t d -> p (a t d)")
        gw1 = xt32[:, 0:KD * HID].rearrange("p (k n) -> p k n", k=KD)
        gw2 = xt32[:, 1024:1024 + KH * D].rearrange("p (k n) -> p k n", k=KH)
        w1T = hT[:].rearrange("p k n -> p (k n)").rearrange("p (c n) -> p c n", c=KH)
        b1b = h2[:].rearrange("p a k n -> p (a k n)").bitcast(F32)[:, 0:KH * P].rearrange("p (c n) -> p c n", c=KH)

        PA = ps("PA", [P, 2, 512])
        PB = ps("PB", [P, 2, 512])
        PT = ps("PT", [P, 2, 512])
        PN = ps("PN", [P, 2, D])
        PL = ps("PL", [P, 2, D])

        def ent_ps(k):
            return PN[:, 0, :] if k % 2 == 0 else PT[:, 0, 0:D]

        def l3_ps(i):
            return PL[:, 0, :] if i % 2 == 0 else PT[:, 1, 0:D]

        s = {n: sem(n) for n in (
            "edges_in", "x_in", "gnnw_in", "small_in", "consts", "keys", "sorted_step", "turned", "diag",
            "srcf_ready", "counted", "x_summed", "nmean_ready", "x_squared", "var_ready", "xsd_ready", "xrs_ready",
            "xnm_ready", "xb_ready", "xn_ready", "xnhi_ready", "xnlo_ready", "xst_stored", "nst_stored0", "nst_stored1",
            "nst_stored2", "nst_stored3", "xst_stored1", "whi_ready", "wlo_ready",
            "prep_pe", "prep_dve", "prep_own", "bn_sqrt", "sched_dve", "sched_pe", "w12_ready", "b12_ready",
            "oh_ready", "w_scaled", "idx_ready", "ent_done", "acc_done",
            "xt_in0", "xt_in1", "hs_ready", "hT_done", "hT_sb", "lin_done", "x1_ready", "ln_dve", "sd_ready", "y_ready",
            "yT_done", "yhi_ready", "ylo_ready", "lg_done", "rt_dve", "ex_ready", "w_ready", "wT_done", "wT_sb",
            "bo_done", "bo_added", "l1_done", "l2_done", "l3_done", "z1_ready", "z2_ready", "lo1_ready", "lo2_ready",
            "y3_added", "out0", "out1", "ord_ready", "mem0")}
        wst_in = [sem(f"wst_in{i}") for i in range(4)]
        gat = [sem(f"gathered{i}") for i in range(SLOTS)]

        block = ctx.enter_context(nc.Block())
        NW = 3 * EX + 1

        def piece(n):
            if n == 3 * EX:
                return Wr.rearrange("(k p) e -> p k e", p=P), EX, wrs[:, :, 0, :], wrs[:, :, 1, :]
            l, e = n // EX, n % EX
            w = (W1, W2, Wo)[l]
            return w[e].rearrange("(k p) n -> p k n", p=P), D, wsp[l][:, e, :, 0, :], wsp[l][:, e, :, 1, :]

        @block.sync
        def _(sp):
            sp.dma_start(edges[0:EP, 0, :], src.rearrange("(p n) -> p n", p=EP)).then_inc(s["edges_in"], 16)
            sp.dma_start(edges[0:EP, 1, :], dst.rearrange("(p n) -> p n", p=EP)).then_inc(s["edges_in"], 16)
            sp.wait_ge(s["mem0"], 1)
            for c in range(4):
                sp.dma_start(acc[:, 12 * c:12 * c + 12, :], x[12 * c * P:(12 * c + 12) * P, :].rearrange(
                    "(t p) d -> p t d", p=P)).then_inc(s["x_in"], 16)
            sp.dma_start(acc[0:LAST, BINS - 1, :], x[(BINS - 1) * P:N, :]).then_inc(s["x_in"], 16)
            sp.dma_start(gw1, gW1.rearrange("(k p) n -> p k n", p=P)).then_inc(s["gnnw_in"], 16)
            sp.dma_start(gw2, gW2.rearrange("(k p) n -> p k n", p=P)).then_inc(s["gnnw_in"], 16)
            for j, a in enumerate(bn):
                sp.dma_start(prm[:, j, :], a.rearrange("e (k p) -> (e k) p", p=P)).then_inc(s["small_in"], 16)
            sp.dma_start(bosb[:], bo).then_inc(s["small_in"], 16)
            sp.dma_start(br1[:], br.rearrange("(a n) -> a n", a=1)).then_inc(s["small_in"], 16)
            sp.dma_start(b2r[:], gb2.rearrange("(a n) -> a n", a=1)).then_inc(s["small_in"], 16)
            with nc.allow_non_contiguous_dma(reason="512 biases, once"):
                sp.dma_start(b1c[:], gb1.rearrange("(c p) -> p c", p=P)).then_inc(s["small_in"], 16)
            for n in range(NW):
                w, width, _, _ = piece(n)
                if n >= 4:
                    sp.wait_ge(s["whi_ready"], n - 3)
                    sp.wait_ge(s["wlo_ready"], n - 3)
                sp.dma_start(wst[:, n % 4, :, 0:width], w).then_inc(wst_in[n % 4], 16)
            for t in range(BINS):
                sp.wait_ge(s["xb_ready"], t + 1)
                sp.dma_start(xb_dram[t * P:(t + 1) * P, :], xst[:, t % 2, :]).then_inc(s["xst_stored" if t % 2 == 0 else "xst_stored1"], 16)
            for t in range(BINS):
                sp.wait_ge(s["xnhi_ready"], t + 1)
                sp.wait_ge(s["xnlo_ready"], t + 1)
                sp.dma_start(xn_dram[t * P:(t + 1) * P, :], nst[:, t % 4, :]).then_inc(s[f"nst_stored{t % 4}"], 16)
            sp.wait_ge(s["xst_stored"], 16 * 25)
            sp.wait_ge(s["xst_stored1"], 16 * 24)
            sp.wait_ge(s["ord_ready"], 1)
            sp.wait_ge(s["prep_pe"], 3)

            def load_x(g, T, par):
                _, b = nc.values_load_multi_w_load_instructions(
                    ordi[0:1, bass.ds(g * GT, T)], engines=[ENG.SP], min_val=0, max_val=BINS - 1)
                for i in range(T):
                    sp.dma_start(xt[:, par, i, :], xb_dram[bass.ds(b[i] * P, P), :]).then_inc(s[f"xt_in{par}"], 16)

            def store(g, T, par):
                _, b = nc.values_load_multi_w_load_instructions(
                    ordi[0:1, bass.ds(g * GT, T)], engines=[ENG.SP], min_val=0, max_val=BINS - 1)
                sp.wait_ge(s["y3_added"], (g + 1) * (EX * GT) - (GT - T) * EX)
                for i in range(T):
                    sp.dma_start(out[bass.ds(b[i] * P, P), :], xt[:, par, i, :]).then_inc(s[f"out{par}"], 16)

            load_x(0, GT, 0)
            load_x(1, GT, 1)
            store(0, GT, 0)
            sp.wait_ge(s["out0"], 16 * GT)
            load_x(2, GT, 0)
            store(1, GT, 1)
            with sp.Fori(1, GROUPS // 2 - 1) as q:
                sp.wait_ge(s["out1"], q * (16 * GT))
                load_x(2 * q + 1, GT, 1)
                store(2 * q, GT, 0)
                sp.wait_ge(s["out0"], q * (16 * GT) + 16 * GT)
                load_x(2 * q + 2, GT, 0)
                store(2 * q + 1, GT, 1)
            sp.wait_ge(s["out1"], 16 * GT * (GROUPS // 2 - 1))
            load_x(GROUPS - 1, GT, 1)
            store(GROUPS - 2, GT, 0)
            sp.wait_ge(s["out0"], 16 * GT * (GROUPS // 2))
            load_x(GROUPS, 1, 0)
            store(GROUPS - 1, GT, 1)
            store(GROUPS, 1, 0)
            sp.wait_ge(s["out0"], 16 * (GT * (GROUPS // 2) + 1))
            sp.wait_ge(s["out1"], 16 * GT * (GROUPS // 2))

        @block.gpsimd
        def _(pool):
            c = [0]

            def step(ins):
                c[0] += 1
                ins.then_inc(s["consts"], 1)

            pool.memset(acc[:, BINS - 1, :], 0.0).then_inc(s["mem0"], 1)
            step(pool.memset(ident[:], 0.0))
            step(pool.iota(pidx[:], pattern=[[0, 1]], base=0, channel_multiplier=1))
            step(pool.iota(iri[:], pattern=[[1, P]], base=0, channel_multiplier=0))
            step(pool.iota(pcoli[:], pattern=[[1, NBLK]], base=0, channel_multiplier=NBLK))
            step(pool.memset(ones[:], 1.0))
            step(pool.memset(epsln[:], EPS_LN))
            step(pool.memset(epsbn[:], EPS_BN))
            step(pool.memset(cnt[:], 0.0))
            step(pool.iota(keyi[0][:, 0:BINS + 1], pattern=[[P, BINS + 1]], base=0, channel_multiplier=0))
            step(pool.iota(iotk.bitcast(I32), pattern=[[1, NENT]], base=0, channel_multiplier=0))
            pool.wait_ge(s["consts"], 10)
            step(pool.affine_select(out=ident[:], in_=ident[:], compare_op=ALU.not_equal, fill=1.0, base=0,
                                    pattern=[[-1, P]], channel_multiplier=1))
            step(pool.tensor_copy(iota_row[:], iri[:]))
            step(pool.tensor_copy(pcol[:], pcoli[:]))
            step(pool.tensor_copy(bcol[:], pidx[:]))
            step(pool.tensor_copy(tk, iotk.bitcast(I32)))
            step(pool.tensor_copy(nst[:, 0, 0:2 * (BINS + 1)].bitcast(F32), keyi[0][:, 0:BINS + 1]))
            pool.wait_ge(s["consts"], 16)
            step(pool.tensor_copy(iotk, tk))
            step(pool.tensor_scalar(cntb[:], nst[:, 0, 0:2 * (BINS + 1)].bitcast(F32), -1.0, 0.5, ALU.mult, ALU.add))
            for n in range(NW):
                _, width, hi, lo = piece(n)
                pool.wait_ge(s["whi_ready"], n + 1)
                part = wst[:, n % 4, :, 0:width]
                pool.tensor_scalar(part, part, WS, None, ALU.mult).then_inc(s["w_scaled"], 1)
                pool.wait_ge(s["w_scaled"], n + 1)
                pool.tensor_tensor(lo, part, hi, ALU.subtract).then_inc(s["wlo_ready"], 1)
            pool.wait_ge(s["x_summed"], BINS)
            pool.tensor_scalar(nmean[:], sums[:], -1.0 / D, None, ALU.mult).then_inc(s["nmean_ready"], 1)
            pool.wait_ge(s["b12_ready"], 1)
            for t in range(BINS):
                if t >= 2:
                    pool.wait_ge(s["xst_stored" if t % 2 == 0 else "xst_stored1"], 16 * (t // 2))
                pool.tensor_tensor(xst[:, t % 2, :], acc[:, t, :], b12[:], ALU.add).then_inc(s["xb_ready"], 1)
            pool.wait_ge(s["xrs_ready"], 1)
            pool.wait_ge(s["nmean_ready"], 1)
            pool.tensor_tensor(xnm[:], nmean[:], xrs[:], ALU.mult).then_inc(s["xnm_ready"], 1)
            for t in range(BINS):
                pool.wait_ge(s["xnhi_ready"], t + 1)
                pool.tensor_tensor(nst[:, t % 4, D:2 * D], acc[:, t, :], nst[:, t % 4, 0:D],
                                   ALU.subtract).then_inc(s["xnlo_ready"], 1)
            for i in range(4):
                pool.wait_ge(s[f"nst_stored{i}"], 16 * ((BINS - 1 - i) // 4 + 1))
            pool.wait_ge(s["ord_ready"], 1)

            def gathers(c2, par, wait):
                if wait:
                    pool.wait_ge(s["ent_done"], c2 * SLOTS + EPC * (par - 1))
                    pool.nop(nofuse=True)
                pool.tensor_copy(idxc[:, par, :], dsti[:, bass.ds(c2 * SLOTS + par * EPC, EPC)]).then_inc(s["idx_ready"], 1)
                pool.wait_ge(s["idx_ready"], c2 * 2 + (par + 1))
                pool.nop(nofuse=True)
                for m in range(EPC):
                    pool.indirect_dma_start(gbuf[:, par * EPC + m, :], None, xn_dram,
                                            bass.IndirectOffsetOnAxis(idxc[:, par, m:m + 1], 0)).then_inc(
                        gat[par * EPC + m], 16)

            gathers(0, 0, False)
            gathers(0, 1, False)
            with pool.Fori(1, NENT // SLOTS) as c2:
                gathers(c2, 0, True)
                gathers(c2, 1, True)

        @block.scalar
        def _(act):
            act.wait_ge(s["srcf_ready"], 1)
            act.wait_ge(s["consts"], 18)
            for b in range(BINS + 1):
                if b:
                    act.wait_ge(s["counted"], b)
                nc.scalar.activation(junk[0:EP, :], srcf[0:EP, :], ACT.Sign, bias=cntb[0:EP, b:b + 1],
                                     accum_out=cnt[0:EP, b:b + 1]).then_inc(s["counted"], 1)
            act.wait_ge(s["small_in"], 16 * 14)
            for l in range(2):
                nc.scalar.activation(prw[:, l, 0, :], prm[:, 5 * l + 4, :], ACT.Sqrt,
                                     bias=epsbn[0:2 * EX, :]).then_inc(s["bn_sqrt"], 1)
            act.wait_ge(s["x_in"], 16 * 5)
            jk = junk[:, 0:D]
            for t in range(BINS):
                if t:
                    act.wait_ge(s["x_summed"], t)
                else:
                    act.wait_ge(s["counted"], BINS + 1)
                nc.scalar.activation(jk, acc[:, t, :], ACT.Copy, accum_out=sums[:, t:t + 1]).then_inc(s["x_summed"], 1)
            for n in range(NW):
                _, width, hi, _ = piece(n)
                act.wait_ge(wst_in[n % 4], 16 * (n // 4 + 1))
                nc.scalar.activation(hi, wst[:, n % 4, :, 0:width], ACT.Copy, scale=WS).then_inc(s["whi_ready"], 1)
            act.wait_ge(s["nmean_ready"], 1)
            for t in range(BINS):
                if t:
                    act.wait_ge(s["x_squared"], t)
                else:
                    act.wait_ge(s["x_summed"], BINS)
                nc.scalar.activation(jk, acc[:, t, :], ACT.Square, bias=nmean[:, t:t + 1],
                                     accum_out=sqs[:, t:t + 1]).then_inc(s["x_squared"], 1)
            act.wait_ge(s["x_squared"], BINS)
            nc.scalar.activation(xsd[:], sqs[:], ACT.Sqrt, bias=epsln[:], scale=1.0 / D).then_inc(s["xsd_ready"], 1)
            act.wait_ge(s["xnm_ready"], 1)
            act.wait_ge(s["xb_ready"], BINS)
            for t in range(BINS):
                nc.scalar.activation(acc[:, t, :], acc[:, t, :], ACT.Identity, bias=xnm[:, t:t + 1],
                                     scale=xrs[:, t:t + 1]).then_inc(s["xn_ready"], 1)
                if t >= 4:
                    act.wait_ge(s[f"nst_stored{t % 4}"], 16 * (t // 4))
                act.wait_ge(s["xn_ready"], t + 1)
                nc.scalar.activation(nst[:, t % 4, 0:D], acc[:, t, :], ACT.Copy).then_inc(s["xnhi_ready"], 1)

            def group(g, T, first):
                w = T * P
                if T == GT:
                    act.wait_ge(s["acc_done"], (g + 1) * (EPC * CPG))
                if first:
                    act.wait_ge(s["ord_ready"], 1)
                    act.wait_ge(s["xnlo_ready"], BINS)
                _, b = nc.values_load_multi_w_load_instructions(
                    ordi[0:1, bass.ds(g * GT, T)], engines=[ENG.Activation], min_val=0, max_val=BINS - 1)
                if not first:
                    act.wait_ge(s["yT_done"], g)
                for i in range(T):
                    nc.scalar.activation(hs[:, i, :], accf[:, bass.ds(b[i] * D, D)], ACT.Copy).then_inc(s["hs_ready"], 1)
                act.wait_ge(s["hT_done"], g + 1)
                if not first:
                    act.wait_ge(s["lin_done"], g)
                for k in range(KD):
                    nc.scalar.activation(hT[:, k, 0:w], PT[:, k, 0:w], ACT.Copy).then_inc(s["hT_sb"], 1)
                act.wait_ge(s["ln_dve"], g * 2 + 1)
                nc.scalar.activation(sd[:, 0:T], mv[:, 0:T, 1], ACT.Sqrt, bias=epsln[:]).then_inc(s["sd_ready"], 1)
                act.wait_ge(s["ln_dve"], g * 2 + 2)
                act.wait_ge(s["hT_done"], g + 1)
                for i in range(T):
                    nc.scalar.activation(hs[:, i, :], xtg(g, i), ACT.Identity, bias=nmr[:, i:i + 1],
                                         scale=rstd[:, i:i + 1]).then_inc(s["y_ready"], 1)
                act.wait_ge(s["yT_done"], g + 1)
                if not first:
                    act.wait_ge(s["l1_done"], g * 2 * EX)
                for k in range(KD):
                    nc.scalar.activation(yT[:, 0, k, 0:w], PT[:, k, 0:w], ACT.Copy).then_inc(s["yhi_ready"], 1)
                z1(g, 0, T, first)
                act.wait_ge(s["rt_dve"], g + 1)
                for i in range(T):
                    nc.scalar.activation(ew[:, i, :], lg[:, i, :], ACT.Exp, bias=nmx[:, i:i + 1],
                                         accum_out=es[:, i:i + 1]).then_inc(s["ex_ready"], 1)
                act.wait_ge(s["wT_done"], g + 1)
                nc.scalar.activation(wT[:, 0:w], PT[0:EX, 0, 0:w], ACT.Copy).then_inc(s["wT_sb"], 1)
                for e in range(EX):
                    if e + 1 < EX:
                        z1(g, e + 1, T, first)
                    z2(g, e, T, first)

            def xtg(g, i):
                return xt[:, par[0], i, :]

            par = [0]

            def z1(g, e, T, first):
                w = T * P
                for h in range(2):
                    act.wait_ge(s["l1_done"], g * 2 * EX + 2 * e + h + 1)
                    if not (first and e < 2):
                        act.wait_ge(s["l2_done"], g * 2 * EX + 2 * (e - 1))
                    if not (first and e == 0):
                        act.wait_ge(s["lo1_ready"], g * 2 * EX + 2 * (e - 1) + h + 1)
                    sc, sh = bns[:, 0, 2 * e + h:2 * e + h + 1], bnt[:, 0, 2 * e + h:2 * e + h + 1]
                    nc.scalar.activation(h1[:, e % 2, 0, h, 0:w], PA[:, h, 0:w], ACT.Relu, bias=sh, scale=sc)
                    nc.scalar.activation(zz[:, 0, h, 0:w], PA[:, h, 0:w], ACT.Relu, bias=sh,
                                         scale=sc).then_inc(s["z1_ready"], 1)

            def z2(g, e, T, first):
                w = T * P
                for h in range(2):
                    act.wait_ge(s["l2_done"], g * 2 * EX + 2 * e + h + 1)
                    if not (first and e == 0):
                        act.wait_ge(s["l3_done"], (g * EX + e) * GT - (GT - T) * e)
                        act.wait_ge(s["lo2_ready"], g * 2 * EX + 2 * (e - 1) + h + 1)
                    sc, sh = bns[:, 1, 2 * e + h:2 * e + h + 1], bnt[:, 1, 2 * e + h:2 * e + h + 1]
                    nc.scalar.activation(h2[:, 0, h, 0:w], PB[:, h, 0:w], ACT.Relu, bias=sh, scale=sc)
                    nc.scalar.activation(zz[:, 1, h, 0:w], PB[:, h, 0:w], ACT.Relu, bias=sh,
                                         scale=sc).then_inc(s["z2_ready"], 1)

            par[0] = 0
            group(0, GT, True)
            par[0] = 1
            group(1, GT, False)
            with act.Fori(1, GROUPS // 2) as q:
                for pp in range(2):
                    par[0] = pp
                    group(2 * q + pp, GT, False)
            par[0] = 0
            group(GROUPS, 1, False)

        @block.vector
        def _(dve):
            V = nc.vector
            V.memset(keyi[1], PADKEY).then_inc(s["keys"], 1)
            dve.wait_ge(s["consts"], 18)
            V.memset(keyi[0], PADKEY).then_inc(s["keys"], 1)
            V.tensor_scalar(gray[:, 0:1], pidx[:], 1, None, ALU.logical_shift_right).then_inc(s["diag"], 1)
            dve.wait_ge(s["edges_in"], 32)
            dve.wait_ge(s["keys"], 2)
            V.tensor_copy(srcf[0:EP, :], edges[0:EP, 0, :]).then_inc(s["srcf_ready"], 1)
            V.tensor_scalar(keyi[0][0:EP, 0:EF], edges[0:EP, 0, :], BITS, None,
                            ALU.logical_shift_left).then_inc(s["keys"], 1)
            dve.wait_ge(s["keys"], 3)
            V.tensor_tensor(keyi[0][0:EP, 0:EF], keyi[0][0:EP, 0:EF], edges[0:EP, 1, :],
                            ALU.bitwise_or).then_inc(s["keys"], 1)
            dve.wait_ge(s["keys"], 4)
            V.tensor_scalar(keyi[0][0:EP, 0:EF], keyi[0][0:EP, 0:EF], KEYBASE, None,
                            ALU.bitwise_or).then_inc(s["keys"], 1)
            dve.wait_ge(s["diag"], 1)
            V.tensor_tensor(gray[:, 1:2], gray[:, 0:1], pidx[:], ALU.bitwise_xor).then_inc(s["diag"], 1)
            V.tensor_scalar(gray[:, 2:3], pidx[:], 1, None, ALU.bitwise_and).then_inc(s["diag"], 1)
            dve.wait_ge(s["diag"], 3)
            for j in range(7):
                V.tensor_scalar(gray[:, 3 + j:4 + j], gray[:, 1:2], j, 1, ALU.logical_shift_right,
                                ALU.bitwise_and).then_inc(s["diag"], 1)
            dve.wait_ge(s["diag"], 10)
            V.tensor_scalar(sgn[:], gray[:, 2:10], -2.0, 1.0, ALU.mult, ALU.add).then_inc(s["diag"], 1)
            dve.wait_ge(s["diag"], 11)
            for j in range(7):
                V.tensor_scalar(dsg[:, j, :], ident[:], sgn[:, 1 + j:2 + j], None, ALU.mult).then_inc(s["diag"], 1)
            dve.wait_ge(s["keys"], 5)
            def prep():
                np_ = [0]

                def own(ins, wait=True):
                    np_[0] += 1
                    ins.then_inc(s["prep_own"], 1)
                    if wait:
                        dve.wait_ge(s["prep_own"], np_[0])

                dve.wait_ge(s["small_in"], 16 * 14)
                for c in range(KH):
                    own(V.tensor_scalar(b1b[:, c, :], ones[:], b1c[:, c:c + 1], None, ALU.mult), False)
                dve.wait_ge(s["prep_pe"], 1)
                own(V.tensor_copy(w1T.rearrange("p c n -> p (c n)"), PT[:].rearrange("p a n -> p (a n)")))
                V.memset(mb[0:1, 0:1], 0.0).then_inc(s["prep_dve"], 1)
                dve.wait_ge(s["bn_sqrt"], 2)
                for l in range(2):
                    b_, g_, be_, m_ = [prm[:, 5 * l + i, :] for i in range(4)]
                    own(V.reciprocal(prw[:, l, 1, :], prw[:, l, 0, :]))
                    own(V.tensor_tensor(prw[:, l, 1, :], prw[:, l, 1, :], g_, ALU.mult), False)
                    own(V.tensor_tensor(prw[:, l, 0, :], b_, m_, ALU.subtract))
                    own(V.tensor_scalar(prw[:, l, 2, :], prw[:, l, 1, :], 1.0 / WS, None, ALU.mult), False)
                    own(V.tensor_tensor(prw[:, l, 3, :], prw[:, l, 0, :], prw[:, l, 1, :], ALU.mult))
                    own(V.tensor_tensor(prw[:, l, 3, :], prw[:, l, 3, :], be_, ALU.add))
                dve.wait_ge(s["prep_pe"], 2)
                own(V.tensor_copy(W12[:], PN[:]))
                own(V.tensor_copy(brb[:], PL[:, 1, 0:EX]))
                V.tensor_copy(b12[:], PL[:, 0, :]).then_inc(s["b12_ready"], 1)
                dve.wait_ge(s["b12_ready"], 1)
                V.memset(mb[0:1, 0:1], 0.0).then_inc(s["prep_dve"], 1)
                dve.wait_ge(s["prep_pe"], 3)
                for l in range(2):
                    own(V.tensor_copy(bns[:, l, :], PT[:, 0, 32 * l:32 * l + 16]))
                    own(V.tensor_copy(bnt[:, l, :], PT[:, 0, 32 * l + 16:32 * l + 32]))

            cnt_ = [0]
            cur = [0]

            def compare(a_lo, a_hi, o_lo, o_hi, from_psum=False):
                if from_psum:
                    size = a_hi.shape[2]
                    sbuf_hi = khalf[:].rearrange("p (b m) -> p b m", m=size)
                    V.tensor_copy(sbuf_hi, a_hi).then_inc(s["sorted_step"], 1)
                    cnt_[0] += 1
                    dve.wait_ge(s["sorted_step"], cnt_[0])
                    a_hi = sbuf_hi
                V.tensor_tensor(o_lo, a_lo, a_hi, ALU.min).then_inc(s["sorted_step"], 1)
                V.tensor_tensor(o_hi, a_hi, a_lo, ALU.max).then_inc(s["sorted_step"], 1)
                cnt_[0] += 2
                dve.wait_ge(s["sorted_step"], cnt_[0])

            def halves(src_, dst_, width, m, mirror, from_psum=False):
                a = src_[:, 0:width].rearrange("p (b m) -> p b m", m=m)
                o = dst_[:, 0:width].rearrange("p (b m) -> p b m", m=m)
                h = m // 2
                if mirror:
                    V.tensor_tensor(o[:, :, 0:h], a[:, :, 0:h], a[:, :, m - 1:h - 1:-1], ALU.min).then_inc(s["sorted_step"], 1)
                    hi_lo = a[:, :, h - 1::-1] if h > 1 else a[:, :, 0:1]
                    V.tensor_tensor(o[:, :, h:m], a[:, :, h:m], hi_lo, ALU.max).then_inc(s["sorted_step"], 1)
                    cnt_[0] += 2
                    dve.wait_ge(s["sorted_step"], cnt_[0])
                else:
                    compare(a[:, :, 0:h], a[:, :, h:m], o[:, :, 0:h], o[:, :, h:m], from_psum)

            for level in range(1, 11):
                m = 1 << level
                width = -(-EF // m) * m
                if level == 10:
                    V.tensor_scalar(keyf[1 - cur[0]], keyf[cur[0]], sgn[:, 0:1], None, ALU.mult).then_inc(s["sorted_step"], 1)
                    cnt_[0] += 1
                    dve.wait_ge(s["sorted_step"], cnt_[0])
                    cur[0] = 1 - cur[0]
                d = m
                while d >= 2:
                    halves(keyf[cur[0]], keyf[1 - cur[0]], width, d, d == m)
                    cur[0] = 1 - cur[0]
                    d //= 2
            pa, pb = [x_[:].rearrange("p a n -> p (a n)") for x_ in (PA, PB)]
            turns = 0
            for j in range(1, 8):
                turns += 1
                dve.wait_ge(s["turned"], turns)
                srcb = pa
                for d in range(j, 0, -1):
                    a = srcb.rearrange("p (b m) -> p b m", m=1 << d)
                    o = keyf[1 - cur[0]].rearrange("p (b m) -> p b m", m=1 << d)
                    h = 1 << (d - 1)
                    compare(a[:, :, 0:h], a[:, :, h:2 * h], o[:, :, 0:h], o[:, :, h:2 * h], d == j)
                    cur[0] = 1 - cur[0]
                    srcb = keyf[cur[0]]
                turns += 1
                dve.wait_ge(s["turned"], turns)
                srcb = pb
                for d in range(10, 0, -1):
                    halves(srcb, keyf[1 - cur[0]], SW, 1 << d, False, d == 10)
                    cur[0] = 1 - cur[0]
                    srcb = keyf[cur[0]]
                if j == 3:
                    prep()
                if j == 5:
                    dve.wait_ge(s["xsd_ready"], 1)
                    V.reciprocal(xrs[:], xsd[:]).then_inc(s["xrs_ready"], 1)
            assert cur[0] == SORTED_IN and cnt_[0] == LOCAL_STEPS + 2 * 28 + 20 * 7 + 14

            dve.wait_ge(s["sched_pe"], 1)
            nS = [0]

            def st(ins, wait=True):
                nS[0] += 1
                ins.then_inc(s["sched_dve"], 1)
                if wait:
                    dve.wait_ge(s["sched_dve"], nS[0])

            st(V.tensor_scalar(smi[:, 0:2], PL[0:BINS, 0, 0:2], -0.5, E_EDGES / 2.0, ALU.mult, ALU.add))
            st(V.tensor_scalar(smi[:, 2:3], smi[:, 0:1], 7, None, ALU.logical_shift_right), False)
            st(V.tensor_scalar(sm[:, 0:1], smi[:, 1:2], 127.0, None, ALU.add))
            st(V.tensor_copy(smi[:, 3:4], sm[:, 0:1]))
            st(V.tensor_scalar(smi[:, 4:5], smi[:, 3:4], 7, None, ALU.logical_shift_right))
            st(V.tensor_copy(sm[:, 1:2], smi[:, 2:3]), False)
            st(V.tensor_copy(sm[:, 2:3], smi[:, 4:5]), False)
            st(V.memset(sm[:, 4:5], 1.0))
            st(V.tensor_tensor(sm[:, 3:4], sm[:, 2:3], sm[:, 1:2], ALU.subtract))
            st(V.scalar_tensor_tensor(out=sm[:, 5:6], in0=sm[:, 3:4], scalar=64.0, in1=bcol[0:BINS, :],
                                      op0=ALU.mult, op1=ALU.add))
            st(V.tensor_scalar(mb[:], ones[0:BINS, 0:BINS], sm[:, 5:6], None, ALU.mult))
            dve.wait_ge(s["sched_pe"], 2)
            st(V.tensor_scalar(Lm[:], PL[0:BINS, 0, 0:BINS], sm[:, 5:6], None, ALU.is_gt))
            SCHED_L = nS[0]
            dve.wait_ge(s["sched_pe"], 3)
            st(V.tensor_copy(sm[:, 6:8], PL[0:BINS, 1, 0:2]))
            st(V.tensor_tensor(sm[:, 8:9], sm[:, 6:7], sm[:, 3:4], ALU.add), False)
            st(V.tensor_tensor(sm[:, 9:10], sm[:, 1:2], sm[:, 6:7], ALU.subtract), False)
            st(V.tensor_scalar(Rm[:], iota_row[0:BINS, 0:BINS], sm[:, 7:8], None, ALU.is_equal), False)
            st(V.tensor_scalar(bbc[:], ones[0:BINS, :], bcol[0:BINS, :], None, ALU.mult))
            st(V.tensor_scalar(dbc[:], ones[0:BINS, :], sm[:, 9:10], None, ALU.mult), False)
            st(V.tensor_scalar(Mm[0:BINS, :], iotk[0:BINS, :], sm[:, 6:7], None, ALU.is_ge))
            st(V.scalar_tensor_tensor(out=Mm[0:BINS, :], in0=iotk[0:BINS, :], scalar=sm[:, 8:9],
                                      in1=Mm[0:BINS, :], op0=ALU.is_lt, op1=ALU.mult))
            assert nS[0] == SCHED_M, nS[0]
            dve.wait_ge(s["sched_pe"], 4)
            for i in range(2):
                st(V.tensor_copy(bk[:, i * HE:(i + 1) * HE], PA[:, i, 0:HE]), False)
                st(V.tensor_tensor(tk[:, i * HE:(i + 1) * HE], iotk[:, i * HE:(i + 1) * HE], PB[:, i, 0:HE], ALU.add), False)
            st(V.tensor_copy(ordi[0:1, 0:BINS], PL[0:1, 0, 0:BINS]))
            st(V.tensor_scalar(bofs[:], bk[0:1, :], float(D), None, ALU.mult), False)
            for blk in range(NBLK):
                if blk >= 2:
                    dve.wait_ge(s["sched_pe"], 4 + blk - 1)
                st(V.tensor_scalar(Pm[blk % 2], tk, pcol[:, blk:blk + 1], None, ALU.is_equal), False)
            assert nS[0] == SCHED_P, nS[0]
            dve.wait_ge(s["sched_pe"], 4 + NBLK)
            for i in range(2):
                st(V.tensor_copy(pat[:, i * HE:(i + 1) * HE], PA[:, i, 0:HE]), False)
            dve.wait_ge(s["sched_dve"], nS[0])
            pati = pat.bitcast(I32)
            st(V.tensor_scalar(tk.bitcast(I32), pati, BITS, MASK, ALU.logical_shift_right, ALU.bitwise_and), False)
            st(V.tensor_scalar(dsti[:], pati, MASK, None, ALU.bitwise_and))
            st(V.tensor_scalar(dsti[:], dsti[:], N - 1, None, ALU.min), False)
            st(V.tensor_copy(iotk, tk.bitcast(I32)))
            st(V.scalar_tensor_tensor(out=srel[:], in0=bk, scalar=-float(P), in1=iotk, op0=ALU.mult, op1=ALU.add))
            V.memset(mb[0:1, 0:1], 0.0).then_inc(s["ord_ready"], 1)

            def onehots(c2, par, wait):
                if wait:
                    dve.wait_ge(s["ent_done"], c2 * SLOTS + EPC * (par - 1))
                k = c2 * SLOTS + par * EPC
                V.tensor_tensor(onehot[:, par, :, :], iota_row[:].unsqueeze(1).broadcast_to([P, EPC, P]),
                                srel[:, bass.ds(k, EPC)].unsqueeze(2).broadcast_to([P, EPC, P]),
                                ALU.is_equal).then_inc(s["oh_ready"], 1)

            regs = [None]

            def load_bins(c2, par):
                _, regs[0] = nc.values_load_multi_w_load_instructions(
                    bofs[0:1, bass.ds(c2 * SLOTS + par * EPC, EPC)], engines=[ENG.DVE],
                    min_val=0, max_val=(BINS - 1) * D)

            def add_entries(c2, par, ms):
                for m in ms:
                    k = par * EPC + m
                    dve.wait_ge(s["ent_done"], c2 * SLOTS + (k + 1))
                    if not (isinstance(c2, int) and c2 * SLOTS + k == 0):
                        dve.wait_ge(s["acc_done"], c2 * SLOTS + k)
                    to = accf[:, bass.ds(regs[0][m], D)]
                    V.tensor_tensor(to, to, ent_ps(k), ALU.add).then_inc(s["acc_done"], 1)

            dve.wait_ge(s["ord_ready"], 1)
            dve.wait_ge(s["xnlo_ready"], BINS)

            def chunk_all(c2, wait):
                for par in range(2):
                    onehots(c2, par, wait)
                    load_bins(c2, par)
                    add_entries(c2, par, range(EPC))

            chunk_all(0, False)
            with dve.Fori(1, CPG // 2) as c2:
                chunk_all(c2, True)

            def group(g, T, par, chunks, first):
                w = T * P
                dve.wait_ge(s[f"xt_in{par}"], xt_need(g, par, T))
                for i in range(T):
                    dve.wait_ge(s["lin_done"], g + 1)
                    V.tensor_tensor(xt[:, par, i, :], xt[:, par, i, :], PB[:, i // 2, (i % 2) * D:(i % 2) * D + D],
                                    ALU.add).then_inc(s["x1_ready"], 1)
                for i in range(T):
                    dve.wait_ge(s["x1_ready"], X1G * g + i + 1)
                    V.bn_stats(stat[:, i, :], xt[:, par, i, :]).then_inc(s["x1_ready"], 1)
                dve.wait_ge(s["x1_ready"], X1G * g + 2 * T)
                V.memset(idle[:, 0:1], 0.0)
                for i in range(T):
                    V.bn_aggr(mv[:, i, :], stat[:, i, :]).then_inc(s["ln_dve" if i == T - 1 else "x1_ready"], 1)
                dve.wait_ge(s["sd_ready"], g + 1)
                V.reciprocal(rstd[:, 0:T], sd[:, 0:T]).then_inc(s["x1_ready"], 1)
                dve.wait_ge(s["x1_ready"], X1G * g + 3 * T)
                V.scalar_tensor_tensor(out=nmr[:, 0:T], in0=mv[:, 0:T, 0], scalar=-1.0, in1=rstd[:, 0:T],
                                       op0=ALU.mult, op1=ALU.mult).then_inc(s["ln_dve"], 1)
                for k in range(KD):
                    dve.wait_ge(s["yhi_ready"], g * KD + k + 1)
                    V.tensor_tensor(yT[:, 1, k, 0:w], PT[:, k, 0:w], yT[:, 0, k, 0:w],
                                    ALU.subtract).then_inc(s["ylo_ready"], 1)
                dve.wait_ge(s["lg_done"], g + 1)
                for i in range(T):
                    V.scalar_tensor_tensor(out=lg[:, i, :], in0=PL[:, 0, i * EX:(i + 1) * EX], scalar=1.0 / WS,
                                           in1=brb[:], op0=ALU.mult, op1=ALU.add).then_inc(s["x1_ready"], 1)
                dve.wait_ge(s["x1_ready"], X1G * g + 4 * T)
                V.tensor_reduce(mx[:, 0:T], lg[:, 0:T, :], AX.X, ALU.max).then_inc(s["x1_ready"], 1)
                dve.wait_ge(s["x1_ready"], X1G * g + 4 * T + 1)
                V.tensor_scalar(nmx[:, 0:T], mx[:, 0:T], -1.0, None, ALU.mult).then_inc(s["rt_dve"], 1)
                lo1(g, 0, T)
                dve.wait_ge(s["ex_ready"], g * GT + T)
                V.reciprocal(er[:, 0:T], es[:, 0:T]).then_inc(s["x1_ready"], 1)
                dve.wait_ge(s["x1_ready"], X1G * g + 4 * T + 2)
                for i in range(T):
                    V.tensor_scalar(wn[:, i, :], ew[:, i, :], er[:, i:i + 1], None, ALU.mult).then_inc(s["w_ready"], 1)
                dve.wait_ge(s["w_ready"], g * GT + T)
                V.tensor_scalar(w64[:, 0:T, :], wn[:, 0:T, :], 1.0 / WS, None, ALU.mult).then_inc(s["x1_ready"], 1)
                dve.wait_ge(s["bo_done"], g + 1)
                dve.wait_ge(s["x1_ready"], X1G * g + 4 * T + 3)
                for i in range(T):
                    V.tensor_tensor(xt[:, par, i, :], xt[:, par, i, :], PB[:, i // 2, (i % 2) * D:(i % 2) * D + D],
                                    ALU.add).then_inc(s["bo_added"], 1)
                dve.wait_ge(s["bo_added"], g * GT + T)
                for e in range(EX):
                    c2, cp = (g + 1) * (CPG // 2) + e // 2, e % 2
                    if chunks:
                        onehots(c2, cp, True)
                        load_bins(c2, cp)
                    if e + 1 < EX:
                        lo1(g, e + 1, T)
                    if chunks:
                        add_entries(c2, cp, range(0, 3))
                    lo2(g, e, T)
                    if chunks:
                        add_entries(c2, cp, range(3, 6))
                    for i in range(T):
                        n = (g * EX + e) * GT + i - (GT - T) * e
                        dve.wait_ge(s["l3_done"], n + 1)
                        if e:
                            dve.wait_ge(s["y3_added"], n - T + 1)
                        V.scalar_tensor_tensor(out=xt[:, par, i, :], in0=l3_ps(i), scalar=w64[:, i, e:e + 1],
                                               in1=xt[:, par, i, :], op0=ALU.mult, op1=ALU.add).then_inc(s["y3_added"], 1)
                    if chunks:
                        add_entries(c2, cp, range(6, 9))

            def lo1(g, e, T):
                w = T * P
                for h in range(2):
                    dve.wait_ge(s["z1_ready"], g * 2 * EX + 2 * e + h + 1)
                    V.tensor_tensor(h1[:, e % 2, 1, h, 0:w], zz[:, 0, h, 0:w], h1[:, e % 2, 0, h, 0:w],
                                    ALU.subtract).then_inc(s["lo1_ready"], 1)

            def lo2(g, e, T):
                w = T * P
                for h in range(2):
                    dve.wait_ge(s["z2_ready"], g * 2 * EX + 2 * e + h + 1)
                    V.tensor_tensor(h2[:, 1, h, 0:w], zz[:, 1, h, 0:w], h2[:, 0, h, 0:w],
                                    ALU.subtract).then_inc(s["lo2_ready"], 1)

            def xt_need(g, par, T):
                if isinstance(g, int):
                    return 16 * GT * ((g - par) // 2) + 16 * T
                return q_[0] * (16 * GT) + 16 * T

            q_ = [None]
            group(0, GT, 0, True, True)
            group(1, GT, 1, True, False)
            with dve.Fori(1, GROUPS // 2 - 1) as q:
                q_[0] = q
                group(2 * q, GT, 0, True, False)
                group(2 * q + 1, GT, 1, True, False)
            group(GROUPS - 2, GT, 0, True, False)
            group(GROUPS - 1, GT, 1, False, False)
            group(GROUPS, 1, 0, False, False)

        @block.tensor
        def _(pe):
            T_ = nc.tensor
            pa, pb = [x_[:].rearrange("p a n -> p (a n)") for x_ in (PA, PB)]

            def prep():
                pe.wait_ge(s["gnnw_in"], 32)
                pe.wait_ge(s["consts"], 18)
                for k in range(KD):
                    for c in range(KH):
                        last = T_.transpose(PT[:, c // 2, (c % 2) * D + k * P:(c % 2) * D + k * P + P],
                                            gw1[:, k, c * P:(c + 1) * P], ident[:])
                last.then_inc(s["prep_pe"], 1)
                pe.wait_ge(s["prep_dve"], 1)
                for m in range(KD):
                    for c in range(KH):
                        T_.matmul(PN[:, m, :], w1T[:, c, m * P:(m + 1) * P], gw2[:, c, :], start=c == 0, stop=c == KH - 1)
                pe.wait_ge(s["small_in"], 16 * 14)
                for c in range(KH):
                    T_.matmul(PL[:, 0, :], b1b[:, c, :], gw2[:, c, :], start=c == 0, stop=False)
                T_.matmul(PL[:, 0, :], ones[0:1, :], b2r[:], start=False, stop=True)
                T_.matmul(PL[:, 1, 0:EX], ones[0:1, :], br1[:], start=True, stop=True).then_inc(s["prep_pe"], 1)
                pe.wait_ge(s["prep_dve"], 2)
                for l in range(2):
                    for q in range(2):
                        last = T_.transpose(PT[:, 0, (2 * l + q) * 16:(2 * l + q) * 16 + 16], prw[:, l, 2 + q, :],
                                            ident[0:2 * EX, 0:2 * EX])
                last.then_inc(s["prep_pe"], 1)

            steps = LOCAL_STEPS
            cur = LOCAL_CUR
            pe.wait_ge(s["diag"], 18)
            for j in range(1, 8):
                pe.wait_ge(s["sorted_step"], steps)
                for b in range(NBLK):
                    last = T_.matmul(pa[:, b * P:(b + 1) * P], keyf[cur][:, b * P:(b + 1) * P], dsg[:, j - 1, :],
                                     start=True, stop=True)
                last.then_inc(s["turned"], 1)
                steps += 2 * j + 1
                cur = (cur + j) % 2
                pe.wait_ge(s["sorted_step"], steps)
                for b in range(NBLK):
                    last = T_.transpose(pb[:, b * P:(b + 1) * P], keyf[cur][:, b * P:(b + 1) * P], ident[:])
                last.then_inc(s["turned"], 1)
                if j == 3:
                    prep()
                steps += 21
            pe.wait_ge(s["sorted_step"], steps)
            pe.wait_ge(s["counted"], BINS + 1)
            T_.matmul(PL[0:BINS, 0, 0:1], cnt[:, 0:BINS], ones[:, 0:1], start=True, stop=True)
            T_.matmul(PL[0:BINS, 0, 1:2], cnt[:, 1:BINS + 1], ones[:, 0:1], start=True, stop=True).then_inc(s["sched_pe"], 1)
            pe.wait_ge(s["sched_dve"], 11)
            T_.matmul(PL[0:BINS, 0, 0:BINS], mb[:], ident[0:BINS, 0:BINS], start=True, stop=True).then_inc(s["sched_pe"], 1)
            pe.wait_ge(s["sched_dve"], 12)
            T_.matmul(PL[0:BINS, 1, 0:2], Lm[:], sm[:, 3:5], start=True, stop=True).then_inc(s["sched_pe"], 1)
            pe.wait_ge(s["sched_dve"], SCHED_M)
            for i in range(2):
                T_.matmul(PA[:, i, 0:HE], bbc[:], Mm[0:BINS, i * HE:(i + 1) * HE], start=True, stop=True)
                T_.matmul(PB[:, i, 0:HE], dbc[:], Mm[0:BINS, i * HE:(i + 1) * HE], start=True, stop=True)
            T_.matmul(PL[:, 0, 0:BINS], bbc[:], Rm[:], start=True, stop=True).then_inc(s["sched_pe"], 1)
            for blk in range(NBLK):
                pe.wait_ge(s["sched_dve"], SCHED_P - NBLK + blk + 1)
                for i in range(2):
                    last = T_.matmul(PA[:, i, 0:HE], keyf[SORTED_IN][:, blk * P:(blk + 1) * P],
                                     Pm[blk % 2][:, i * HE:(i + 1) * HE], start=blk == 0, stop=blk == NBLK - 1)
                last.then_inc(s["sched_pe"], 1)

            def entries(c2, par, ms, ready):
                if ready:
                    pe.wait_ge(s["oh_ready"], c2 * 2 + (par + 1))
                for m in ms:
                    k = par * EPC + m
                    pe.wait_ge(gat[k], c2 * 16 + 16)
                    if not (isinstance(c2, int) and c2 * SLOTS + k < 2):
                        pe.wait_ge(s["acc_done"], c2 * SLOTS + (k - 1))
                    T_.matmul(ent_ps(k), onehot[:, par, m, :], gbuf[:, k, 0:D], start=True, stop=False)
                    T_.matmul(ent_ps(k), onehot[:, par, m, :], gbuf[:, k, D:2 * D], start=False,
                              stop=True).then_inc(s["ent_done"], 1)

            for par in range(2):
                entries(0, par, range(EPC), True)
            with pe.Fori(1, CPG // 2) as c2:
                for par in range(2):
                    entries(c2, par, range(EPC), True)

            def group(g, T, chunks, first):
                w = T * P
                pe.wait_ge(s["hs_ready"], g * GT + T)
                if not first:
                    pe.wait_ge(s["y3_added"], g * GT * EX)
                for i in range(T):
                    for k in range(KD):
                        last = T_.transpose(PT[:, k, i * P:(i + 1) * P], hs[:, i, k * P:(k + 1) * P], ident[:])
                last.then_inc(s["hT_done"], 1)
                pe.wait_ge(s["hT_sb"], g * KD + KD)
                if not first:
                    pe.wait_ge(s["z2_ready"], g * 2 * EX)
                for i in range(T):
                    for k in range(KD):
                        last = T_.matmul(PB[:, i // 2, (i % 2) * D:(i % 2) * D + D], hT[:, k, i * P:(i + 1) * P],
                                         W12[:, k, :], start=k == 0, stop=k == KD - 1)
                last.then_inc(s["lin_done"], 1)
                pe.wait_ge(s["y_ready"], g * GT + T)
                for i in range(T):
                    for k in range(KD):
                        last = T_.transpose(PT[:, k, i * P:(i + 1) * P], hs[:, i, k * P:(k + 1) * P], ident[:])
                last.then_inc(s["yT_done"], 1)
                pe.wait_ge(s["yhi_ready"], g * KD + KD)
                pe.wait_ge(s["ylo_ready"], g * KD + KD)
                if not first:
                    pe.wait_ge(s["y3_added"], g * GT * EX)
                for i in range(T):
                    n = 0
                    for k in range(KD):
                        for wp, yp in PASSES:
                            last = T_.matmul(PL[:, 0, i * EX:(i + 1) * EX], yT[:, yp, k, i * P:(i + 1) * P],
                                             wrs[:, k, wp, :], start=n == 0, stop=n == 5)
                            n += 1
                last.then_inc(s["lg_done"], 1)
                L1(g, 0, w, first)
                pe.wait_ge(s["w_ready"], g * GT + T)
                for i in range(T):
                    last = T_.transpose(PT[0:EX, 0, i * P:(i + 1) * P], wn[:, i, :], ident[:])
                last.then_inc(s["wT_done"], 1)
                pe.wait_ge(s["wT_sb"], g + 1)
                for i in range(T):
                    last = T_.matmul(PB[:, i // 2, (i % 2) * D:(i % 2) * D + D], wT[:, i * P:(i + 1) * P], bosb[:],
                                     start=True, stop=True)
                last.then_inc(s["bo_done"], 1)
                for e in range(EX):
                    c2, cp = (g + 1) * (CPG // 2) + e // 2, e % 2
                    if e + 1 < EX:
                        L1(g, e + 1, w, first)
                    if chunks:
                        entries(c2, cp, range(0, 3), True)
                    if e == 0:
                        pe.wait_ge(s["bo_added"], g * GT + T)
                    L2(g, e, w, first)
                    if chunks:
                        entries(c2, cp, range(3, 6), False)
                    pe.wait_ge(s["z2_ready"], g * 2 * EX + 2 * e + 2)
                    pe.wait_ge(s["lo2_ready"], g * 2 * EX + 2 * e + 2)
                    for i in range(T):
                        m = (g * EX + e) * GT + i - (GT - T) * e
                        if not (first and e == 0 and i < 2):
                            pe.wait_ge(s["y3_added"], m - 1 if T > 1 else m)
                        n = 0
                        for k in range(KD):
                            for wp, yp in PASSES:
                                last = T_.matmul(l3_ps(i), h2[:, yp, k, i * P:(i + 1) * P],
                                                 wsp[2][:, e, k, wp, :], start=n == 0, stop=n == 5)
                                n += 1
                        last.then_inc(s["l3_done"], 1)
                    if chunks:
                        entries(c2, cp, range(6, 9), False)

            def L1(g, e, w, first):
                for h in range(2):
                    if not (first and e == 0):
                        pe.wait_ge(s["z1_ready"], g * 2 * EX + 2 * (e - 1) + h + 1)
                    n = 0
                    for k in range(KD):
                        for wp, yp in PASSES:
                            last = T_.matmul(PA[:, h, 0:w], wsp[0][:, e, k, wp, h * P:(h + 1) * P], yT[:, yp, k, 0:w],
                                             start=n == 0, stop=n == 5)
                            n += 1
                    last.then_inc(s["l1_done"], 1)

            def L2(g, e, w, first):
                pe.wait_ge(s["z1_ready"], g * 2 * EX + 2 * e + 2)
                pe.wait_ge(s["lo1_ready"], g * 2 * EX + 2 * e + 2)
                for h in range(2):
                    if e:
                        pe.wait_ge(s["z2_ready"], g * 2 * EX + 2 * (e - 1) + h + 1)
                    n = 0
                    for k in range(KD):
                        for wp, yp in PASSES:
                            last = T_.matmul(PB[:, h, 0:w], wsp[1][:, e, k, wp, h * P:(h + 1) * P],
                                             h1[:, e % 2, yp, k, 0:w], start=n == 0, stop=n == 5)
                            n += 1
                    last.then_inc(s["l2_done"], 1)

            group(0, GT, True, True)
            group(1, GT, True, False)
            with pe.Fori(1, GROUPS // 2 - 1) as q:
                group(2 * q, GT, True, False)
                group(2 * q + 1, GT, True, False)
            group(GROUPS - 2, GT, True, False)
            group(GROUPS - 1, GT, False, False)
            group(GROUPS, 1, False, False)


PASSES = [(0, 0), (0, 1), (1, 0)]
X1G = 4 * GT + 3
LOCAL_STEPS = 2 * 55 + 1
LOCAL_CUR = 56 % 2
SORTED_IN = (56 + 28 + 70) % 2
SCHED_M = 20
SCHED_P = SCHED_M + 6 + NBLK


def kernel(**inputs):
    import numpy as _np
    import concourse.bacc as _bacc
    from concourse import mybir as _mybir
    from concourse.bass_utils import run_bass_kernel_spmd as _run

    names = ["x", "src", "dst", "L0_gnn_W1", "L0_gnn_b1", "L0_gnn_W2", "L0_gnn_b2", "L0_ffn_Wr", "L0_ffn_br"]
    bn_names = ["L0_ffn_" + n for n in BN_NAMES]
    names += bn_names + ["L0_ffn_W1", "L0_ffn_W2", "L0_ffn_Wo", "L0_ffn_bo"]
    nc = _bacc.Bacc("TRN2", target_bir_lowering=False, num_devices=1)
    arrays, aps = {}, {}
    for name in names:
        a = _np.ascontiguousarray(inputs[name])
        arrays[f"in_{name}"] = a
        aps[name] = nc.dram_tensor(f"in_{name}", a.shape, _mybir.dt.from_np(a.dtype), kind="ExternalInput").ap()
    out = nc.dram_tensor("out_0", (NPAD, D), _mybir.dt.float32, kind="ExternalOutput").ap()
    build(nc, *[aps[n] for n in names[:9]], [aps[n] for n in bn_names], *[aps[n] for n in names[-4:]], out)
    r = _run(nc, [arrays], core_ids=[0])
    return r.results[0]["out_0"][:N]
```

```python
from contextlib import ExitStack

import concourse.bass as bass
from concourse import mybir

F32 = mybir.dt.float32
F16 = mybir.dt.float16
I32 = mybir.dt.int32
ALU = mybir.AluOpType
ACT = mybir.ActivationFunctionType
AX = mybir.AxisListType
ENG = mybir.EngineType

P = 128
N = 6250
D = 256
KD = D // P
HID = 512
KH = HID // P
E_EDGES = 100000
EX = 8
BINS = -(-N // P)
LAST = N - (BINS - 1) * P
NPAD = BINS * P

EP, EF = 125, 800
SW = 1024
NBLK = SW // P
TILES = -(-E_EDGES // P)
BOUND = TILES + BINS - 1
GT = 4
GROUPS = BINS // GT
EPC = 9
PRO = 12
CHUNKS = PRO + EX * (GROUPS - 2) + 2
NENT = EPC * CHUNKS
HE = NENT // 2
NEED = -(-GT * BOUND // BINS)
RW = 12
assert BINS == GROUPS * GT + 1 and NENT >= BOUND and CHUNKS % 2 == 0 and 2 * HE == NENT
assert all(EPC * PRO + EPC * EX * min(g, GROUPS - 2) + (3 * EPC + 2 if g < GROUPS - 2 else 2 * EPC)
           >= min(NEED * (g + 2), BOUND) for g in range(GROUPS))
SLOTS = 2 * EPC
BITS = 13
MASK = (1 << BITS) - 1
KEYBASE = 0x20000000
PADKEY = KEYBASE | (MASK << BITS) | MASK
EPS_LN = 1e-5
EPS_BN = 1e-3
WS = 64.0

BN_NAMES = ["b1", "g1", "be1", "m1", "v1", "b2", "g2", "be2", "m2", "v2"]


def build(nc, x, src, dst, gW1, gb1, gW2, gb2, Wr, br, bn, W1, W2, Wo, bo, out):
    xn_dram = nc.dram_tensor("xn_hilo", (NPAD, 2 * D), F16, kind="Internal").ap()
    xb_dram = nc.dram_tensor("x_plus_bias", (NPAD, D), F32, kind="Internal").ap()
    with ExitStack() as ctx:
        def sb(name, shape, dt):
            return ctx.enter_context(nc.sbuf_tensor(name, shape, dt))

        def ps(name, shape, dt=F32):
            return ctx.enter_context(nc.psum_tensor(name, shape, dt))

        def sem(name):
            return ctx.enter_context(nc.semaphore(name))

        acc = sb("acc", [P, BINS, D], F32)
        accf = acc[:].rearrange("p b d -> p (b d)")
        wsp = [sb(f"wsplit{l}", [P, EX, KD, 2, D], F16) for l in range(3)]
        wrs = sb("wrs", [P, KD, 2, EX], F16)
        gbuf = sb("gbuf", [P, SLOTS, 2 * D], F16)
        onehot = sb("onehot", [P, 2, EPC, P], F16)
        dsti = sb("dsti", [P, NENT], I32)
        khalf = sb("khalf", [P, SW // 2], F32)
        idle = sb("idle", [P, 2], F32)
        idxc = sb("idxc", [P, 2, EPC], I32)
        srel = sb("srel", [P, NENT], F16)
        bofs = sb("bofs", [1, CHUNKS, RW], I32)
        ordi = sb("ordi", [1, 64], I32)
        W12 = sb("W12", [P, KD, D], F32)
        b12 = sb("b12", [P, D], F32)
        bosb = sb("bosb", [EX, D], F32)
        brb = sb("brb", [P, EX], F32)
        bns = sb("bns", [P, 2, 2 * EX], F32)
        bnt = sb("bnt", [P, 2, 2 * EX], F32)
        ident = sb("ident", [P, P], F32)
        iota_row = sb("iota_row", [P, P], F16)
        xt = sb("xt", [P, 2, GT, D], F32)
        hs = sb("hs", [P, GT, D], F32)
        hT = sb("hT", [P, KD, GT * P], F32)
        yT = sb("yT", [P, 2, 2, KD, GT * P], F16)
        zz = sb("zz", [P, 2, 2, GT * P], F32)
        h1 = sb("h1", [P, 2, 2, KD, GT * P], F16)
        h2 = sb("h2", [P, 2, 2, KD, GT * P], F16)
        stat = sb("stat", [P, GT, 6], F32)
        mv = sb("mv", [P, GT, 2], F32)
        sd = sb("sd", [P, GT], F32)
        rstd = sb("rstd", [P, GT], F32)
        nmr = sb("nmr", [P, GT], F32)
        lg = sb("lg", [P, GT, EX], F32)
        mx = sb("mx", [P, GT], F32)
        nmx = sb("nmx", [P, GT], F32)
        ew = sb("ew", [P, GT, EX], F32)
        es = sb("es", [P, GT], F32)
        er = sb("er", [P, GT], F32)
        wn = sb("wn", [P, GT, EX], F32)
        w64 = sb("w64", [P, 2, GT, EX], F32)
        wT = sb("wT", [EX, GT * P], F32)
        xst = sb("xst", [P, 2, D], F32)
        junk = sb("junk", [P, EF], F16)
        cntb = sb("cntb", [P, BINS + 1], F32)
        cnt = sb("cnt", [P, BINS + 1], F32)
        sums = sb("sums", [P, BINS], F32)
        nmean = sb("nmean", [P, BINS], F32)
        sqs = sb("sqs", [P, BINS], F32)
        xsd = sb("xsd", [P, BINS], F32)
        xrs = sb("xrs", [P, BINS], F32)
        xnm = sb("xnm", [P, BINS], F32)
        epsln = sb("epsln", [P, 1], F32)
        epsbn = sb("epsbn", [P, 1], F32)
        ones = sb("ones", [P, P], F32)
        pidx = sb("pidx", [P, 1], I32)
        gray = sb("gray", [P, 10], I32)
        sgn = sb("sgn", [P, 8], F32)
        pcoli = sb("pcoli", [P, NBLK], I32)
        pcol = sb("pcol", [P, NBLK], F32)
        iri = sb("iri", [P, P], I32)
        bcol = sb("bcol", [P, 1], F32)
        prm = sb("prm", [2 * EX, 10, P], F32)
        sm = sb("sm", [BINS, 16], F32)
        smi = sb("smi", [BINS, 8], I32)
        mb = sb("mb", [BINS, BINS], F32)
        Lm = sb("Lm", [BINS, BINS], F32)
        Rm = sb("Rm", [BINS, BINS], F32)
        bbc = sb("bbc", [BINS, P], F32)
        dbc = sb("dbc", [BINS, P], F32)
        br1 = sb("br1", [1, EX], F32)
        b2r = sb("b2r", [1, D], F32)
        b1c = sb("b1c", [P, KH], F32)
        wst = h2[:].rearrange("p q a k n -> p (q a k n)").bitcast(F32).rearrange(
            "p (s k n) -> p s k n", s=4, k=KD)
        nst = onehot[:].rearrange("p a e n -> p (a e n)")[:, 0:4 * 2 * D].rearrange("p (s d) -> p s d", s=4)
        dsg = hs[:].rearrange("p a d -> p (a d)")[:, 0:7 * P].rearrange("p (j q) -> p j q", q=P)
        keyf = [zz[:, i].rearrange("p h n -> p (h n)") for i in range(2)]
        keyi = [k.bitcast(I32) for k in keyf]
        edges = h1[:].rearrange("p a b k n -> p (a b k n)").bitcast(I32)[:, 0:2 * EF].rearrange("p (s n) -> p s n", s=2)
        srcf = wsp[2][:].rearrange("p e k h d -> p (e k h d)").bitcast(F32)[:, 0:EF]
        cbi = nst[:, 0, 0:2 * (BINS + 1)].bitcast(I32)
        cbf = nst[:, 1, 0:2 * (BINS + 1)].bitcast(F32)
        gb32 = gbuf[:].rearrange("p s d -> p (s d)").bitcast(F32)
        iotk = gb32[:, 0:NENT]
        tk = gb32[:, NENT:2 * NENT]
        Mm = gb32[:, 2 * NENT:3 * NENT]
        bk = hT[:].rearrange("p k n -> p (k n)")[:, 0:NENT]
        prw = gb32[0:2 * EX, 4 * NENT:4 * NENT + 8 * P].rearrange("p (l q n) -> p l q n", l=2, q=4)
        yt32 = yT[:].rearrange("p q a k n -> p (q a k n)").bitcast(F32)
        pat = yt32[:, 0:NENT]
        srcs = yt32[:, 1024:1024 + NENT]
        h132 = h1[:].rearrange("p a b k n -> p (a b k n)").bitcast(F32)
        Pm = [h132[:, i * NENT:(i + 1) * NENT] for i in range(2)]
        xt32 = xt[:].rearrange("p a t d -> p (a t d)")
        gw1 = xt32[:, 0:KD * HID].rearrange("p (k n) -> p k n", k=KD)
        gw2 = xt32[:, 1024:1024 + KH * D].rearrange("p (k n) -> p k n", k=KH)
        w1T = hT[:].rearrange("p k n -> p (k n)").rearrange("p (c n) -> p c n", c=KH)
        b1b = yt32[:, 1024:1024 + KH * P].rearrange("p (c n) -> p c n", c=KH)

        PA = ps("PA", [P, 2, 512])
        PB = ps("PB", [P, 2, 512])
        PT = ps("PT", [P, 2, 512])
        PN = ps("PN", [P, 2, D])
        PL = ps("PL", [P, 2, D])

        s = {n: sem(n) for n in (
            "edges_in", "x_in", "gnnw_in", "small_in", "consts", "keys", "sorted_step", "turned", "diag",
            "srcf_ready", "counted", "x_summed", "nmean_ready", "x_squared", "var_ready", "xsd_ready", "xrs_ready",
            "xnm_ready", "xb_ready", "xn_ready", "xnhi_ready", "xnlo_ready", "xst_stored", "nst_stored0", "nst_stored1",
            "nst_stored2", "nst_stored3", "xst_stored1", "whi_ready", "wlo_ready",
            "prep_pe", "prep_dve", "prep_own", "bn_sqrt", "sched_dve", "sched_pe", "w12_ready", "b12_ready",
            "oh_ready", "select", "own", "nmr_ready", "max_ready", "w_scaled", "idx_ready", "ent_done", "acc_done",
            "xt_in0", "xt_in1", "hs_ready", "hT_done", "hT_sb", "lin_done", "x1_ready", "ln_dve", "sd_ready", "y_ready",
            "yT_done", "yhi_ready", "ylo_ready", "lg_done", "rt_dve", "ex_ready", "w_ready", "wT_done", "wT_sb",
            "bo_done", "bo_added", "l1_done", "l2_done", "l3_done", "z1_ready", "z2_ready", "lo1_ready", "lo2_ready",
            "y3_added", "out0", "out1", "ord_ready", "mem0")}
        wst_in = [sem(f"wst_in{i}") for i in range(4)]
        gat = [sem(f"gathered{i}") for i in range(SLOTS)]

        def first_group(g):
            return isinstance(g, int) and g == 0

        def GB_ENT(g):
            return min(NEED * (g + 1), NENT) if isinstance(g, int) else g * NEED + NEED

        def thirds(g, e, half=1):
            if isinstance(g, int) and g == GROUPS and e >= 0:
                return 2 * EX * GROUPS + e + 1
            return g * (2 * EX) + (2 * e + half + 1)

        turn_at = []

        block = ctx.enter_context(nc.Block())
        NW = 3 * EX + 1

        def piece(n):
            if n == 3 * EX:
                return Wr.rearrange("(k p) e -> p k e", p=P), EX, wrs[:, :, 0, :], wrs[:, :, 1, :]
            l, e = n // EX, n % EX
            w = (W1, W2, Wo)[l]
            return w[e].rearrange("(k p) n -> p k n", p=P), D, wsp[l][:, e, :, 0, :], wsp[l][:, e, :, 1, :]

        @block.sync
        def _(sp):
            sp.dma_start(edges[0:EP, 0, :], src.rearrange("(p n) -> p n", p=EP)).then_inc(s["edges_in"], 16)
            sp.dma_start(edges[0:EP, 1, :], dst.rearrange("(p n) -> p n", p=EP)).then_inc(s["edges_in"], 16)
            sp.wait_ge(s["mem0"], 1)
            for c in range(4):
                sp.dma_start(acc[:, 12 * c:12 * c + 12, :], x[12 * c * P:(12 * c + 12) * P, :].rearrange(
                    "(t p) d -> p t d", p=P)).then_inc(s["x_in"], 16)
            sp.dma_start(acc[0:LAST, BINS - 1, :], x[(BINS - 1) * P:N, :]).then_inc(s["x_in"], 16)
            sp.dma_start(gw1, gW1.rearrange("(k p) n -> p k n", p=P)).then_inc(s["gnnw_in"], 16)
            sp.dma_start(gw2, gW2.rearrange("(k p) n -> p k n", p=P)).then_inc(s["gnnw_in"], 16)
            for j, a in enumerate(bn):
                sp.dma_start(prm[:, j, :], a.rearrange("e (k p) -> (e k) p", p=P)).then_inc(s["small_in"], 16)
            sp.dma_start(bosb[:], bo).then_inc(s["small_in"], 16)
            sp.dma_start(br1[:], br.rearrange("(a n) -> a n", a=1)).then_inc(s["small_in"], 16)
            sp.dma_start(b2r[:], gb2.rearrange("(a n) -> a n", a=1)).then_inc(s["small_in"], 16)
            with nc.allow_non_contiguous_dma(reason="512 biases, once"):
                sp.dma_start(b1c[:], gb1.rearrange("(c p) -> p c", p=P)).then_inc(s["small_in"], 16)

            def load_weights(pieces):
                for n in pieces:
                    w, width, _, _ = piece(n)
                    if n >= 4:
                        sp.wait_ge(s["whi_ready"], n - 3)
                        sp.wait_ge(s["wlo_ready"], n - 3)
                    sp.dma_start(wst[:, n % 4, :, 0:width], w).then_inc(wst_in[n % 4], 16)

            load_weights(range(W_FIRST + 4))
            for t in range(BINS + LN_LAG):
                if t < BINS:
                    sp.wait_ge(s["xb_ready"], t + 1)
                    sp.dma_start(xb_dram[t * P:(t + 1) * P, :], xst[:, t % 2, :]).then_inc(
                        s["xst_stored" if t % 2 == 0 else "xst_stored1"], 16)
                if t >= LN_LAG:
                    u = t - LN_LAG
                    sp.wait_ge(s["xnhi_ready"], u + 1)
                    sp.wait_ge(s["xnlo_ready"], u + 1)
                    sp.dma_start(xn_dram[u * P:(u + 1) * P, :], nst[:, u % 4, :]).then_inc(s[f"nst_stored{u % 4}"], 16)
            load_weights(range(W_FIRST + 4, NW))
            sp.wait_ge(s["xst_stored"], 16 * 25)
            sp.wait_ge(s["xst_stored1"], 16 * 24)
            sp.wait_ge(s["ord_ready"], 1)
            sp.wait_ge(s["prep_pe"], 3)

            def load_x(g, T, par):
                _, b = nc.values_load_multi_w_load_instructions(
                    ordi[0:1, bass.ds(g * GT, T)], engines=[ENG.SP], min_val=0, max_val=BINS - 1,
                    skip_runtime_bounds_check_because=IN_RANGE)
                for i in range(T):
                    sp.dma_start(xt[:, par, i, :], xb_dram[bass.ds(b[i] * P, P), :]).then_inc(s[f"xt_in{par}"], 16)

            def store(g, T, par):
                _, b = nc.values_load_multi_w_load_instructions(
                    ordi[0:1, bass.ds(g * GT, T)], engines=[ENG.SP], min_val=0, max_val=BINS - 1,
                    skip_runtime_bounds_check_because=IN_RANGE)
                sp.wait_ge(s["y3_added"], (g + 1) * (2 * EX) - (EX if T < GT else 0))
                for i in range(T):
                    sp.dma_start(out[bass.ds(b[i] * P, P), :], xt[:, par, i, :]).then_inc(s[f"out{par}"], 16)

            load_x(0, GT, 0)
            load_x(1, GT, 1)
            store(0, GT, 0)
            sp.wait_ge(s["out0"], 16 * GT)
            load_x(2, GT, 0)
            store(1, GT, 1)
            with sp.Fori(1, GROUPS // 2 - 1) as q:
                sp.wait_ge(s["out1"], q * (16 * GT))
                load_x(2 * q + 1, GT, 1)
                store(2 * q, GT, 0)
                sp.wait_ge(s["out0"], q * (16 * GT) + 16 * GT)
                load_x(2 * q + 2, GT, 0)
                store(2 * q + 1, GT, 1)
            sp.wait_ge(s["out1"], 16 * GT * (GROUPS // 2 - 1))
            load_x(GROUPS - 1, GT, 1)
            store(GROUPS - 2, GT, 0)
            sp.wait_ge(s["out0"], 16 * GT * (GROUPS // 2))
            load_x(GROUPS, 1, 0)
            store(GROUPS - 1, GT, 1)
            store(GROUPS, 1, 0)
            sp.wait_ge(s["out0"], 16 * (GT * (GROUPS // 2) + 1))
            sp.wait_ge(s["out1"], 16 * GT * (GROUPS // 2))

        @block.gpsimd
        def _(pool):
            c = [0]

            def step(ins):
                c[0] += 1
                ins.then_inc(s["consts"], 1)

            pool.memset(acc[:, BINS - 1, :], 0.0).then_inc(s["mem0"], 1)
            step(pool.memset(ident[:], 0.0))
            step(pool.iota(pidx[:], pattern=[[0, 1]], base=0, channel_multiplier=1))
            step(pool.iota(iri[:], pattern=[[1, P]], base=0, channel_multiplier=0))
            step(pool.iota(pcoli[:], pattern=[[1, NBLK]], base=0, channel_multiplier=NBLK))
            step(pool.memset(ones[:], 1.0))
            step(pool.memset(epsln[:], EPS_LN))
            step(pool.memset(epsbn[:], EPS_BN))
            step(pool.memset(cnt[:], 0.0))
            step(pool.iota(cbi, pattern=[[P, BINS + 1]], base=0, channel_multiplier=0))
            step(pool.iota(iotk.bitcast(I32), pattern=[[1, NENT]], base=0, channel_multiplier=0))
            pool.wait_ge(s["consts"], 10)
            step(pool.affine_select(out=ident[:], in_=ident[:], compare_op=ALU.not_equal, fill=1.0, base=0,
                                    pattern=[[-1, P]], channel_multiplier=1))
            step(pool.tensor_copy(iota_row[:], iri[:]))
            step(pool.tensor_copy(pcol[:], pcoli[:]))
            step(pool.tensor_copy(bcol[:], pidx[:]))
            step(pool.tensor_copy(tk, iotk.bitcast(I32)))
            step(pool.tensor_copy(cbf, cbi))
            pool.wait_ge(s["consts"], 16)
            step(pool.tensor_copy(iotk, tk))
            step(pool.tensor_scalar(cntb[:], cbf, -1.0, 0.5, ALU.mult, ALU.add))
            pool.wait_ge(s["x_summed"], BINS)
            pool.tensor_scalar(nmean[:], sums[:], -1.0 / D, None, ALU.mult).then_inc(s["nmean_ready"], 1)

            def weights_low(pieces):
                for n in pieces:
                    _, width, hi, lo = piece(n)
                    pool.wait_ge(s["whi_ready"], n + 1)
                    part = wst[:, n % 4, :, 0:width]
                    pool.tensor_scalar(part, part, WS, None, ALU.mult).then_inc(s["w_scaled"], 1)
                    pool.wait_ge(s["w_scaled"], n + 1)
                    pool.tensor_tensor(lo, part, hi, ALU.subtract).then_inc(s["wlo_ready"], 1)

            weights_low(range(W_FIRST))
            pool.wait_ge(s["b12_ready"], 1)
            for t in range(BINS + LN_LAG):
                if t < BINS:
                    if t >= 2:
                        pool.wait_ge(s["xst_stored" if t % 2 == 0 else "xst_stored1"], 16 * (t // 2))
                    pool.tensor_tensor(xst[:, t % 2, :], acc[:, t, :], b12[:], ALU.add).then_inc(s["xb_ready"], 1)
                if t == LN_LAG - 1:
                    pool.wait_ge(s["xrs_ready"], 1)
                    pool.wait_ge(s["nmean_ready"], 1)
                    pool.tensor_tensor(xnm[:], nmean[:], xrs[:], ALU.mult).then_inc(s["xnm_ready"], 1)
                if t >= LN_LAG:
                    u = t - LN_LAG
                    pool.wait_ge(s["xnhi_ready"], u + 1)
                    pool.tensor_tensor(nst[:, u % 4, D:2 * D], acc[:, u, :], nst[:, u % 4, 0:D],
                                       ALU.subtract).then_inc(s["xnlo_ready"], 1)
            weights_low(range(W_FIRST, NW))
            for i in range(4):
                pool.wait_ge(s[f"nst_stored{i}"], 16 * ((BINS - 1 - i) // 4 + 1))
            pool.wait_ge(s["ord_ready"], 1)

            def gathers(c2, par, wait):
                if wait:
                    pool.wait_ge(s["ent_done"], c2 * SLOTS + EPC * (par - 1))
                    pool.nop(nofuse=True)
                pool.tensor_copy(idxc[:, par, :], dsti[:, bass.ds(c2 * SLOTS + par * EPC, EPC)]).then_inc(s["idx_ready"], 1)
                pool.wait_ge(s["idx_ready"], c2 * 2 + (par + 1))
                pool.nop(nofuse=True)
                for m in range(EPC):
                    pool.indirect_dma_start(gbuf[:, par * EPC + m, :], None, xn_dram,
                                            bass.IndirectOffsetOnAxis(idxc[:, par, m:m + 1], 0)).then_inc(
                        gat[par * EPC + m], 16)

            gathers(0, 0, False)
            gathers(0, 1, False)
            with pool.Fori(1, NENT // SLOTS) as c2:
                gathers(c2, 0, True)
                gathers(c2, 1, True)

        @block.scalar
        def _(act):
            act.wait_ge(s["srcf_ready"], 1)
            act.wait_ge(s["consts"], 18)
            for b in range(BINS + 1):
                if b:
                    act.wait_ge(s["counted"], b)
                nc.scalar.activation(junk[0:EP, :], srcf[0:EP, :], ACT.Sign, bias=cntb[0:EP, b:b + 1],
                                     accum_out=cnt[0:EP, b:b + 1]).then_inc(s["counted"], 1)
            act.wait_ge(s["small_in"], 16 * 14)
            for l in range(2):
                nc.scalar.activation(prw[:, l, 0, :], prm[:, 5 * l + 4, :], ACT.Sqrt,
                                     bias=epsbn[0:2 * EX, :]).then_inc(s["bn_sqrt"], 1)
            act.wait_ge(s["x_in"], 16 * 5)
            jk = junk[:, 0:D]
            for t in range(BINS):
                if t:
                    act.wait_ge(s["x_summed"], t)
                else:
                    act.wait_ge(s["counted"], BINS + 1)
                nc.scalar.activation(jk, acc[:, t, :], ACT.Copy, accum_out=sums[:, t:t + 1]).then_inc(s["x_summed"], 1)
            def weights_high(pieces):
                for n in pieces:
                    _, width, hi, _ = piece(n)
                    act.wait_ge(wst_in[n % 4], 16 * (n // 4 + 1))
                    nc.scalar.activation(hi, wst[:, n % 4, :, 0:width], ACT.Copy, scale=WS).then_inc(s["whi_ready"], 1)

            weights_high(range(W_FIRST))
            act.wait_ge(s["nmean_ready"], 1)
            for t in range(BINS):
                if t:
                    act.wait_ge(s["x_squared"], t)
                else:
                    act.wait_ge(s["x_summed"], BINS)
                nc.scalar.activation(jk, acc[:, t, :], ACT.Square, bias=nmean[:, t:t + 1],
                                     accum_out=sqs[:, t:t + 1]).then_inc(s["x_squared"], 1)
            act.wait_ge(s["x_squared"], BINS)
            nc.scalar.activation(xsd[:], sqs[:], ACT.Sqrt, bias=epsln[:], scale=1.0 / D).then_inc(s["xsd_ready"], 1)
            act.wait_ge(s["xnm_ready"], 1)
            for t in range(BINS):
                act.wait_ge(s["xb_ready"], t + 1)
                nc.scalar.activation(acc[:, t, :], acc[:, t, :], ACT.Identity, bias=xnm[:, t:t + 1],
                                     scale=xrs[:, t:t + 1]).then_inc(s["xn_ready"], 1)
                if t >= 4:
                    act.wait_ge(s[f"nst_stored{t % 4}"], 16 * (t // 4))
                act.wait_ge(s["xn_ready"], t + 1)
                nc.scalar.activation(nst[:, t % 4, 0:D], acc[:, t, :], ACT.Copy).then_inc(s["xnhi_ready"], 1)

            weights_high(range(W_FIRST, NW))

            def rows(g, T):
                act.wait_ge(s["acc_done"], GB_ENT(g))
                _, b = nc.values_load_multi_w_load_instructions(
                    ordi[0:1, bass.ds(g * GT, T)], engines=[ENG.Activation], min_val=0, max_val=BINS - 1,
                    skip_runtime_bounds_check_because=IN_RANGE)
                if not first_group(g):
                    act.wait_ge(s["yT_done"], g)
                for i in range(T):
                    nc.scalar.activation(hs[:, i, :], accf[:, bass.ds(b[i] * D, D)], ACT.Copy).then_inc(s["hs_ready"], 1)

            def rows_T(g, T):
                w = T * P
                act.wait_ge(s["hT_done"], g + 1)
                if not first_group(g):
                    act.wait_ge(s["lin_done"], g)
                for k in range(KD):
                    nc.scalar.activation(hT[:, k, 0:w], PT[:, k, 0:w], ACT.Copy).then_inc(s["hT_sb"], 1)

            def deviation(g, T):
                act.wait_ge(s["var_ready"], g + 1)
                nc.scalar.activation(sd[:, 0:T], mv[:, 0:T, 1], ACT.Sqrt, bias=epsln[:]).then_inc(s["sd_ready"], 1)

            def normalise(g, T, par):
                act.wait_ge(s["nmr_ready"], g + 1)
                act.wait_ge(s["hT_done"], g + 1)
                for i in range(T):
                    nc.scalar.activation(hs[:, i, :], xt[:, par, i, :], ACT.Identity, bias=nmr[:, i:i + 1],
                                         scale=rstd[:, i:i + 1]).then_inc(s["y_ready"], 1)

            def y_high(g, T, par):
                w = T * P
                act.wait_ge(s["yT_done"], g + 1)
                for k in range(KD):
                    nc.scalar.activation(yT[:, par, 0, k, 0:w], PT[:, k, 0:w], ACT.Copy).then_inc(s["yhi_ready"], 1)

            def exps(g, T):
                act.wait_ge(s["max_ready"], g + 1)
                for i in range(T):
                    nc.scalar.activation(ew[:, i, :], lg[:, i, :], ACT.Exp, bias=nmx[:, i:i + 1],
                                         accum_out=es[:, i:i + 1]).then_inc(s["ex_ready"], 1)

            def weights_T(g, T):
                act.wait_ge(s["wT_done"], g + 1)
                nc.scalar.activation(wT[:, 0:T * P], PT[0:EX, 0, 0:T * P], ACT.Copy).then_inc(s["wT_sb"], 1)

            def z1(g, e, T):
                w, x_ = T * P, g * EX + e
                for h in range(2):
                    act.wait_ge(s["l1_done"], 2 * x_ + h + 1)
                    if not (isinstance(x_, int) and x_ < 2):
                        act.wait_ge(s["l2_done"], 2 * x_ - 2)
                    if not (isinstance(x_, int) and x_ < 1):
                        act.wait_ge(s["lo1_ready"], 2 * x_ + (h - 1))
                    sc, sh = bns[:, 0, 2 * e + h:2 * e + h + 1], bnt[:, 0, 2 * e + h:2 * e + h + 1]
                    nc.scalar.activation(h1[:, e % 2, 0, h, 0:w], PA[:, h, 0:w], ACT.Relu, bias=sh, scale=sc)
                    nc.scalar.activation(zz[:, 0, h, 0:w], PA[:, h, 0:w], ACT.Relu, bias=sh,
                                         scale=sc).then_inc(s["z1_ready"], 1)

            def z2(g, e, T):
                w, x_ = T * P, g * EX + e
                for h in range(2):
                    act.wait_ge(s["l2_done"], 2 * x_ + h + 1)
                    if not (isinstance(x_, int) and x_ < 2):
                        act.wait_ge(s["l3_done"], thirds(g, e - 2))
                    if not (isinstance(x_, int) and x_ < 1):
                        act.wait_ge(s["lo2_ready"], 2 * x_ + (h - 1))
                    sc, sh = bns[:, 1, 2 * e + h:2 * e + h + 1], bnt[:, 1, 2 * e + h:2 * e + h + 1]
                    nc.scalar.activation(h2[:, e % 2, 0, h, 0:w], PB[:, h, 0:w], ACT.Relu, bias=sh, scale=sc)
                    nc.scalar.activation(zz[:, 1, h, 0:w], PB[:, h, 0:w], ACT.Relu, bias=sh,
                                         scale=sc).then_inc(s["z2_ready"], 1)

            act.wait_ge(s["ord_ready"], 1)
            act.wait_ge(s["xnlo_ready"], BINS)
            act.wait_ge(s["wlo_ready"], NW)
            rows(0, GT)
            rows_T(0, GT)
            deviation(0, GT)
            normalise(0, GT, 0)
            y_high(0, GT, 0)
            exps(0, GT)
            z1(0, 0, GT)

            def group(g, T, par, after):
                for e in range(EX):
                    if e + 1 < EX:
                        z1(g, e + 1, T)
                    elif after:
                        z1(g + 1, 0, after)
                    if after:
                        if e == 3:
                            rows(g + 1, after)
                        if e == 4:
                            rows_T(g + 1, after)
                        if e == 6:
                            y_high(g + 1, after, 1 - par)
                    z2(g, e, T)
                    if e == 0:
                        weights_T(g, T)
                    if after and e == 7:
                        exps(g + 1, after)
                    if after and e == 4:
                        deviation(g + 1, after)
                    if after and e == 5:
                        normalise(g + 1, after, 1 - par)

            group(0, GT, 0, GT)
            with act.Fori(0, (GROUPS - 4) // 2) as q:
                group(2 * q + 1, GT, 1, GT)
                group(2 * q + 2, GT, 0, GT)
            group(GROUPS - 3, GT, 1, GT)
            group(GROUPS - 2, GT, 0, GT)
            group(GROUPS - 1, GT, 1, 1)
            group(GROUPS, 1, 0, 0)

        @block.vector
        def _(dve):
            V = nc.vector
            V.memset(keyi[1], PADKEY).then_inc(s["keys"], 1)
            V.memset(keyi[0], PADKEY).then_inc(s["keys"], 1)
            dve.wait_ge(s["edges_in"], 32)
            dve.wait_ge(s["keys"], 2)
            V.tensor_copy(srcf[0:EP, :], edges[0:EP, 0, :]).then_inc(s["srcf_ready"], 1)
            V.tensor_scalar(keyi[0][0:EP, 0:EF], edges[0:EP, 0, :], BITS, None,
                            ALU.logical_shift_left).then_inc(s["keys"], 1)
            dve.wait_ge(s["keys"], 3)
            V.tensor_tensor(keyi[0][0:EP, 0:EF], keyi[0][0:EP, 0:EF], edges[0:EP, 1, :],
                            ALU.bitwise_or).then_inc(s["keys"], 1)
            dve.wait_ge(s["keys"], 4)
            V.tensor_scalar(keyi[0][0:EP, 0:EF], keyi[0][0:EP, 0:EF], KEYBASE, None,
                            ALU.bitwise_or).then_inc(s["keys"], 1)
            dve.wait_ge(s["keys"], 5)
            def prep():
                np_ = [0]

                def own(ins, wait=True):
                    np_[0] += 1
                    ins.then_inc(s["prep_own"], 1)
                    if wait:
                        dve.wait_ge(s["prep_own"], np_[0])

                dve.wait_ge(s["small_in"], 16 * 14)
                for c in range(KH):
                    own(V.tensor_scalar(b1b[:, c, :], ones[:], b1c[:, c:c + 1], None, ALU.mult), False)
                dve.wait_ge(s["prep_pe"], 1)
                own(V.tensor_copy(w1T.rearrange("p c n -> p (c n)"), PT[:].rearrange("p a n -> p (a n)")))
                V.memset(mb[0:1, 0:1], 0.0).then_inc(s["prep_dve"], 1)
                dve.wait_ge(s["bn_sqrt"], 2)
                for l in range(2):
                    b_, g_, be_, m_ = [prm[:, 5 * l + i, :] for i in range(4)]
                    own(V.reciprocal(prw[:, l, 1, :], prw[:, l, 0, :]))
                    own(V.tensor_tensor(prw[:, l, 1, :], prw[:, l, 1, :], g_, ALU.mult), False)
                    own(V.tensor_tensor(prw[:, l, 0, :], b_, m_, ALU.subtract))
                    own(V.tensor_scalar(prw[:, l, 2, :], prw[:, l, 1, :], 1.0 / WS, None, ALU.mult), False)
                    own(V.tensor_tensor(prw[:, l, 3, :], prw[:, l, 0, :], prw[:, l, 1, :], ALU.mult))
                    own(V.tensor_tensor(prw[:, l, 3, :], prw[:, l, 3, :], be_, ALU.add))
                dve.wait_ge(s["prep_pe"], 2)
                own(V.tensor_copy(W12[:], PN[:]))
                own(V.tensor_copy(brb[:], PL[:, 1, 0:EX]))
                V.tensor_copy(b12[:], PL[:, 0, :]).then_inc(s["b12_ready"], 1)
                dve.wait_ge(s["b12_ready"], 1)
                V.memset(mb[0:1, 0:1], 0.0).then_inc(s["prep_dve"], 1)
                dve.wait_ge(s["prep_pe"], 3)
                for l in range(2):
                    own(V.tensor_copy(bns[:, l, :], PT[:, 0, 32 * l:32 * l + 16]))
                    own(V.tensor_copy(bnt[:, l, :], PT[:, 0, 32 * l + 16:32 * l + 32]))

            cnt_ = [0]
            cur = [0]

            def compare(a_lo, a_hi, o_lo, o_hi):
                V.tensor_tensor(o_lo, a_lo, a_hi, ALU.min).then_inc(s["sorted_step"], 1)
                V.tensor_tensor(o_hi, a_hi, a_lo, ALU.max).then_inc(s["sorted_step"], 1)
                cnt_[0] += 2
                dve.wait_ge(s["sorted_step"], cnt_[0])

            def halves(src_, dst_, width, m, mirror):
                a = src_[:, 0:width].rearrange("p (b m) -> p b m", m=m)
                o = dst_[:, 0:width].rearrange("p (b m) -> p b m", m=m)
                h = m // 2
                if mirror:
                    V.tensor_tensor(o[:, :, 0:h], a[:, :, 0:h], a[:, :, m - 1:h - 1:-1], ALU.min).then_inc(s["sorted_step"], 1)
                    hi_lo = a[:, :, h - 1::-1] if h > 1 else a[:, :, 0:1]
                    V.tensor_tensor(o[:, :, h:m], a[:, :, h:m], hi_lo, ALU.max).then_inc(s["sorted_step"], 1)
                    cnt_[0] += 2
                    dve.wait_ge(s["sorted_step"], cnt_[0])
                else:
                    compare(a[:, :, 0:h], a[:, :, h:m], o[:, :, 0:h], o[:, :, h:m])

            def schedule():
                nS = [0]

                def st(ins, wait=True):
                    nS[0] += 1
                    ins.then_inc(s["sched_dve"], 1)
                    if wait:
                        dve.wait_ge(s["sched_dve"], nS[0])

                dve.wait_ge(s["sched_pe"], 1)
                st(V.tensor_scalar(smi[:, 0:2], PL[0:BINS, 0, 0:2], -0.5, E_EDGES / 2.0, ALU.mult, ALU.add))
                st(V.tensor_scalar(smi[:, 2:3], smi[:, 0:1], 7, None, ALU.logical_shift_right), False)
                st(V.tensor_scalar(sm[:, 0:1], smi[:, 1:2], 127.0, None, ALU.add))
                st(V.tensor_copy(smi[:, 3:4], sm[:, 0:1]))
                st(V.tensor_scalar(smi[:, 4:5], smi[:, 3:4], 7, None, ALU.logical_shift_right))
                st(V.tensor_copy(sm[:, 1:2], smi[:, 2:3]), False)
                st(V.tensor_copy(sm[:, 2:3], smi[:, 4:5]), False)
                st(V.memset(sm[:, 4:5], 1.0))
                st(V.tensor_tensor(sm[:, 3:4], sm[:, 2:3], sm[:, 1:2], ALU.subtract))
                st(V.scalar_tensor_tensor(out=sm[:, 5:6], in0=sm[:, 3:4], scalar=64.0, in1=bcol[0:BINS, :],
                                          op0=ALU.mult, op1=ALU.add))
                st(V.tensor_scalar(mb[:], ones[0:BINS, 0:BINS], sm[:, 5:6], None, ALU.mult))
                assert nS[0] == SCHED_B
                yield
                dve.wait_ge(s["sched_pe"], 2)
                st(V.tensor_scalar(Lm[:], PL[0:BINS, 0, 0:BINS], sm[:, 5:6], None, ALU.is_gt))
                yield
                dve.wait_ge(s["sched_pe"], 3)
                st(V.tensor_copy(sm[:, 6:8], PL[0:BINS, 1, 0:2]))
                st(V.tensor_tensor(sm[:, 8:9], sm[:, 6:7], sm[:, 3:4], ALU.add), False)
                st(V.tensor_tensor(sm[:, 9:10], sm[:, 1:2], sm[:, 6:7], ALU.subtract), False)
                st(V.tensor_scalar(Rm[:], iota_row[0:BINS, 0:BINS], sm[:, 7:8], None, ALU.is_equal), False)
                st(V.tensor_scalar(bbc[:], ones[0:BINS, :], bcol[0:BINS, :], None, ALU.mult))
                st(V.tensor_scalar(dbc[:], ones[0:BINS, :], sm[:, 9:10], None, ALU.mult), False)
                st(V.tensor_scalar(Mm[0:BINS, :], iotk[0:BINS, :], sm[:, 6:7], None, ALU.is_ge))
                st(V.scalar_tensor_tensor(out=Mm[0:BINS, :], in0=iotk[0:BINS, :], scalar=sm[:, 8:9],
                                          in1=Mm[0:BINS, :], op0=ALU.is_lt, op1=ALU.mult))
                assert nS[0] == SCHED_M
                yield
                dve.wait_ge(s["sched_pe"], 4)
                for i in range(2):
                    st(V.tensor_copy(bk[:, i * HE:(i + 1) * HE], PT[:, i, 0:HE]), False)
                    st(V.tensor_tensor(tk[:, i * HE:(i + 1) * HE], iotk[:, i * HE:(i + 1) * HE],
                                       (PN, PL)[i][:].rearrange("p a d -> p (a d)")[:, 0:HE], ALU.add), False)
                dve.wait_ge(s["sched_dve"], nS[0])
                st(V.tensor_scalar(bofs[0:1, :, 0:EPC], bk[0:1, :].rearrange("p (c m) -> p c m", m=EPC), float(D),
                                   None, ALU.mult))
                assert nS[0] == SCHED_T
                yield
                dve.wait_ge(s["sched_pe"], 5)
                st(V.tensor_copy(ordi[0:1, 0:BINS], PN[0:1, 0, 0:BINS]))
                for blk in range(2):
                    V.tensor_scalar(Pm[blk % 2], tk, pcol[:, blk:blk + 1], None, ALU.is_equal).then_inc(s["select"], 1)
                yield
                yield

            def partition_signs():
                dve.wait_ge(s["consts"], 18)
                V.tensor_scalar(gray[:, 0:1], pidx[:], 1, None, ALU.logical_shift_right).then_inc(s["diag"], 1)
                dve.wait_ge(s["diag"], 1)
                V.tensor_tensor(gray[:, 1:2], gray[:, 0:1], pidx[:], ALU.bitwise_xor).then_inc(s["diag"], 1)
                V.tensor_scalar(gray[:, 2:3], pidx[:], 1, None, ALU.bitwise_and).then_inc(s["diag"], 1)
                dve.wait_ge(s["diag"], 3)
                for j in range(7):
                    V.tensor_scalar(gray[:, 3 + j:4 + j], gray[:, 1:2], j, 1, ALU.logical_shift_right,
                                    ALU.bitwise_and).then_inc(s["diag"], 1)
                dve.wait_ge(s["diag"], 10)
                V.tensor_scalar(sgn[:], gray[:, 2:10], -2.0, 1.0, ALU.mult, ALU.add).then_inc(s["diag"], 1)
                dve.wait_ge(s["diag"], 11)
                for j in range(7):
                    V.tensor_scalar(dsg[:, j, :], ident[:], sgn[:, 1 + j:2 + j], None, ALU.mult).then_inc(s["diag"], 1)

            def last_step(src_, dst_, m):
                for hf in range(2):
                    a = src_[:, hf * 512:hf * 512 + 512].rearrange("p (b m) -> p b m", m=m)
                    o = dst_[:, hf * 512:hf * 512 + 512].rearrange("p (b m) -> p b m", m=m)
                    h = m // 2
                    V.tensor_tensor(o[:, :, 0:h], a[:, :, 0:h], a[:, :, h:m], ALU.min).then_inc(s["sorted_step"], 1)
                    V.tensor_tensor(o[:, :, h:m], a[:, :, h:m], a[:, :, 0:h], ALU.max).then_inc(s["sorted_step"], 1)
                    cnt_[0] += 2
                    turn_at.append(cnt_[0])
                dve.wait_ge(s["sorted_step"], cnt_[0])

            for level in range(1, 11):
                m = 1 << level
                width = -(-EF // m) * m
                if level == 6:
                    partition_signs()
                if level == 10:
                    V.tensor_scalar(keyf[1 - cur[0]], keyf[cur[0]], sgn[:, 0:1], None, ALU.mult).then_inc(s["sorted_step"], 1)
                    cnt_[0] += 1
                    dve.wait_ge(s["sorted_step"], cnt_[0])
                    cur[0] = 1 - cur[0]
                d = m
                while d >= 2:
                    if level == 10 and d == 2:
                        last_step(keyf[cur[0]], keyf[1 - cur[0]], 2)
                    else:
                        halves(keyf[cur[0]], keyf[1 - cur[0]], width, d, d == m)
                    cur[0] = 1 - cur[0]
                    d //= 2
            pieces = schedule()
            for j in range(1, 8):
                for hf in range(2):
                    dve.wait_ge(s["turned"], 4 * (j - 1) + hf + 1)
                    part = slice(hf * 512, hf * 512 + 512)
                    a = PA[:, hf, :].rearrange("p (b m) -> p b m", m=1 << j)
                    o = keyf[1 - cur[0]][:, part].rearrange("p (b m) -> p b m", m=1 << j)
                    h = 1 << (j - 1)
                    low = khalf[:, hf * 256:hf * 256 + 256].rearrange("p (b m) -> p b m", m=h)
                    V.tensor_copy(low, a[:, :, 0:h]).then_inc(s["sorted_step"], 1)
                    cnt_[0] += 1
                    dve.wait_ge(s["sorted_step"], cnt_[0])
                    compare(low, a[:, :, h:2 * h], o[:, :, 0:h], o[:, :, h:2 * h])
                    if j == 1:
                        turn_at.append(cnt_[0])
                cur[0] = 1 - cur[0]
                for d in range(j - 1, 0, -1):
                    if d == 1:
                        last_step(keyf[cur[0]], keyf[1 - cur[0]], 2)
                    else:
                        halves(keyf[cur[0]], keyf[1 - cur[0]], SW, 1 << d, False)
                    cur[0] = 1 - cur[0]
                if j >= 5:
                    next(pieces)
                o = keyf[1 - cur[0]]
                dve.wait_ge(s["turned"], 4 * (j - 1) + 3)
                V.tensor_copy(khalf[:], PB[:, 0, :]).then_inc(s["sorted_step"], 1)
                cnt_[0] += 1
                dve.wait_ge(s["sorted_step"], cnt_[0])
                dve.wait_ge(s["turned"], 4 * (j - 1) + 4)
                compare(khalf[:], PB[:, 1, :], o[:, 0:512], o[:, 512:SW])
                cur[0] = 1 - cur[0]
                for d in range(9, 0, -1):
                    if d == 1 and j < 7:
                        last_step(keyf[cur[0]], keyf[1 - cur[0]], 2)
                    else:
                        halves(keyf[cur[0]], keyf[1 - cur[0]], SW, 1 << d, False)
                    cur[0] = 1 - cur[0]
                if j == 2:
                    prep()
                if j == 3:
                    dve.wait_ge(s["xsd_ready"], 1)
                    V.reciprocal(xrs[:], xsd[:]).then_inc(s["xrs_ready"], 1)
                if 4 <= j < 7:
                    next(pieces)
            turn_at.append(cnt_[0])
            assert cur[0] == SORTED_IN

            for blk in range(2, NBLK):
                dve.wait_ge(s["sched_pe"], 5 + blk - 1)
                V.tensor_scalar(Pm[blk % 2], tk, pcol[:, blk:blk + 1], None, ALU.is_equal).then_inc(s["select"], 1)
            dve.wait_ge(s["sched_pe"], 5 + NBLK)
            for i in range(2):
                V.tensor_copy(pat[:, i * HE:(i + 1) * HE], PT[:, i, 0:HE]).then_inc(s["select"], 1)
            pati = pat.bitcast(I32)
            dve.wait_ge(s["select"], NBLK + 2)
            V.tensor_scalar(dsti[:], pati, MASK, None, ALU.bitwise_and).then_inc(s["select"], 1)
            dve.wait_ge(s["select"], NBLK + 3)
            V.tensor_scalar(dsti[:], dsti[:], N - 1, None, ALU.min).then_inc(s["ord_ready"], 1)
            V.tensor_scalar(srcs.bitcast(I32), pati, BITS, MASK, ALU.logical_shift_right, ALU.bitwise_and).then_inc(s["select"], 1)
            dve.wait_ge(s["select"], NBLK + 4)
            V.tensor_copy(srcs, srcs.bitcast(I32)).then_inc(s["select"], 1)
            dve.wait_ge(s["select"], NBLK + 5)
            V.scalar_tensor_tensor(out=srel[:], in0=bk, scalar=-float(P), in1=srcs, op0=ALU.mult,
                                   op1=ALU.add).then_inc(s["select"], 1)
            dve.wait_ge(s["select"], NBLK + 6)

            def onehots(c2, par, part):
                m0, m1 = OH_PARTS[part]
                if not (isinstance(c2, int) and c2 == 0):
                    dve.wait_ge(s["ent_done"], c2 * SLOTS + EPC * (par - 1))
                k = c2 * SLOTS + (par * EPC + m0)
                V.tensor_tensor(onehot[:, par, m0:m1, :], iota_row[:].unsqueeze(1).broadcast_to([P, m1 - m0, P]),
                                srel[:, bass.ds(k, m1 - m0)].unsqueeze(2).broadcast_to([P, m1 - m0, P]),
                                ALU.is_equal).then_inc(s["oh_ready"], 1)

            regs = [None]

            def load_bins(c2, par):
                _, regs[0] = nc.values_load_multi_w_load_instructions(
                    bofs[0:1, bass.ds(c2 * 2 + par, 1), 0:EPC].rearrange("p c m -> p (c m)"), engines=[ENG.DVE],
                    min_val=0, max_val=(BINS - 1) * D,
                    skip_runtime_bounds_check_because=IN_RANGE)

            def add_entry(c2, par, m):
                k = par * EPC + m
                if m % 2 == 0:
                    dve.wait_ge(s["ent_done"], c2 * SLOTS + (par * EPC + min(m + 2, EPC)))
                if not (isinstance(c2, int) and c2 * SLOTS + k == 0):
                    dve.wait_ge(s["acc_done"], c2 * SLOTS + k)
                to = accf[:, bass.ds(regs[0][m], D)]
                V.tensor_tensor(to, to, PN[:, m % 2, :], ALU.add).then_inc(s["acc_done"], 1)

            for i in range(4):
                dve.wait_ge(s[f"nst_stored{i}"], 16 * ((BINS - 1 - i) // 4 + 1))

            def own(ins, wait=True):
                ins.then_inc(s["own"], 1)
                count[0] = count[0] + 1
                if wait:
                    dve.wait_ge(s["own"], count[0])

            count = [0]

            def linear_add(g, T, par):
                count[0] = g * OWN
                dve.wait_ge(s[f"xt_in{par}"], (g // 2 if isinstance(g, int) else half_of[0]) * (16 * GT) + 16 * T)
                dve.wait_ge(s["lin_done"], g + 1)
                for i in range(T):
                    own(V.tensor_tensor(xt[:, par, i, :], xt[:, par, i, :], PT[:, i // 2, (i % 2) * D:(i % 2) * D + D],
                                        ALU.add), i == T - 1)

            def variance(g, T, par):
                for i in range(T):
                    own(V.bn_stats(stat[:, i, :], xt[:, par, i, :]), i == T - 1)
                own(V.memset(idle[:, 0:1], 0.0), False)
                for i in range(T):
                    ins = V.bn_aggr(mv[:, i, :], stat[:, i, :])
                    if i == T - 1:
                        ins.then_inc(s["var_ready"], 1)

            def shift(g, T):
                dve.wait_ge(s["sd_ready"], g + 1)
                own(V.reciprocal(rstd[:, 0:T], sd[:, 0:T]))
                V.scalar_tensor_tensor(out=nmr[:, 0:T], in0=mv[:, 0:T, 0], scalar=-1.0, in1=rstd[:, 0:T],
                                       op0=ALU.mult, op1=ALU.mult).then_inc(s["nmr_ready"], 1)

            def y_low(g, T, par):
                w = T * P
                for k in range(KD):
                    dve.wait_ge(s["yhi_ready"], g * KD + k + 1)
                    V.tensor_tensor(yT[:, par, 1, k, 0:w], PT[:, k, 0:w], yT[:, par, 0, k, 0:w],
                                    ALU.subtract).then_inc(s["ylo_ready"], 1)

            def maxima(g, T):
                dve.wait_ge(s["lg_done"], g + 1)
                for i in range(T):
                    own(V.scalar_tensor_tensor(out=lg[:, i, :], in0=PT[:, 0, i * EX:(i + 1) * EX], scalar=1.0 / WS,
                                               in1=brb[:], op0=ALU.mult, op1=ALU.add), i == T - 1)
                own(V.tensor_reduce(mx[:, 0:T], lg[:, 0:T, :], AX.X, ALU.max))
                V.tensor_scalar(nmx[:, 0:T], mx[:, 0:T], -1.0, None, ALU.mult).then_inc(s["max_ready"], 1)

            def router(g, T, par):
                count[0] = g * OWN + ((OWN if T == GT else OWN_LAST) - 2)
                dve.wait_ge(s["ex_ready"], g * GT + T)
                own(V.reciprocal(er[:, 0:T], es[:, 0:T]))
                for i in range(T):
                    V.tensor_scalar(wn[:, i, :], ew[:, i, :], er[:, i:i + 1], None, ALU.mult).then_inc(s["w_ready"], 1)
                dve.wait_ge(s["w_ready"], g * GT + T)
                own(V.tensor_scalar(w64[:, par, 0:T, :], wn[:, 0:T, :], 1.0 / WS, None, ALU.mult), False)

            def biases(g, T, par):
                dve.wait_ge(s["bo_done"], g + 1)
                for i in range(T):
                    ins = V.tensor_tensor(xt[:, par, i, :], xt[:, par, i, :],
                                          PT[:, i // 2, (i % 2) * D:(i % 2) * D + D], ALU.add)
                    if i == T - 1:
                        ins.then_inc(s["bo_added"], 1)

            half_of = [None]

            def lo1(g, e, T, h):
                w = T * P
                dve.wait_ge(s["z1_ready"], g * 2 * EX + 2 * e + h + 1)
                V.tensor_tensor(h1[:, e % 2, 1, h, 0:w], zz[:, 0, h, 0:w], h1[:, e % 2, 0, h, 0:w],
                                ALU.subtract).then_inc(s["lo1_ready"], 1)

            def lo2(g, e, T, h):
                w = T * P
                dve.wait_ge(s["z2_ready"], g * 2 * EX + 2 * e + h + 1)
                V.tensor_tensor(h2[:, e % 2, 1, h, 0:w], zz[:, 1, h, 0:w], h2[:, e % 2, 0, h, 0:w],
                                ALU.subtract).then_inc(s["lo2_ready"], 1)

            def weigh(g, e, T, par, half):
                if T < GT and half:
                    return
                dve.wait_ge(s["l3_done"], thirds(g, e, half))
                if e == 0:
                    dve.wait_ge(s["bo_added"], g + 1)
                    dve.wait_ge(s["own"], (g + 1) * OWN - (OWN - OWN_LAST if T < GT else 0))
                else:
                    dve.wait_ge(s["y3_added"], thirds(g, e - 1, half))
                for i in range(2 * half, min(2 * half + 2, T)):
                    ins = V.scalar_tensor_tensor(out=xt[:, par, i, :], in0=PL[:, i % 2, :], scalar=w64[:, par, i, e:e + 1],
                                                 in1=xt[:, par, i, :], op0=ALU.mult, op1=ALU.add)
                ins.then_inc(s["y3_added"], 1)

            def chunk(c2, par, nxt):
                load_bins(c2, par)
                if nxt:
                    onehots(c2 + par, 1 - par, 0)
                    onehots(c2 + par, 1 - par, 1)
                for m in range(EPC):
                    add_entry(c2, par, m)

            onehots(0, 0, 0)
            onehots(0, 0, 1)
            chunk(0, 0, True)
            chunk(0, 1, True)
            with dve.Fori(1, PRO // 2 - 2) as c2:
                chunk(c2, 0, True)
                chunk(c2, 1, True)
            C2 = PRO // 2 - 2
            chunk(C2, 0, True)
            linear_add(0, GT, 0)
            variance(0, GT, 0)
            chunk(C2, 1, True)
            shift(0, GT)
            chunk(C2 + 1, 0, True)
            y_low(0, GT, 0)
            maxima(0, GT)
            chunk(C2 + 1, 1, True)
            for h in range(2):
                lo1(0, 0, GT, h)

            def group(g, T, par, after, chunks, prev):
                for e in range(EX):
                    c2, cp = PRO // 2 + g * (EX // 2) + e // 2, e % 2
                    has = e < chunks
                    n_g, n_e, n_T = (g, e + 1, T) if e + 1 < EX else (g + 1, 0, after)
                    l_g, l_e, l_T, l_par = (g, e - 1, T, par) if e else (g - 1, EX - 1, prev, 1 - par)
                    nxt = has and (e + 1 < chunks or chunks == EX)
                    if has:
                        load_bins(c2, cp)
                        add_entry(c2, cp, 0)
                        add_entry(c2, cp, 1)
                    if n_T:
                        lo1(n_g, n_e, n_T, 0)
                    if has:
                        add_entry(c2, cp, 2)
                        add_entry(c2, cp, 3)
                    if n_T:
                        lo1(n_g, n_e, n_T, 1)
                    if e == 0:
                        router(g, T, par)
                    if e == 1:
                        biases(g, T, par)
                    if after and e == 5:
                        shift(g + 1, after)
                    if after and e == 6:
                        y_low(g + 1, after, 1 - par)
                    if after and e == 7:
                        maxima(g + 1, after)
                    if l_T:
                        weigh(l_g, l_e, l_T, l_par, 0)
                    if nxt:
                        onehots(c2 + cp, 1 - cp, 0)
                    if after and e == 4:
                        linear_add(g + 1, after, 1 - par)
                    if has:
                        add_entry(c2, cp, 4)
                        add_entry(c2, cp, 5)
                    lo2(g, e, T, 0)
                    if has:
                        add_entry(c2, cp, 6)
                        add_entry(c2, cp, 7)
                    if after and e == 4:
                        variance(g + 1, after, 1 - par)
                    lo2(g, e, T, 1)
                    if l_T:
                        weigh(l_g, l_e, l_T, l_par, 1)
                    if has:
                        add_entry(c2, cp, 8)
                    if nxt:
                        onehots(c2 + cp, 1 - cp, 1)

            half_of[0] = None
            group(0, GT, 0, GT, EX, 0)
            with dve.Fori(0, (GROUPS - 4) // 2) as q:
                half_of[0] = q + 1
                group(2 * q + 1, GT, 1, GT, EX, GT)
                group(2 * q + 2, GT, 0, GT, EX, GT)
            group(GROUPS - 3, GT, 1, GT, EX, GT)
            group(GROUPS - 2, GT, 0, GT, 2, GT)
            group(GROUPS - 1, GT, 1, 1, 0, GT)
            group(GROUPS, 1, 0, 0, 0, GT)
            weigh(GROUPS, EX - 1, 1, 0, 0)

        @block.tensor
        def _(pe):
            T_ = nc.tensor
            pa, pb = [x_[:].rearrange("p a n -> p (a n)") for x_ in (PA, PB)]

            def prep():
                pe.wait_ge(s["gnnw_in"], 32)
                pe.wait_ge(s["consts"], 18)
                for k in range(KD):
                    for c in range(KH):
                        last = T_.transpose(PT[:, c // 2, (c % 2) * D + k * P:(c % 2) * D + k * P + P],
                                            gw1[:, k, c * P:(c + 1) * P], ident[:])
                last.then_inc(s["prep_pe"], 1)
                pe.wait_ge(s["prep_dve"], 1)
                for m in range(KD):
                    for c in range(KH):
                        T_.matmul(PN[:, m, :], w1T[:, c, m * P:(m + 1) * P], gw2[:, c, :], start=c == 0, stop=c == KH - 1)
                pe.wait_ge(s["small_in"], 16 * 14)
                for c in range(KH):
                    T_.matmul(PL[:, 0, :], b1b[:, c, :], gw2[:, c, :], start=c == 0, stop=False)
                T_.matmul(PL[:, 0, :], ones[0:1, :], b2r[:], start=False, stop=True)
                T_.matmul(PL[:, 1, 0:EX], ones[0:1, :], br1[:], start=True, stop=True).then_inc(s["prep_pe"], 1)
                pe.wait_ge(s["prep_dve"], 2)
                for l in range(2):
                    for q in range(2):
                        last = T_.transpose(PT[:, 0, (2 * l + q) * 16:(2 * l + q) * 16 + 16], prw[:, l, 2 + q, :],
                                            ident[0:2 * EX, 0:2 * EX])
                last.then_inc(s["prep_pe"], 1)

            pe.wait_ge(s["diag"], 18)
            turn = iter(turn_at)
            cur = LOCAL_CUR
            for j in range(1, 8):
                for hf in range(2):
                    pe.wait_ge(s["sorted_step"], next(turn))
                    for b in range(4 * hf, 4 * hf + 4):
                        last = T_.matmul(pa[:, b * P:(b + 1) * P], keyf[cur][:, b * P:(b + 1) * P], dsg[:, j - 1, :],
                                         start=True, stop=True)
                    last.then_inc(s["turned"], 1)
                cur = (cur + j) % 2
                for hf in range(2):
                    pe.wait_ge(s["sorted_step"], next(turn))
                    for b in range(4 * hf, 4 * hf + 4):
                        last = T_.transpose(pb[:, b * P:(b + 1) * P], keyf[cur][:, b * P:(b + 1) * P], ident[:])
                    last.then_inc(s["turned"], 1)
                if j == 2:
                    prep()
                if j == 4:
                    pe.wait_ge(s["counted"], BINS + 1)
                    T_.matmul(PL[0:BINS, 0, 0:1], cnt[:, 0:BINS], ones[:, 0:1], start=True, stop=True)
                    T_.matmul(PL[0:BINS, 0, 1:2], cnt[:, 1:BINS + 1], ones[:, 0:1], start=True,
                              stop=True).then_inc(s["sched_pe"], 1)
                    pe.wait_ge(s["sched_dve"], SCHED_B)
                    T_.matmul(PL[0:BINS, 0, 0:BINS], mb[:], ident[0:BINS, 0:BINS], start=True,
                              stop=True).then_inc(s["sched_pe"], 1)
                if j == 5:
                    pe.wait_ge(s["sched_dve"], SCHED_B + 1)
                    T_.matmul(PL[0:BINS, 1, 0:2], Lm[:], sm[:, 3:5], start=True, stop=True).then_inc(s["sched_pe"], 1)
                    pe.wait_ge(s["sched_dve"], SCHED_M)
                    for i in range(2):
                        T_.matmul(PT[:, i, 0:HE], bbc[:], Mm[0:BINS, i * HE:(i + 1) * HE], start=True, stop=True)
                        last = T_.matmul((PN, PL)[i][:].rearrange("p a d -> p (a d)")[:, 0:HE], dbc[:],
                                         Mm[0:BINS, i * HE:(i + 1) * HE], start=True, stop=True)
                    last.then_inc(s["sched_pe"], 1)
                if j == 6:
                    pe.wait_ge(s["sched_dve"], SCHED_T)
                    T_.matmul(PN[:, 0, 0:BINS], bbc[:], Rm[:], start=True, stop=True).then_inc(s["sched_pe"], 1)
            pe.wait_ge(s["sorted_step"], next(turn))
            for blk in range(NBLK):
                pe.wait_ge(s["select"], blk + 1)
                for i in range(2):
                    last = T_.matmul(PT[:, i, 0:HE], keyf[SORTED_IN][:, blk * P:(blk + 1) * P],
                                     Pm[blk % 2][:, i * HE:(i + 1) * HE], start=blk == 0, stop=blk == NBLK - 1)
                last.then_inc(s["sched_pe"], 1)

            def entries(c2, par, pair):
                if pair == 0:
                    pe.wait_ge(s["oh_ready"], c2 * 4 + (2 * par + 1))
                if pair == 2:
                    pe.wait_ge(s["oh_ready"], c2 * 4 + (2 * par + 2))
                for m in PAIRS[pair]:
                    k = par * EPC + m
                    pe.wait_ge(gat[k], c2 * 16 + 16)
                    if m == PAIRS[pair][0] and not (isinstance(c2, int) and c2 * SLOTS + k == 0):
                        pe.wait_ge(s["acc_done"], c2 * SLOTS + k)
                    T_.matmul(PN[:, m % 2, :], onehot[:, par, m, :], gbuf[:, k, 0:D], start=True, stop=False)
                    T_.matmul(PN[:, m % 2, :], onehot[:, par, m, :], gbuf[:, k, D:2 * D], start=False,
                              stop=True).then_inc(s["ent_done"], 1)

            def chunk(c2, par):
                for pair in range(len(PAIRS)):
                    entries(c2, par, pair)

            def rows_T(g, T):
                pe.wait_ge(s["hs_ready"], g * GT + T)
                if not first_group(g):
                    pe.wait_ge(s["bo_added"], g)
                for i in range(T):
                    for k in range(KD):
                        last = T_.transpose(PT[:, k, i * P:(i + 1) * P], hs[:, i, k * P:(k + 1) * P], ident[:])
                last.then_inc(s["hT_done"], 1)

            def linear(g, T):
                pe.wait_ge(s["hT_sb"], g * KD + KD)
                for i in range(T):
                    for k in range(KD):
                        last = T_.matmul(PT[:, i // 2, (i % 2) * D:(i % 2) * D + D], hT[:, k, i * P:(i + 1) * P],
                                         W12[:, k, :], start=k == 0, stop=k == KD - 1)
                last.then_inc(s["lin_done"], 1)

            def y_T(g, T):
                pe.wait_ge(s["y_ready"], g * GT + T)
                for i in range(T):
                    for k in range(KD):
                        last = T_.transpose(PT[:, k, i * P:(i + 1) * P], hs[:, i, k * P:(k + 1) * P], ident[:])
                last.then_inc(s["yT_done"], 1)

            def logits(g, T, par):
                pe.wait_ge(s["yhi_ready"], g * KD + KD)
                pe.wait_ge(s["ylo_ready"], g * KD + KD)
                for i in range(T):
                    n = 0
                    for k in range(KD):
                        for wp, yp in PASSES:
                            last = T_.matmul(PT[:, 0, i * EX:(i + 1) * EX], yT[:, par, yp, k, i * P:(i + 1) * P],
                                             wrs[:, k, wp, :], start=n == 0, stop=n == 5)
                            n += 1
                last.then_inc(s["lg_done"], 1)

            def weights_T(g, T):
                pe.wait_ge(s["w_ready"], g * GT + T)
                for i in range(T):
                    last = T_.transpose(PT[0:EX, 0, i * P:(i + 1) * P], wn[:, i, :], ident[:])
                last.then_inc(s["wT_done"], 1)

            def biases(g, T):
                pe.wait_ge(s["wT_sb"], g + 1)
                for i in range(T):
                    last = T_.matmul(PT[:, i // 2, (i % 2) * D:(i % 2) * D + D], wT[:, i * P:(i + 1) * P], bosb[:],
                                     start=True, stop=True)
                last.then_inc(s["bo_done"], 1)

            def L1(g, e, T, par, h):
                w, x_ = T * P, g * EX + e
                if not (isinstance(x_, int) and x_ < 1):
                    pe.wait_ge(s["z1_ready"], 2 * x_ + (h - 1))
                n = 0
                for k in range(KD):
                    for wp, yp in PASSES:
                        last = T_.matmul(PA[:, h, 0:w], wsp[0][:, e, k, wp, h * P:(h + 1) * P], yT[:, par, yp, k, 0:w],
                                         start=n == 0, stop=n == 5)
                        n += 1
                last.then_inc(s["l1_done"], 1)

            def L2(g, e, T, h):
                w, x_ = T * P, g * EX + e
                if h == 0:
                    pe.wait_ge(s["z1_ready"], 2 * x_ + 2)
                    pe.wait_ge(s["lo1_ready"], 2 * x_ + 2)
                if not (isinstance(x_, int) and x_ < 1):
                    pe.wait_ge(s["z2_ready"], 2 * x_ + (h - 1))
                n = 0
                for k in range(KD):
                    for wp, yp in PASSES:
                        last = T_.matmul(PB[:, h, 0:w], wsp[1][:, e, k, wp, h * P:(h + 1) * P],
                                         h1[:, e % 2, yp, k, 0:w], start=n == 0, stop=n == 5)
                        n += 1
                last.then_inc(s["l2_done"], 1)

            def L3(g, e, T, half):
                if T < GT and half:
                    return
                pe.wait_ge(s["z2_ready"], g * (2 * EX) + (2 * e + 2))
                pe.wait_ge(s["lo2_ready"], g * (2 * EX) + (2 * e + 2))
                if not (isinstance(g, int) and g == 0 and e == 0 and half == 0):
                    pe.wait_ge(s["y3_added"], thirds(g, e, half) - 1)
                for i in range(2 * half, min(2 * half + 2, T)):
                    n = 0
                    for k in range(KD):
                        for wp, yp in PASSES:
                            last = T_.matmul(PL[:, i % 2, :], h2[:, e % 2, yp, k, i * P:(i + 1) * P],
                                             wsp[2][:, e, k, wp, :], start=n == 0, stop=n == 5)
                            n += 1
                last.then_inc(s["l3_done"], 1)

            chunk(0, 0)
            chunk(0, 1)
            with pe.Fori(1, PRO // 2 - 2) as c2:
                chunk(c2, 0)
                chunk(c2, 1)
            C2 = PRO // 2 - 2
            rows_T(0, GT)
            linear(0, GT)
            chunk(C2, 0)
            chunk(C2, 1)
            y_T(0, GT)
            chunk(C2 + 1, 0)
            pe.wait_ge(s["wlo_ready"], NW)
            logits(0, GT, 0)
            for h in range(2):
                L1(0, 0, GT, 0, h)
            chunk(C2 + 1, 1)

            def group(g, T, par, after, chunks, prev):
                for e in range(EX):
                    c2, cp = PRO // 2 + g * (EX // 2) + e // 2, e % 2
                    has = e < chunks
                    n_g, n_e, n_T, n_par = (g, e + 1, T, par) if e + 1 < EX else (g + 1, 0, after, 1 - par)
                    l_g, l_e, l_T = (g, e - 1, T) if e else (g - 1, EX - 1, prev)
                    if n_T:
                        L1(n_g, n_e, n_T, n_par, 0)
                    if has:
                        entries(c2, cp, 0)
                    if n_T:
                        L1(n_g, n_e, n_T, n_par, 1)
                    if has:
                        entries(c2, cp, 1)
                    if after and e == 6:
                        y_T(g + 1, after)
                    if e == 1:
                        biases(g, T)
                    if l_T:
                        L3(l_g, l_e, l_T, 0)
                    if after and e == 4:
                        linear(g + 1, after)
                    L2(g, e, T, 0)
                    if has:
                        entries(c2, cp, 2)
                    L2(g, e, T, 1)
                    if has:
                        entries(c2, cp, 3)
                    if e == 0:
                        weights_T(g, T)
                    if l_T:
                        L3(l_g, l_e, l_T, 1)
                    if has:
                        entries(c2, cp, 4)
                    if after and e == 3:
                        rows_T(g + 1, after)
                    if after and e == 6:
                        logits(g + 1, after, 1 - par)

            group(0, GT, 0, GT, EX, 0)
            with pe.Fori(0, (GROUPS - 4) // 2) as q:
                group(2 * q + 1, GT, 1, GT, EX, GT)
                group(2 * q + 2, GT, 0, GT, EX, GT)
            group(GROUPS - 3, GT, 1, GT, EX, GT)
            group(GROUPS - 2, GT, 0, GT, 2, GT)
            group(GROUPS - 1, GT, 1, 1, 0, GT)
            group(GROUPS, 1, 0, 0, 0, GT)
            L3(GROUPS, EX - 1, 1, 0)


IN_RANGE = ("a bin is a sum of at most BINS - 1 ones of the schedule's masks, or the place of the one in a row "
            "of a permutation matrix, whatever the edges are")
OH_PARTS = [(0, 4), (4, EPC)]
PAIRS = [(0, 1), (2, 3), (4, 5), (6, 7), (8,)]
OWN = 3 * GT + 5
OWN_LAST = 3 + 5
SCHED_B = 11
SCHED_M = SCHED_B + 9
SCHED_T = SCHED_M + 5
W_FIRST = 12
LN_LAG = 3
PASSES = [(0, 0), (0, 1), (1, 0)]
LOCAL_CUR = 56 % 2
SORTED_IN = (56 + 28 + 70) % 2

def kernel(**inputs):
    import numpy as _np
    import concourse.bacc as _bacc
    from concourse import mybir as _mybir
    from concourse.bass_utils import run_bass_kernel_spmd as _run

    names = ["x", "src", "dst", "L0_gnn_W1", "L0_gnn_b1", "L0_gnn_W2", "L0_gnn_b2", "L0_ffn_Wr", "L0_ffn_br"]
    bn_names = ["L0_ffn_" + n for n in BN_NAMES]
    names += bn_names + ["L0_ffn_W1", "L0_ffn_W2", "L0_ffn_Wo", "L0_ffn_bo"]
    nc = _bacc.Bacc("TRN2", target_bir_lowering=False, num_devices=1)
    arrays, aps = {}, {}
    for name in names:
        a = _np.ascontiguousarray(inputs[name])
        arrays[f"in_{name}"] = a
        aps[name] = nc.dram_tensor(f"in_{name}", a.shape, _mybir.dt.from_np(a.dtype), kind="ExternalInput").ap()
    out = nc.dram_tensor("out_0", (NPAD, D), _mybir.dt.float32, kind="ExternalOutput").ap()
    build(nc, *[aps[n] for n in names[:9]], [aps[n] for n in bn_names], *[aps[n] for n in names[-4:]], out)
    r = _run(nc, [arrays], core_ids=[0])
    return r.results[0]["out_0"][:N]
```

```python
from contextlib import ExitStack

import concourse.bass as bass
from concourse import mybir

F32 = mybir.dt.float32
F16 = mybir.dt.float16
I32 = mybir.dt.int32
ALU = mybir.AluOpType
ACT = mybir.ActivationFunctionType
AX = mybir.AxisListType
ENG = mybir.EngineType

P = 128
N = 6250
D = 256
KD = D // P
HID = 512
KH = HID // P
E_EDGES = 100000
EX = 8
BINS = -(-N // P)
LAST = N - (BINS - 1) * P
NPAD = BINS * P

EP, EF = 125, 800
SW = 1024
NBLK = SW // P
TILES = -(-E_EDGES // P)
BOUND = TILES + BINS - 1
GT = 4
GROUPS = BINS // GT
EPC = 9
PRO = 12
CHUNKS = PRO + EX * (GROUPS - 2) + 2
NENT = EPC * CHUNKS
HE = NENT // 2
NEED = -(-GT * BOUND // BINS)
RW = 12
assert BINS == GROUPS * GT + 1 and NENT >= BOUND and CHUNKS % 2 == 0 and 2 * HE == NENT
assert all(EPC * min(PRO + EX * g + 4, CHUNKS) >= min(NEED * (g + 2), BOUND) for g in range(GROUPS))
assert EPC * (PRO - 3) >= NEED
SLOTS = 2 * EPC
TK_SLOT = (SLOTS * D - NENT) // D
RE = (NENT - SLOTS) // 2
BITS = 13
MASK = (1 << BITS) - 1
KEYBASE = 0x20000000
PADKEY = KEYBASE | (MASK << BITS) | MASK
EPS_LN = 1e-5
EPS_BN = 1e-3
WS = 64.0

BN_NAMES = ["b1", "g1", "be1", "m1", "v1", "b2", "g2", "be2", "m2", "v2"]


def build(nc, x, src, dst, gW1, gb1, gW2, gb2, Wr, br, bn, W1, W2, Wo, bo, out):
    xn_dram = nc.dram_tensor("xn_hilo", (NPAD, 2 * D), F16, kind="Internal").ap()
    xb_dram = nc.dram_tensor("x_plus_bias", (NPAD, D), F32, kind="Internal").ap()
    with ExitStack() as ctx:
        def sb(name, shape, dt):
            return ctx.enter_context(nc.sbuf_tensor(name, shape, dt))

        def ps(name, shape, dt=F32):
            return ctx.enter_context(nc.psum_tensor(name, shape, dt))

        def sem(name):
            return ctx.enter_context(nc.semaphore(name))

        acc = sb("acc", [P, BINS, D], F32)
        accf = acc[:].rearrange("p b d -> p (b d)")
        wsp = [sb(f"wsplit{l}", [P, EX, KD, 2, D], F16) for l in range(3)]
        wrs = sb("wrs", [P, KD, 2, EX], F16)
        gbuf = sb("gbuf", [P, SLOTS, 2 * D], F16)
        onehot = sb("onehot", [P, 2, EPC, P], F16)
        dsti = sb("dsti", [P, NENT], I32)
        khalf = sb("khalf", [P, SW // 2], F32)
        idle = sb("idle", [P, 2], F32)
        idxc = sb("idxc", [P, 2, EPC], I32)
        srel = sb("srel", [P, NENT], F16)
        bofs = sb("bofs", [1, CHUNKS, RW], I32)
        ordi = sb("ordi", [1, 64], I32)
        W12 = sb("W12", [P, KD, D], F32)
        b12 = sb("b12", [P, D], F32)
        bosb = sb("bosb", [3 * EX, D], F32)
        bo3 = sb("bo3", [3 * EX, D], F16)
        brb = sb("brb", [P, EX], F32)
        bns = sb("bns", [P, 2, 2 * EX], F32)
        bnt = sb("bnt", [P, 2, 2 * EX], F32)
        ident = sb("ident", [P, P], F32)
        iota_row = sb("iota_row", [P, P], F16)
        xt = sb("xt", [P, 2, GT, D], F32)
        hs = sb("hs", [P, GT, D], F32)
        hT = sb("hT", [P, KD, GT * P], F32)
        yT = sb("yT", [P, 2, 2, KD, GT * P], F16)
        zz = sb("zz", [P, 2, 2, GT * P], F32)
        h1 = sb("h1", [P, 2, 2, KD, GT * P], F16)
        h2 = sb("h2", [P, 2, 2, KD, GT * P], F16)
        stat = sb("stat", [P, GT, 6], F32)
        mv = sb("mv", [P, GT, 2], F32)
        sd = sb("sd", [P, GT], F32)
        rstd = sb("rstd", [P, GT], F32)
        nmr = sb("nmr", [P, GT], F32)
        lg = sb("lg", [P, GT, EX], F32)
        mx = sb("mx", [P, GT], F32)
        nmx = sb("nmx", [P, GT], F32)
        ew = sb("ew", [P, GT, EX], F32)
        es = sb("es", [P, GT], F32)
        er = sb("er", [P, GT], F32)
        wn = sb("wn", [P, GT, EX], F32)
        w64 = sb("w64", [P, 2, GT, EX], F32)
        wh = sb("wh", [P, GT, EX], F16)
        w3 = sb("w3", [P, GT, 3 * EX], F32)
        wT = sb("wT", [3 * EX, GT * P], F16)
        lowrow = sb("lowrow", [3 * EX, 2], F32)
        xst = sb("xst", [P, 2, D], F32)
        junk = sb("junk", [P, EF], F16)
        cntb = sb("cntb", [P, BINS + 1], F32)
        cnt = sb("cnt", [P, BINS + 1], F32)
        sums = sb("sums", [P, BINS], F32)
        nmean = sb("nmean", [P, BINS], F32)
        sqs = sb("sqs", [P, BINS], F32)
        xsd = sb("xsd", [P, BINS], F32)
        xrs = sb("xrs", [P, BINS], F32)
        xnm = sb("xnm", [P, BINS], F32)
        epsln = sb("epsln", [P, 1], F32)
        epsbn = sb("epsbn", [P, 1], F32)
        ones = sb("ones", [P, P], F32)
        pidx = sb("pidx", [P, 1], I32)
        gray = sb("gray", [P, 10], I32)
        sgn = sb("sgn", [P, 8], F32)
        pcoli = sb("pcoli", [P, NBLK], I32)
        pcol = sb("pcol", [P, NBLK], F32)
        iri = sb("iri", [P, P], I32)
        bcol = sb("bcol", [P, 1], F32)
        prm = sb("prm", [2 * EX, 10, P], F32)
        sm = sb("sm", [BINS, 16], F32)
        smi = sb("smi", [BINS, 8], I32)
        mb = sb("mb", [BINS, BINS], F32)
        Lm = sb("Lm", [BINS, BINS], F32)
        Rm = sb("Rm", [BINS, BINS], F32)
        bbc = sb("bbc", [BINS, P], F32)
        dbc = sb("dbc", [BINS, P], F32)
        br1 = sb("br1", [1, EX], F32)
        b2r = sb("b2r", [1, D], F32)
        b1c = sb("b1c", [P, KH], F32)
        wst = h2[:].rearrange("p q a k n -> p (q a k n)").bitcast(F32).rearrange(
            "p (s k n) -> p s k n", s=4, k=KD)
        nst = onehot[:].rearrange("p a e n -> p (a e n)")[:, 0:4 * 2 * D].rearrange("p (s d) -> p s d", s=4)
        dsg = hs[:].rearrange("p a d -> p (a d)")[:, 0:7 * P].rearrange("p (j q) -> p j q", q=P)
        keyf = [zz[:, i].rearrange("p h n -> p (h n)") for i in range(2)]
        keyi = [k.bitcast(I32) for k in keyf]
        edges = h1[:].rearrange("p a b k n -> p (a b k n)").bitcast(I32)[:, 0:2 * EF].rearrange("p (s n) -> p s n", s=2)
        srcf = wsp[2][:].rearrange("p e k h d -> p (e k h d)").bitcast(F32)[:, 0:EF]
        cbi = nst[:, 0, 0:2 * (BINS + 1)].bitcast(I32)
        cbf = nst[:, 1, 0:2 * (BINS + 1)].bitcast(F32)
        gb32 = gbuf[:].rearrange("p s d -> p (s d)").bitcast(F32)
        iotk = gb32[:, 0:NENT]
        tk = gb32[:, SLOTS * D - NENT:SLOTS * D]
        Mm = gb32[:, 2 * NENT:3 * NENT]
        bk = hT[:].rearrange("p k n -> p (k n)")[:, 0:NENT]
        prw = gb32[0:2 * EX, 4 * NENT:4 * NENT + 8 * P].rearrange("p (l q n) -> p l q n", l=2, q=4)
        yt32 = yT[:].rearrange("p q a k n -> p (q a k n)").bitcast(F32)
        pat = yt32[:, 0:NENT]
        srcs = yt32[:, 1024:1024 + NENT]
        h132 = h1[:].rearrange("p a b k n -> p (a b k n)").bitcast(F32)
        Pm = [h132[:, i * NENT:i * NENT + 2 * RE] for i in range(2)]
        PmA = junk[:].bitcast(F32)[:, 0:NBLK * SLOTS]
        xt32 = xt[:].rearrange("p a t d -> p (a t d)")
        gw1 = xt32[:, 0:KD * HID].rearrange("p (k n) -> p k n", k=KD)
        gw2 = xt32[:, 1024:1024 + KH * D].rearrange("p (k n) -> p k n", k=KH)
        w1T = hT[:].rearrange("p k n -> p (k n)").rearrange("p (c n) -> p c n", c=KH)
        b1b = yt32[:, 1024:1024 + KH * P].rearrange("p (c n) -> p c n", c=KH)

        PA = ps("PA", [P, 2, 512])
        PB = ps("PB", [P, 2, 512])
        PT = ps("PT", [P, 2, 512])
        PN = ps("PN", [P, 2, D])
        PL = ps("PL", [P, 2, D])

        s = {n: sem(n) for n in (
            "edges_in", "x_in", "gnnw_in", "small_in", "consts", "keys", "sorted_step", "turned", "diag",
            "srcf_ready", "counted", "x_summed", "nmean_ready", "x_squared", "var_ready", "xsd_ready", "xrs_ready",
            "xnm_ready", "xb_ready", "xn_ready", "xnhi_ready", "xnlo_ready", "xst_stored", "nst_stored0", "nst_stored1",
            "nst_stored2", "nst_stored3", "xst_stored1", "whi_ready", "wlo_ready",
            "prep_pe", "prep_dve", "prep_act", "firsts", "first_ready", "prep_own", "bn_sqrt", "sched_dve", "sched_pe", "b12_ready",
            "oh_ready", "select", "own", "nmr_ready", "max_ready", "bo_split", "idx_ready", "ent_done", "acc_done",
            "xt_in0", "xt_in1", "hs_ready", "hT_done", "hT_sb", "lin_done", "sd_ready", "y_ready",
            "yT_done", "yhi_ready", "ylo_ready", "lg_done", "ex_ready", "w_ready", "wT_done", "wT_sb",
            "bo_done", "bo_added", "l1_done", "l2_done", "l3_done", "z1_ready", "z2_ready", "lo1_ready", "lo2_ready",
            "y3_added", "out0", "out1", "ord_ready", "mem0")}
        wst_in = [sem(f"wst_in{i}") for i in range(4)]
        gat = [sem(f"gathered{i}") for i in range(SLOTS)]

        def first_group(g):
            return isinstance(g, int) and g == 0

        def GB_ENT(g):
            return min(NEED * (g + 1), NENT) if isinstance(g, int) else g * NEED + NEED

        def thirds(g, e, half=1):
            if isinstance(g, int) and g == GROUPS and e >= 0:
                return 2 * EX * GROUPS + e + 1
            return g * (2 * EX) + (2 * e + half + 1)

        turn_at = []

        block = ctx.enter_context(nc.Block())
        NW = 3 * EX + 1

        def piece(n):
            if n == 3 * EX:
                return Wr.rearrange("(k p) e -> p k e", p=P), EX, wrs[:, :, 0, :], wrs[:, :, 1, :]
            l, e = n // EX, n % EX
            w = (W1, W2, Wo)[l]
            return w[e].rearrange("(k p) n -> p k n", p=P), D, wsp[l][:, e, :, 0, :], wsp[l][:, e, :, 1, :]

        @block.sync
        def _(sp):
            sp.dma_start(edges[0:EP, 0, :], src.rearrange("(p n) -> p n", p=EP)).then_inc(s["edges_in"], 16)
            sp.dma_start(edges[0:EP, 1, :], dst.rearrange("(p n) -> p n", p=EP)).then_inc(s["edges_in"], 16)
            sp.wait_ge(s["mem0"], 1)
            for c in range(4):
                sp.dma_start(acc[:, 12 * c:12 * c + 12, :], x[12 * c * P:(12 * c + 12) * P, :].rearrange(
                    "(t p) d -> p t d", p=P)).then_inc(s["x_in"], 16)
            sp.dma_start(acc[0:LAST, BINS - 1, :], x[(BINS - 1) * P:N, :]).then_inc(s["x_in"], 16)
            sp.dma_start(gw1, gW1.rearrange("(k p) n -> p k n", p=P)).then_inc(s["gnnw_in"], 16)
            sp.dma_start(gw2, gW2.rearrange("(k p) n -> p k n", p=P)).then_inc(s["gnnw_in"], 16)
            for j, a in enumerate(bn):
                sp.dma_start(prm[:, j, :], a.rearrange("e (k p) -> (e k) p", p=P)).then_inc(s["small_in"], 16)
            for i in range(3):
                sp.dma_start(bosb[i * EX:(i + 1) * EX, :], bo).then_inc(s["small_in"], 16)
            sp.dma_start(br1[:], br.rearrange("(a n) -> a n", a=1)).then_inc(s["small_in"], 16)
            sp.dma_start(b2r[:], gb2.rearrange("(a n) -> a n", a=1)).then_inc(s["small_in"], 16)
            with nc.allow_non_contiguous_dma(reason="512 biases, once"):
                sp.dma_start(b1c[:], gb1.rearrange("(c p) -> p c", p=P)).then_inc(s["small_in"], 16)

            def load_weights(pieces):
                for n in pieces:
                    w, width, _, _ = piece(n)
                    if n >= 4:
                        sp.wait_ge(s["whi_ready"], n - 3)
                        sp.wait_ge(s["wlo_ready"], n - 3)
                    sp.dma_start(wst[:, n % 4, :, 0:width], w).then_inc(wst_in[n % 4], 16)

            load_weights(range(W_FIRST + 4))
            for t in range(BINS + LN_LAG):
                if t < BINS:
                    sp.wait_ge(s["xb_ready"], t + 1)
                    sp.dma_start(xb_dram[t * P:(t + 1) * P, :], xst[:, t % 2, :]).then_inc(
                        s["xst_stored" if t % 2 == 0 else "xst_stored1"], 16)
                if t >= LN_LAG:
                    u = t - LN_LAG
                    sp.wait_ge(s["xnhi_ready"], u + 1)
                    sp.wait_ge(s["xnlo_ready"], u + 1)
                    sp.dma_start(xn_dram[u * P:(u + 1) * P, :], nst[:, u % 4, :]).then_inc(s[f"nst_stored{u % 4}"], 16)
            load_weights(range(W_FIRST + 4, NW))
            sp.wait_ge(s["xst_stored"], 16 * 25)
            sp.wait_ge(s["xst_stored1"], 16 * 24)
            sp.wait_ge(s["ord_ready"], 1)
            sp.wait_ge(s["prep_pe"], 3)

            def load_x(g, T, par):
                _, b = nc.values_load_multi_w_load_instructions(
                    ordi[0:1, bass.ds(g * GT, T)], engines=[ENG.SP], min_val=0, max_val=BINS - 1,
                    skip_runtime_bounds_check_because=IN_RANGE)
                for i in range(T):
                    sp.dma_start(xt[:, par, i, :], xb_dram[bass.ds(b[i] * P, P), :]).then_inc(s[f"xt_in{par}"], 16)

            def store(g, T, par):
                _, b = nc.values_load_multi_w_load_instructions(
                    ordi[0:1, bass.ds(g * GT, T)], engines=[ENG.SP], min_val=0, max_val=BINS - 1,
                    skip_runtime_bounds_check_because=IN_RANGE)
                sp.wait_ge(s["y3_added"], (g + 1) * (2 * EX) - (EX if T < GT else 0))
                for i in range(T):
                    sp.dma_start(out[bass.ds(b[i] * P, P), :], xt[:, par, i, :]).then_inc(s[f"out{par}"], 16)

            load_x(0, GT, 0)
            load_x(1, GT, 1)
            store(0, GT, 0)
            sp.wait_ge(s["out0"], 16 * GT)
            load_x(2, GT, 0)
            store(1, GT, 1)
            with sp.Fori(1, GROUPS // 2 - 1) as q:
                sp.wait_ge(s["out1"], q * (16 * GT))
                load_x(2 * q + 1, GT, 1)
                store(2 * q, GT, 0)
                sp.wait_ge(s["out0"], q * (16 * GT) + 16 * GT)
                load_x(2 * q + 2, GT, 0)
                store(2 * q + 1, GT, 1)
            sp.wait_ge(s["out1"], 16 * GT * (GROUPS // 2 - 1))
            load_x(GROUPS - 1, GT, 1)
            store(GROUPS - 2, GT, 0)
            sp.wait_ge(s["out0"], 16 * GT * (GROUPS // 2))
            load_x(GROUPS, 1, 0)
            store(GROUPS - 1, GT, 1)
            store(GROUPS, 1, 0)
            sp.wait_ge(s["out0"], 16 * (GT * (GROUPS // 2) + 1))
            sp.wait_ge(s["out1"], 16 * GT * (GROUPS // 2))

        @block.gpsimd
        def _(pool):
            c = [0]

            def step(ins):
                c[0] += 1
                ins.then_inc(s["consts"], 1)

            pool.memset(acc[:, BINS - 1, :], 0.0).then_inc(s["mem0"], 1)
            step(pool.memset(ident[:], 0.0))
            step(pool.iota(pidx[:], pattern=[[0, 1]], base=0, channel_multiplier=1))
            step(pool.iota(iri[:], pattern=[[1, P]], base=0, channel_multiplier=0))
            step(pool.iota(pcoli[:], pattern=[[1, NBLK]], base=0, channel_multiplier=NBLK))
            step(pool.memset(ones[:], 1.0))
            step(pool.memset(epsln[:], EPS_LN))
            step(pool.memset(epsbn[:], EPS_BN))
            step(pool.memset(cnt[:], 0.0))
            step(pool.iota(cbi, pattern=[[P, BINS + 1]], base=0, channel_multiplier=0))
            step(pool.iota(iotk.bitcast(I32), pattern=[[1, NENT]], base=0, channel_multiplier=0))
            pool.wait_ge(s["consts"], 10)
            step(pool.affine_select(out=ident[:], in_=ident[:], compare_op=ALU.not_equal, fill=1.0, base=0,
                                    pattern=[[-1, P]], channel_multiplier=1))
            step(pool.tensor_copy(iota_row[:], iri[:]))
            step(pool.tensor_copy(pcol[:], pcoli[:]))
            step(pool.tensor_copy(bcol[:], pidx[:]))
            step(pool.tensor_copy(tk, iotk.bitcast(I32)))
            step(pool.tensor_copy(cbf, cbi))
            pool.wait_ge(s["consts"], 16)
            step(pool.tensor_copy(iotk, tk))
            step(pool.tensor_scalar(cntb[:], cbf, -1.0, 0.5, ALU.mult, ALU.add))
            split = [0]

            def bias(ins):
                split[0] += 1
                ins.then_inc(s["bo_split"], 1)
                pool.wait_ge(s["bo_split"], split[0])

            high, low = nst[0:3 * EX, 2, 0:D], xst[0:3 * EX, 0, :]
            pool.wait_ge(s["small_in"], 16 * 16)
            bias(pool.tensor_scalar(lowrow[:, 1:2], bcol[0:3 * EX, :], 2 * EX - 0.5, None, ALU.is_gt))
            bias(pool.tensor_scalar(lowrow[:, 0:1], lowrow[:, 1:2], -1.0, 1.0, ALU.mult, ALU.add))
            bias(pool.tensor_copy(high, bosb[:]))
            bias(pool.tensor_tensor(low, bosb[:], high, ALU.subtract))
            bias(pool.tensor_scalar(low, low, lowrow[:, 1:2], None, ALU.mult))
            bias(pool.tensor_scalar(bosb[:], high, lowrow[:, 0:1], None, ALU.mult))
            bias(pool.tensor_tensor(bo3[:], bosb[:], low, ALU.add))
            pool.wait_ge(s["x_summed"], BINS)
            pool.tensor_scalar(nmean[:], sums[:], -1.0 / D, None, ALU.mult).then_inc(s["nmean_ready"], 1)

            def weights_low(pieces):
                for n in pieces:
                    _, width, hi, lo = piece(n)
                    pool.wait_ge(s["whi_ready"], n + 1)
                    pool.tensor_tensor(lo, wst[:, n % 4, :, 0:width], hi, ALU.subtract).then_inc(s["wlo_ready"], 1)

            weights_low(range(W_FIRST))
            pool.wait_ge(s["b12_ready"], 1)
            for t in range(BINS + LN_LAG):
                if t < BINS:
                    if t >= 2:
                        pool.wait_ge(s["xst_stored" if t % 2 == 0 else "xst_stored1"], 16 * (t // 2))
                    pool.tensor_tensor(xst[:, t % 2, :], acc[:, t, :], b12[:], ALU.add).then_inc(s["xb_ready"], 1)
                if t == LN_LAG - 1:
                    pool.wait_ge(s["xrs_ready"], 1)
                    pool.wait_ge(s["nmean_ready"], 1)
                    pool.tensor_tensor(xnm[:], nmean[:], xrs[:], ALU.mult).then_inc(s["xnm_ready"], 1)
                if t >= LN_LAG:
                    u = t - LN_LAG
                    pool.wait_ge(s["xnhi_ready"], u + 1)
                    pool.tensor_tensor(nst[:, u % 4, D:2 * D], acc[:, u, :], nst[:, u % 4, 0:D],
                                       ALU.subtract).then_inc(s["xnlo_ready"], 1)
            weights_low(range(W_FIRST, NW))
            for i in range(4):
                pool.wait_ge(s[f"nst_stored{i}"], 16 * ((BINS - 1 - i) // 4 + 1))
            pool.wait_ge(s["first_ready"], 1)

            def gathers(c2, par, wait):
                if wait:
                    pool.wait_ge(s["ent_done"], c2 * SLOTS + EPC * (par - 1))
                    pool.nop(nofuse=True)
                pool.tensor_copy(idxc[:, par, :], dsti[:, bass.ds(c2 * SLOTS + par * EPC, EPC)]).then_inc(s["idx_ready"], 1)
                pool.wait_ge(s["idx_ready"], c2 * 2 + (par + 1))
                pool.nop(nofuse=True)
                for m in range(EPC):
                    if not wait and par * EPC + m == TK_SLOT:
                        pool.wait_ge(s["ord_ready"], 1)
                        pool.nop(nofuse=True)
                    pool.indirect_dma_start(gbuf[:, par * EPC + m, :], None, xn_dram,
                                            bass.IndirectOffsetOnAxis(idxc[:, par, m:m + 1], 0)).then_inc(
                        gat[par * EPC + m], 16)

            gathers(0, 0, False)
            gathers(0, 1, False)
            with pool.Fori(1, NENT // SLOTS) as c2:
                gathers(c2, 0, True)
                gathers(c2, 1, True)

        @block.scalar
        def _(act):
            act.wait_ge(s["srcf_ready"], 1)
            act.wait_ge(s["consts"], 18)
            for b in range(BINS + 1):
                if b:
                    act.wait_ge(s["counted"], b)
                nc.scalar.activation(junk[0:EP, :], srcf[0:EP, :], ACT.Sign, bias=cntb[0:EP, b:b + 1],
                                     accum_out=cnt[0:EP, b:b + 1]).then_inc(s["counted"], 1)
            act.wait_ge(s["small_in"], 16 * 16)
            for l in range(2):
                nc.scalar.activation(prw[:, l, 0, :], prm[:, 5 * l + 4, :], ACT.Sqrt,
                                     bias=epsbn[0:2 * EX, :]).then_inc(s["bn_sqrt"], 1)
            act.wait_ge(s["x_in"], 16 * 5)
            jk = junk[:, 0:D]
            for t in range(BINS):
                if t:
                    act.wait_ge(s["x_summed"], t)
                else:
                    act.wait_ge(s["counted"], BINS + 1)
                nc.scalar.activation(jk, acc[:, t, :], ACT.Copy, accum_out=sums[:, t:t + 1]).then_inc(s["x_summed"], 1)

            def weights_high(pieces):
                for n in pieces:
                    _, width, hi, _ = piece(n)
                    act.wait_ge(wst_in[n % 4], 16 * (n // 4 + 1))
                    part = wst[:, n % 4, :, 0:width]
                    nc.scalar.activation(hi, part, ACT.Copy, scale=WS)
                    nc.scalar.activation(part, part, ACT.Copy, scale=WS).then_inc(s["whi_ready"], 1)

            weights_high(range(W_FIRST))

            def prep(ins):
                ins.then_inc(s["prep_act"], 1)

            for c in range(KH):
                prep(nc.scalar.activation(b1b[:, c, :], ones[:], ACT.Copy, scale=b1c[:, c:c + 1]))
            act.wait_ge(s["prep_pe"], 1)
            prep(nc.scalar.activation(w1T.rearrange("p c n -> p (c n)"), PT[:].rearrange("p a n -> p (a n)"), ACT.Copy))
            act.wait_ge(s["prep_pe"], 2)
            prep(nc.scalar.activation(W12[:], PN[:], ACT.Copy))
            prep(nc.scalar.activation(brb[:], PL[:, 1, 0:EX], ACT.Copy))
            nc.scalar.activation(b12[:], PL[:, 0, :], ACT.Copy).then_inc(s["b12_ready"], 1)
            act.wait_ge(s["prep_pe"], 3)
            for l in range(2):
                prep(nc.scalar.activation(bns[:, l, :], PT[:, 0, 32 * l:32 * l + 16], ACT.Copy))
                prep(nc.scalar.activation(bnt[:, l, :], PT[:, 0, 32 * l + 16:32 * l + 32], ACT.Copy))
            act.wait_ge(s["nmean_ready"], 1)
            for t in range(BINS):
                if t:
                    act.wait_ge(s["x_squared"], t)
                else:
                    act.wait_ge(s["x_summed"], BINS)
                nc.scalar.activation(jk, acc[:, t, :], ACT.Square, bias=nmean[:, t:t + 1],
                                     accum_out=sqs[:, t:t + 1]).then_inc(s["x_squared"], 1)
            act.wait_ge(s["x_squared"], BINS)
            nc.scalar.activation(xsd[:], sqs[:], ACT.Sqrt, bias=epsln[:], scale=1.0 / D).then_inc(s["xsd_ready"], 1)
            act.wait_ge(s["xnm_ready"], 1)
            for t in range(BINS):
                act.wait_ge(s["xb_ready"], t + 1)
                nc.scalar.activation(acc[:, t, :], acc[:, t, :], ACT.Identity, bias=xnm[:, t:t + 1],
                                     scale=xrs[:, t:t + 1]).then_inc(s["xn_ready"], 1)
                if t >= 4:
                    act.wait_ge(s[f"nst_stored{t % 4}"], 16 * (t // 4))
                act.wait_ge(s["xn_ready"], t + 1)
                nc.scalar.activation(nst[:, t % 4, 0:D], acc[:, t, :], ACT.Copy).then_inc(s["xnhi_ready"], 1)

            weights_high(range(W_FIRST, NW))

            def rows(g, T):
                act.wait_ge(s["acc_done"], GB_ENT(g))
                _, b = nc.values_load_multi_w_load_instructions(
                    ordi[0:1, bass.ds(g * GT, T)], engines=[ENG.Activation], min_val=0, max_val=BINS - 1,
                    skip_runtime_bounds_check_because=IN_RANGE)
                if not first_group(g):
                    act.wait_ge(s["yT_done"], g)
                for i in range(T):
                    nc.scalar.activation(hs[:, i, :], accf[:, bass.ds(b[i] * D, D)], ACT.Copy).then_inc(s["hs_ready"], 1)

            def rows_T(g, T):
                w = T * P
                act.wait_ge(s["hT_done"], g + 1)
                if not first_group(g):
                    act.wait_ge(s["lin_done"], g)
                for k in range(KD):
                    nc.scalar.activation(hT[:, k, 0:w], PT[:, k, 0:w], ACT.Copy).then_inc(s["hT_sb"], 1)

            def deviation(g, T):
                act.wait_ge(s["var_ready"], g + 1)
                nc.scalar.activation(sd[:, 0:T], mv[:, 0:T, 1], ACT.Sqrt, bias=epsln[:]).then_inc(s["sd_ready"], 1)

            def normalise(g, T, par):
                act.wait_ge(s["nmr_ready"], g + 1)
                act.wait_ge(s["hT_done"], g + 1)
                for i in range(T):
                    nc.scalar.activation(hs[:, i, :], xt[:, par, i, :], ACT.Identity, bias=nmr[:, i:i + 1],
                                         scale=rstd[:, i:i + 1]).then_inc(s["y_ready"], 1)

            def y_high(g, T, par):
                w = T * P
                act.wait_ge(s["yT_done"], g + 1)
                for k in range(KD):
                    nc.scalar.activation(yT[:, par, 0, k, 0:w], PT[:, k, 0:w], ACT.Copy).then_inc(s["yhi_ready"], 1)

            def exps(g, T):
                act.wait_ge(s["max_ready"], g + 1)
                for i in range(T):
                    nc.scalar.activation(ew[:, i, :], lg[:, i, :], ACT.Exp, bias=nmx[:, i:i + 1],
                                         accum_out=es[:, i:i + 1]).then_inc(s["ex_ready"], 1)

            def weights_T(g, T):
                act.wait_ge(s["wT_done"], g + 1)
                nc.scalar.activation(wT[:, 0:T * P], PT[0:3 * EX, 0, 0:T * P], ACT.Copy).then_inc(s["wT_sb"], 1)

            def z1(g, e, T):
                w, x_ = T * P, g * EX + e
                for h in range(2):
                    act.wait_ge(s["l1_done"], 2 * x_ + h + 1)
                    if not (isinstance(x_, int) and x_ < 2):
                        act.wait_ge(s["l2_done"], 2 * x_ - 2)
                    if not (isinstance(x_, int) and x_ < 1):
                        act.wait_ge(s["lo1_ready"], 2 * x_ + (h - 1))
                    sc, sh = bns[:, 0, 2 * e + h:2 * e + h + 1], bnt[:, 0, 2 * e + h:2 * e + h + 1]
                    nc.scalar.activation(h1[:, e % 2, 0, h, 0:w], PA[:, h, 0:w], ACT.Relu, bias=sh, scale=sc)
                    nc.scalar.activation(zz[:, 0, h, 0:w], PA[:, h, 0:w], ACT.Relu, bias=sh,
                                         scale=sc).then_inc(s["z1_ready"], 1)

            def z2(g, e, T):
                w, x_ = T * P, g * EX + e
                for h in range(2):
                    act.wait_ge(s["l2_done"], 2 * x_ + h + 1)
                    if not (isinstance(x_, int) and x_ < 2):
                        act.wait_ge(s["l3_done"], thirds(g, e - 2))
                    if not (isinstance(x_, int) and x_ < 1):
                        act.wait_ge(s["lo2_ready"], 2 * x_ + (h - 1))
                    sc, sh = bns[:, 1, 2 * e + h:2 * e + h + 1], bnt[:, 1, 2 * e + h:2 * e + h + 1]
                    nc.scalar.activation(h2[:, e % 2, 0, h, 0:w], PB[:, h, 0:w], ACT.Relu, bias=sh, scale=sc)
                    nc.scalar.activation(zz[:, 1, h, 0:w], PB[:, h, 0:w], ACT.Relu, bias=sh,
                                         scale=sc).then_inc(s["z2_ready"], 1)

            act.wait_ge(s["ord_ready"], 1)
            act.wait_ge(s["xnlo_ready"], BINS)
            act.wait_ge(s["wlo_ready"], NW)
            rows(0, GT)
            rows_T(0, GT)
            deviation(0, GT)
            normalise(0, GT, 0)
            y_high(0, GT, 0)
            exps(0, GT)
            z1(0, 0, GT)

            def group(g, T, par, after):
                for e in range(EX):
                    if e + 1 < EX:
                        z1(g, e + 1, T)
                    elif after:
                        z1(g + 1, 0, after)
                    if after:
                        if e == 5:
                            deviation(g + 1, after)
                        if e == 4:
                            rows_T(g + 1, after)
                        if e == 6:
                            y_high(g + 1, after, 1 - par)
                    if e == 1:
                        weights_T(g, T)
                    z2(g, e, T)
                    if after and e == 7:
                        exps(g + 1, after)
                    if after and e == 3:
                        rows(g + 1, after)
                    if after and e == 5:
                        normalise(g + 1, after, 1 - par)

            group(0, GT, 0, GT)
            with act.Fori(0, (GROUPS - 4) // 2) as q:
                group(2 * q + 1, GT, 1, GT)
                group(2 * q + 2, GT, 0, GT)
            group(GROUPS - 3, GT, 1, GT)
            group(GROUPS - 2, GT, 0, GT)
            group(GROUPS - 1, GT, 1, 1)
            group(GROUPS, 1, 0, 0)

        @block.vector
        def _(dve):
            V = nc.vector
            V.memset(keyi[1], PADKEY).then_inc(s["keys"], 1)
            V.memset(keyi[0], PADKEY).then_inc(s["keys"], 1)
            dve.wait_ge(s["edges_in"], 32)
            dve.wait_ge(s["keys"], 2)
            V.tensor_copy(srcf[0:EP, :], edges[0:EP, 0, :]).then_inc(s["srcf_ready"], 1)
            V.tensor_scalar(keyi[0][0:EP, 0:EF], edges[0:EP, 0, :], BITS, None,
                            ALU.logical_shift_left).then_inc(s["keys"], 1)
            dve.wait_ge(s["keys"], 3)
            V.tensor_tensor(keyi[0][0:EP, 0:EF], keyi[0][0:EP, 0:EF], edges[0:EP, 1, :],
                            ALU.bitwise_or).then_inc(s["keys"], 1)
            dve.wait_ge(s["keys"], 4)
            V.tensor_scalar(keyi[0][0:EP, 0:EF], keyi[0][0:EP, 0:EF], KEYBASE, None,
                            ALU.bitwise_or).then_inc(s["keys"], 1)
            dve.wait_ge(s["keys"], 5)
            def batch_norm():
                np_ = [0]

                def own(ins, wait=True):
                    np_[0] += 1
                    ins.then_inc(s["prep_own"], 1)
                    if wait:
                        dve.wait_ge(s["prep_own"], np_[0])

                dve.wait_ge(s["bn_sqrt"], 2)
                own(V.reciprocal(prw[:, :, 1, :], prw[:, :, 0, :]))
                for l in range(2):
                    b_, g_, be_, m_ = [prm[:, 5 * l + i, :] for i in range(4)]
                    own(V.tensor_tensor(prw[:, l, 1, :], prw[:, l, 1, :], g_, ALU.mult), False)
                    own(V.tensor_tensor(prw[:, l, 0, :], b_, m_, ALU.subtract), l == 1)
                own(V.tensor_scalar(prw[:, :, 2, :], prw[:, :, 1, :], 1.0 / WS, None, ALU.mult), False)
                own(V.tensor_tensor(prw[:, :, 3, :], prw[:, :, 0, :], prw[:, :, 1, :], ALU.mult))
                for l in range(2):
                    V.tensor_tensor(prw[:, l, 3, :], prw[:, l, 3, :], prm[:, 5 * l + 2, :], ALU.add).then_inc(s["prep_dve"], 1)

            cnt_ = [0]
            cur = [0]

            def compare(a_lo, a_hi, o_lo, o_hi):
                V.tensor_tensor(o_lo, a_lo, a_hi, ALU.min).then_inc(s["sorted_step"], 1)
                V.tensor_tensor(o_hi, a_hi, a_lo, ALU.max).then_inc(s["sorted_step"], 1)
                cnt_[0] += 2
                dve.wait_ge(s["sorted_step"], cnt_[0])

            def halves(src_, dst_, width, m, mirror):
                a = src_[:, 0:width].rearrange("p (b m) -> p b m", m=m)
                o = dst_[:, 0:width].rearrange("p (b m) -> p b m", m=m)
                h = m // 2
                if mirror:
                    V.tensor_tensor(o[:, :, 0:h], a[:, :, 0:h], a[:, :, m - 1:h - 1:-1], ALU.min).then_inc(s["sorted_step"], 1)
                    hi_lo = a[:, :, h - 1::-1] if h > 1 else a[:, :, 0:1]
                    V.tensor_tensor(o[:, :, h:m], a[:, :, h:m], hi_lo, ALU.max).then_inc(s["sorted_step"], 1)
                    cnt_[0] += 2
                    dve.wait_ge(s["sorted_step"], cnt_[0])
                else:
                    compare(a[:, :, 0:h], a[:, :, h:m], o[:, :, 0:h], o[:, :, h:m])

            def schedule():
                nS = [0]

                def st(ins, wait=True):
                    nS[0] += 1
                    ins.then_inc(s["sched_dve"], 1)
                    if wait:
                        dve.wait_ge(s["sched_dve"], nS[0])

                dve.wait_ge(s["sched_pe"], 1)
                st(V.tensor_scalar(smi[:, 0:2], PL[0:BINS, 0, 0:2], -0.5, E_EDGES / 2.0, ALU.mult, ALU.add))
                st(V.tensor_scalar(smi[:, 2:3], smi[:, 0:1], 7, None, ALU.logical_shift_right), False)
                st(V.tensor_scalar(sm[:, 0:1], smi[:, 1:2], 127.0, None, ALU.add))
                st(V.tensor_copy(smi[:, 3:4], sm[:, 0:1]))
                st(V.tensor_scalar(smi[:, 4:5], smi[:, 3:4], 7, None, ALU.logical_shift_right))
                st(V.tensor_copy(sm[:, 1:2], smi[:, 2:3]), False)
                st(V.tensor_copy(sm[:, 2:3], smi[:, 4:5]), False)
                st(V.memset(sm[:, 4:5], 1.0))
                st(V.tensor_tensor(sm[:, 3:4], sm[:, 2:3], sm[:, 1:2], ALU.subtract))
                st(V.scalar_tensor_tensor(out=sm[:, 5:6], in0=sm[:, 3:4], scalar=64.0, in1=bcol[0:BINS, :],
                                          op0=ALU.mult, op1=ALU.add))
                st(V.tensor_scalar(mb[:], ones[0:BINS, 0:BINS], sm[:, 5:6], None, ALU.mult))
                assert nS[0] == SCHED_B
                yield
                dve.wait_ge(s["sched_pe"], 2)
                st(V.tensor_scalar(Lm[:], PL[0:BINS, 0, 0:BINS], sm[:, 5:6], None, ALU.is_gt))
                yield
                dve.wait_ge(s["sched_pe"], 3)
                st(V.tensor_copy(sm[:, 6:8], PL[0:BINS, 1, 0:2]))
                st(V.tensor_tensor(sm[:, 8:9], sm[:, 6:7], sm[:, 3:4], ALU.add), False)
                st(V.tensor_tensor(sm[:, 9:10], sm[:, 1:2], sm[:, 6:7], ALU.subtract), False)
                st(V.tensor_scalar(Rm[:], iota_row[0:BINS, 0:BINS], sm[:, 7:8], None, ALU.is_equal), False)
                st(V.tensor_scalar(bbc[:], ones[0:BINS, :], bcol[0:BINS, :], None, ALU.mult))
                st(V.tensor_scalar(dbc[:], ones[0:BINS, :], sm[:, 9:10], None, ALU.mult), False)
                st(V.tensor_scalar(Mm[0:BINS, :], iotk[0:BINS, :], sm[:, 6:7], None, ALU.is_ge))
                st(V.scalar_tensor_tensor(out=Mm[0:BINS, :], in0=iotk[0:BINS, :], scalar=sm[:, 8:9],
                                          in1=Mm[0:BINS, :], op0=ALU.is_lt, op1=ALU.mult))
                assert nS[0] == SCHED_M
                yield
                dve.wait_ge(s["sched_pe"], 4)
                for i in range(2):
                    st(V.tensor_copy(bk[:, i * HE:(i + 1) * HE], PT[:, i, 0:HE]), False)
                    st(V.tensor_tensor(tk[:, i * HE:(i + 1) * HE], iotk[:, i * HE:(i + 1) * HE],
                                       (PN, PL)[i][:].rearrange("p a d -> p (a d)")[:, 0:HE], ALU.add), False)
                dve.wait_ge(s["sched_dve"], nS[0])
                st(V.tensor_scalar(bofs[0:1, :, 0:EPC], bk[0:1, :].rearrange("p (c m) -> p c m", m=EPC), float(D),
                                   None, ALU.mult))
                assert nS[0] == SCHED_T
                yield
                dve.wait_ge(s["sched_pe"], 5)
                st(V.tensor_copy(ordi[0:1, 0:BINS], PN[0:1, 0, 0:BINS]))
                for blk in range(NBLK):
                    V.tensor_scalar(PmA[:, blk * SLOTS:(blk + 1) * SLOTS], tk[:, 0:SLOTS], pcol[:, blk:blk + 1], None,
                                    ALU.is_equal).then_inc(s["firsts"], 1)
                for blk in range(2):
                    V.tensor_scalar(Pm[blk % 2], tk[:, SLOTS:], pcol[:, blk:blk + 1], None,
                                    ALU.is_equal).then_inc(s["select"], 1)
                yield

            def partition_signs():
                dve.wait_ge(s["consts"], 18)
                V.tensor_scalar(gray[:, 0:1], pidx[:], 1, None, ALU.logical_shift_right).then_inc(s["diag"], 1)
                dve.wait_ge(s["diag"], 1)
                V.tensor_tensor(gray[:, 1:2], gray[:, 0:1], pidx[:], ALU.bitwise_xor).then_inc(s["diag"], 1)
                V.tensor_scalar(gray[:, 2:3], pidx[:], 1, None, ALU.bitwise_and).then_inc(s["diag"], 1)
                dve.wait_ge(s["diag"], 3)
                for j in range(7):
                    V.tensor_scalar(gray[:, 3 + j:4 + j], gray[:, 1:2], j, 1, ALU.logical_shift_right,
                                    ALU.bitwise_and).then_inc(s["diag"], 1)
                dve.wait_ge(s["diag"], 10)
                V.tensor_scalar(sgn[:], gray[:, 2:10], -2.0, 1.0, ALU.mult, ALU.add).then_inc(s["diag"], 1)
                dve.wait_ge(s["diag"], 11)
                for j in range(7):
                    V.tensor_scalar(dsg[:, j, :], ident[:], sgn[:, 1 + j:2 + j], None, ALU.mult).then_inc(s["diag"], 1)

            def last_step(src_, dst_, m):
                for hf in range(2):
                    a = src_[:, hf * 512:hf * 512 + 512].rearrange("p (b m) -> p b m", m=m)
                    o = dst_[:, hf * 512:hf * 512 + 512].rearrange("p (b m) -> p b m", m=m)
                    h = m // 2
                    V.tensor_tensor(o[:, :, 0:h], a[:, :, 0:h], a[:, :, h:m], ALU.min).then_inc(s["sorted_step"], 1)
                    V.tensor_tensor(o[:, :, h:m], a[:, :, h:m], a[:, :, 0:h], ALU.max).then_inc(s["sorted_step"], 1)
                    cnt_[0] += 2
                    turn_at.append(cnt_[0])
                dve.wait_ge(s["sorted_step"], cnt_[0])

            for level in range(1, 11):
                m = 1 << level
                width = -(-EF // m) * m
                if level == 6:
                    partition_signs()
                if level == 10:
                    V.tensor_scalar(keyf[1 - cur[0]], keyf[cur[0]], sgn[:, 0:1], None, ALU.mult).then_inc(s["sorted_step"], 1)
                    cnt_[0] += 1
                    dve.wait_ge(s["sorted_step"], cnt_[0])
                    cur[0] = 1 - cur[0]
                d = m
                while d >= 2:
                    if level == 10 and d == 2:
                        last_step(keyf[cur[0]], keyf[1 - cur[0]], 2)
                    else:
                        halves(keyf[cur[0]], keyf[1 - cur[0]], width, d, d == m)
                    cur[0] = 1 - cur[0]
                    d //= 2
            pieces = schedule()
            for j in range(1, 8):
                for hf in range(2):
                    dve.wait_ge(s["turned"], 4 * (j - 1) + hf + 1)
                    part = slice(hf * 512, hf * 512 + 512)
                    a = PA[:, hf, :].rearrange("p (b m) -> p b m", m=1 << j)
                    o = keyf[1 - cur[0]][:, part].rearrange("p (b m) -> p b m", m=1 << j)
                    h = 1 << (j - 1)
                    low = khalf[:, hf * 256:hf * 256 + 256].rearrange("p (b m) -> p b m", m=h)
                    V.tensor_copy(low, a[:, :, 0:h]).then_inc(s["sorted_step"], 1)
                    cnt_[0] += 1
                    dve.wait_ge(s["sorted_step"], cnt_[0])
                    compare(low, a[:, :, h:2 * h], o[:, :, 0:h], o[:, :, h:2 * h])
                    if j == 1:
                        turn_at.append(cnt_[0])
                cur[0] = 1 - cur[0]
                for d in range(j - 1, 0, -1):
                    if d == 1:
                        last_step(keyf[cur[0]], keyf[1 - cur[0]], 2)
                    else:
                        halves(keyf[cur[0]], keyf[1 - cur[0]], SW, 1 << d, False)
                    cur[0] = 1 - cur[0]
                if j == 4:
                    dve.wait_ge(s["xsd_ready"], 1)
                    V.reciprocal(xrs[:], xsd[:]).then_inc(s["xrs_ready"], 1)
                if j in (5, 7):
                    next(pieces)
                o = keyf[1 - cur[0]]
                dve.wait_ge(s["turned"], 4 * (j - 1) + 3)
                V.tensor_copy(khalf[:], PB[:, 0, :]).then_inc(s["sorted_step"], 1)
                cnt_[0] += 1
                dve.wait_ge(s["sorted_step"], cnt_[0])
                dve.wait_ge(s["turned"], 4 * (j - 1) + 4)
                compare(khalf[:], PB[:, 1, :], o[:, 0:512], o[:, 512:SW])
                cur[0] = 1 - cur[0]
                for d in range(9, 0, -1):
                    if d == 1 and j < 7:
                        last_step(keyf[cur[0]], keyf[1 - cur[0]], 2)
                    else:
                        halves(keyf[cur[0]], keyf[1 - cur[0]], SW, 1 << d, False)
                    cur[0] = 1 - cur[0]
                if j == 1:
                    batch_norm()
                if 4 <= j < 7:
                    next(pieces)
            turn_at.append(cnt_[0])
            assert cur[0] == SORTED_IN

            def onehots(c2, par, pair):
                m0, m1 = PAIRS[pair][0], PAIRS[pair][-1] + 1
                k = c2 * SLOTS + (par * EPC + m0)
                V.tensor_tensor(onehot[:, par, m0:m1, :], iota_row[:].unsqueeze(1).broadcast_to([P, m1 - m0, P]),
                                srel[:, bass.ds(k, m1 - m0)].unsqueeze(2).broadcast_to([P, m1 - m0, P]),
                                ALU.is_equal).then_inc(s["oh_ready"], 1)

            pati = pat.bitcast(I32)
            dve.wait_ge(s["sched_pe"], 6)
            V.tensor_copy(pat[:, 0:SLOTS], PL[:, 1, 0:SLOTS]).then_inc(s["firsts"], 1)
            dve.wait_ge(s["firsts"], NBLK + 1)
            V.tensor_scalar(dsti[:, 0:SLOTS], pati[:, 0:SLOTS], MASK, None, ALU.bitwise_and).then_inc(s["firsts"], 1)
            dve.wait_ge(s["firsts"], NBLK + 2)
            V.tensor_scalar(dsti[:, 0:SLOTS], dsti[:, 0:SLOTS], N - 1, None, ALU.min).then_inc(s["first_ready"], 1)
            first_columns = slice(0, SLOTS)
            V.tensor_scalar(srcs[:, first_columns].bitcast(I32), pati[:, first_columns], BITS, MASK,
                            ALU.logical_shift_right, ALU.bitwise_and).then_inc(s["firsts"], 1)
            dve.wait_ge(s["firsts"], NBLK + 3)
            V.tensor_copy(srcs[:, first_columns], srcs[:, first_columns].bitcast(I32)).then_inc(s["firsts"], 1)
            dve.wait_ge(s["firsts"], NBLK + 4)
            V.scalar_tensor_tensor(out=srel[:, first_columns], in0=bk[:, first_columns], scalar=-float(P),
                                   in1=srcs[:, first_columns], op0=ALU.mult, op1=ALU.add).then_inc(s["firsts"], 1)
            for i in range(4):
                dve.wait_ge(s[f"nst_stored{i}"], 16 * ((BINS - 1 - i) // 4 + 1))
            for blk in range(2, NBLK):
                dve.wait_ge(s["sched_pe"], 6 + blk - 1)
                V.tensor_scalar(Pm[blk % 2], tk[:, SLOTS:], pcol[:, blk:blk + 1], None,
                                ALU.is_equal).then_inc(s["select"], 1)
                if blk == 3:
                    dve.wait_ge(s["firsts"], NBLK + 5)
                for pair in {3: (0, 1), 4: (2, 3), 5: (4,)}.get(blk, ()):
                    onehots(0, 0, pair)
            dve.wait_ge(s["sched_pe"], 6 + NBLK)
            for i in range(2):
                V.tensor_copy(pat[:, SLOTS + i * RE:SLOTS + (i + 1) * RE], PT[:, i, 0:RE]).then_inc(s["select"], 1)
            dve.wait_ge(s["select"], NBLK + 2)
            V.tensor_scalar(dsti[:, SLOTS:], pati[:, SLOTS:], MASK, None, ALU.bitwise_and).then_inc(s["select"], 1)
            dve.wait_ge(s["select"], NBLK + 3)
            V.tensor_scalar(dsti[:, SLOTS:], dsti[:, SLOTS:], N - 1, None, ALU.min).then_inc(s["ord_ready"], 1)

            def other_rows():
                V.tensor_scalar(srcs[:, SLOTS:].bitcast(I32), pati[:, SLOTS:], BITS, MASK, ALU.logical_shift_right,
                                ALU.bitwise_and).then_inc(s["select"], 1)
                dve.wait_ge(s["select"], NBLK + 4)
                V.tensor_copy(srcs[:, SLOTS:], srcs[:, SLOTS:].bitcast(I32)).then_inc(s["select"], 1)
                dve.wait_ge(s["select"], NBLK + 5)
                V.scalar_tensor_tensor(out=srel[:, SLOTS:], in0=bk[:, SLOTS:], scalar=-float(P), in1=srcs[:, SLOTS:],
                                       op0=ALU.mult, op1=ALU.add).then_inc(s["select"], 1)
                dve.wait_ge(s["select"], NBLK + 6)

            regs = [None]

            def load_bins(c2, par):
                _, regs[0] = nc.values_load_multi_w_load_instructions(
                    bofs[0:1, bass.ds(c2 * 2 + par, 1), 0:EPC].rearrange("p c m -> p (c m)"), engines=[ENG.DVE],
                    min_val=0, max_val=(BINS - 1) * D,
                    skip_runtime_bounds_check_because=IN_RANGE)

            def add_pair(c2, par, pair, nxt, banks=1):
                bank = PL if banks == 2 and pair % 2 else PN
                k = par * EPC + PAIRS[pair][0]
                dve.wait_ge(s["ent_done"], c2 * SLOTS + (k + len(PAIRS[pair])))
                for i, m in enumerate(PAIRS[pair]):
                    if i and nxt:
                        onehots(c2 + par, 1 - par, pair)
                    if not (isinstance(c2, int) and c2 * SLOTS + k + i == 0):
                        dve.wait_ge(s["acc_done"], c2 * SLOTS + (k + i))
                    to = accf[:, bass.ds(regs[0][m], D)]
                    V.tensor_tensor(to, to, bank[:, i, :], ALU.add).then_inc(s["acc_done"], 1)
                if nxt and len(PAIRS[pair]) == 1:
                    onehots(c2 + par, 1 - par, pair)

            def own(ins, wait=True):
                ins.then_inc(s["own"], 1)
                count[0] = count[0] + 1
                if wait:
                    dve.wait_ge(s["own"], count[0])

            count = [0]

            def linear_add(g, T, par):
                count[0] = g * OWN
                dve.wait_ge(s[f"xt_in{par}"], (g // 2 if isinstance(g, int) else half_of[0]) * (16 * GT) + 16 * T)
                dve.wait_ge(s["lin_done"], g + 1)
                for i in range(T):
                    own(V.tensor_tensor(xt[:, par, i, :], xt[:, par, i, :], PT[:, i // 2, (i % 2) * D:(i % 2) * D + D],
                                        ALU.add), i == T - 1)

            def statistics(g, T, par, half):
                for i in range(*{0: (0, T // 2), 1: (T // 2, 3 * T // 4), 2: (3 * T // 4, T)}[half]):
                    own(V.bn_stats(stat[:, i, :], xt[:, par, i, :]), i == T - 1)
                if half < 2:
                    return
                own(V.memset(idle[:, 0:1], 0.0), False)
                for i in range(T):
                    ins = V.bn_aggr(mv[:, i, :], stat[:, i, :])
                    if i == T - 1:
                        ins.then_inc(s["var_ready"], 1)

            def shift(g, T):
                dve.wait_ge(s["sd_ready"], g + 1)
                own(V.reciprocal(rstd[:, 0:T], sd[:, 0:T]))
                V.scalar_tensor_tensor(out=nmr[:, 0:T], in0=mv[:, 0:T, 0], scalar=-1.0, in1=rstd[:, 0:T],
                                       op0=ALU.mult, op1=ALU.mult).then_inc(s["nmr_ready"], 1)

            def y_low(g, T, par, k):
                w = T * P
                dve.wait_ge(s["yhi_ready"], g * KD + k + 1)
                V.tensor_tensor(yT[:, par, 1, k, 0:w], PT[:, k, 0:w], yT[:, par, 0, k, 0:w],
                                ALU.subtract).then_inc(s["ylo_ready"], 1)

            def maxima(g, T):
                dve.wait_ge(s["lg_done"], g + 1)
                for i in range(T):
                    own(V.scalar_tensor_tensor(out=lg[:, i, :], in0=PT[:, 0, i * EX:(i + 1) * EX], scalar=1.0 / WS,
                                               in1=brb[:], op0=ALU.mult, op1=ALU.add), i == T - 1)
                own(V.tensor_reduce(mx[:, 0:T], lg[:, 0:T, :], AX.X, ALU.max))
                V.tensor_scalar(nmx[:, 0:T], mx[:, 0:T], -1.0, None, ALU.mult).then_inc(s["max_ready"], 1)

            def router(g, T, par):
                count[0] = g * OWN + ((OWN if T == GT else OWN_LAST) - (T + 3))
                dve.wait_ge(s["ex_ready"], g * GT + T)
                own(V.reciprocal(er[:, 0:T], es[:, 0:T]))
                for i in range(T):
                    own(V.tensor_scalar(wn[:, i, :], ew[:, i, :], er[:, i:i + 1], None, ALU.mult), i == T - 1)

            def router_parts(g, T, par):
                if not first_group(g):
                    dve.wait_ge(s["wT_done"], g)
                own(V.tensor_copy(wh[:, 0:T, :], wn[:, 0:T, :]), False)
                own(V.tensor_scalar(w64[:, par, 0:T, :], wn[:, 0:T, :], 1.0 / WS, None, ALU.mult))
                V.tensor_tensor(w3[:, 0:T, EX:2 * EX], wn[:, 0:T, :], wh[:, 0:T, :], ALU.subtract).then_inc(s["w_ready"], 1)
                for i in (0, 2):
                    V.tensor_copy(w3[:, 0:T, i * EX:(i + 1) * EX], wh[:, 0:T, :]).then_inc(s["w_ready"], 1)

            def biases(g, T, par, half):
                dve.wait_ge(s["bo_done"], g + 1)
                dve.wait_ge(s["y3_added"], thirds(g, 0, half))
                for i in range(2 * half, min(2 * half + 2, T)):
                    ins = V.tensor_tensor(xt[:, par, i, :], xt[:, par, i, :],
                                          PT[:, half, (i % 2) * D:(i % 2) * D + D], ALU.add)
                ins.then_inc(s["bo_added"], 1)

            half_of = [None]

            def lo1(g, e, T, h):
                w = T * P
                dve.wait_ge(s["z1_ready"], g * 2 * EX + 2 * e + h + 1)
                V.tensor_tensor(h1[:, e % 2, 1, h, 0:w], zz[:, 0, h, 0:w], h1[:, e % 2, 0, h, 0:w],
                                ALU.subtract).then_inc(s["lo1_ready"], 1)

            def lo2(g, e, T, h):
                w = T * P
                dve.wait_ge(s["z2_ready"], g * 2 * EX + 2 * e + h + 1)
                V.tensor_tensor(h2[:, e % 2, 1, h, 0:w], zz[:, 1, h, 0:w], h2[:, e % 2, 0, h, 0:w],
                                ALU.subtract).then_inc(s["lo2_ready"], 1)

            def weigh(g, e, T, par, half):
                if T < GT and half:
                    return
                dve.wait_ge(s["l3_done"], thirds(g, e, half))
                if e == 1:
                    dve.wait_ge(s["bo_added"], g * 2 + (half + 1))
                if e == 0:
                    dve.wait_ge(s["own"], (g + 1) * OWN - (OWN - OWN_LAST if T < GT else 0))
                else:
                    dve.wait_ge(s["y3_added"], thirds(g, e - 1, half))
                for i in range(2 * half, min(2 * half + 2, T)):
                    ins = V.scalar_tensor_tensor(out=xt[:, par, i, :], in0=PL[:, i % 2, :], scalar=w64[:, par, i, e:e + 1],
                                                 in1=xt[:, par, i, :], op0=ALU.mult, op1=ALU.add)
                ins.then_inc(s["y3_added"], 1)

            def chunk(c2, par, between=None):
                load_bins(c2, par)
                for pair in range(len(PAIRS)):
                    add_pair(c2, par, pair, True, 2)
                    if between and pair in between:
                        between[pair]()

            chunk(0, 0)
            other_rows()
            chunk(0, 1)
            with dve.Fori(1, PRO // 2 - 2) as c2:
                chunk(c2, 0)
                chunk(c2, 1)
            C2 = PRO // 2 - 2
            chunk(C2, 0)
            chunk(C2, 1, {3: lambda: linear_add(0, GT, 0), 4: lambda: [statistics(0, GT, 0, h) for h in range(3)]})
            chunk(C2 + 1, 0, {0: lambda: shift(0, GT), 3: lambda: y_low(0, GT, 0, 0),
                                  4: lambda: y_low(0, GT, 0, 1)})
            chunk(C2 + 1, 1, {1: lambda: maxima(0, GT)})
            for h in range(2):
                lo1(0, 0, GT, h)

            def group(g, T, par, after, chunks, prev):
                for e in range(EX):
                    c2, cp = PRO // 2 + g * (EX // 2) + e // 2, e % 2
                    has = e < chunks
                    n_g, n_e, n_T = (g, e + 1, T) if e + 1 < EX else (g + 1, 0, after)
                    l_g, l_e, l_T, l_par = (g, e - 1, T, par) if e else (g - 1, EX - 1, prev, 1 - par)
                    nxt = has and (e + 1 < chunks or chunks == EX)
                    if has:
                        load_bins(c2, cp)
                        add_pair(c2, cp, 0, nxt)
                    if n_T:
                        lo1(n_g, n_e, n_T, 0)
                    if after and e == 5:
                        statistics(g + 1, after, 1 - par, 1)
                    if has:
                        add_pair(c2, cp, 1, nxt)
                    if n_T:
                        lo1(n_g, n_e, n_T, 1)
                    if e == 2:
                        biases(g, T, par, 0)
                    if after and e == 5:
                        statistics(g + 1, after, 1 - par, 2)
                    if after and e == 6:
                        y_low(g + 1, after, 1 - par, 0)
                    if after and e == 7:
                        maxima(g + 1, after)
                    if l_T:
                        weigh(l_g, l_e, l_T, l_par, 0)
                    if has:
                        add_pair(c2, cp, 2, nxt)
                    lo2(g, e, T, 0)
                    if e == 2 and T == GT:
                        biases(g, T, par, 1)
                    if after and e == 5:
                        shift(g + 1, after)
                    if after and e == 6:
                        y_low(g + 1, after, 1 - par, 1)
                    if after and e == 4:
                        linear_add(g + 1, after, 1 - par)
                    if has:
                        add_pair(c2, cp, 3, nxt)
                    if e == 0:
                        router(g, T, par)
                    if after and e == 4:
                        statistics(g + 1, after, 1 - par, 0)
                    lo2(g, e, T, 1)
                    if e == 0:
                        router_parts(g, T, par)
                    if has:
                        add_pair(c2, cp, 4, nxt)
                    if l_T:
                        weigh(l_g, l_e, l_T, l_par, 1)

            half_of[0] = None
            group(0, GT, 0, GT, EX, 0)
            with dve.Fori(0, (GROUPS - 4) // 2) as q:
                half_of[0] = q + 1
                group(2 * q + 1, GT, 1, GT, EX, GT)
                group(2 * q + 2, GT, 0, GT, EX, GT)
            group(GROUPS - 3, GT, 1, GT, EX, GT)
            group(GROUPS - 2, GT, 0, GT, 2, GT)
            group(GROUPS - 1, GT, 1, 1, 0, GT)
            group(GROUPS, 1, 0, 0, 0, GT)
            weigh(GROUPS, EX - 1, 1, 0, 0)

        @block.tensor
        def _(pe):
            T_ = nc.tensor
            pa, pb = [x_[:].rearrange("p a n -> p (a n)") for x_ in (PA, PB)]

            def prep():
                pe.wait_ge(s["gnnw_in"], 32)
                pe.wait_ge(s["consts"], 18)
                for k in range(KD):
                    for c in range(KH):
                        last = T_.transpose(PT[:, c // 2, (c % 2) * D + k * P:(c % 2) * D + k * P + P],
                                            gw1[:, k, c * P:(c + 1) * P], ident[:])
                last.then_inc(s["prep_pe"], 1)
                pe.wait_ge(s["prep_act"], KH + 1)
                for m in range(KD):
                    for c in range(KH):
                        T_.matmul(PN[:, m, :], w1T[:, c, m * P:(m + 1) * P], gw2[:, c, :], start=c == 0, stop=c == KH - 1)
                pe.wait_ge(s["small_in"], 16 * 16)
                for c in range(KH):
                    T_.matmul(PL[:, 0, :], b1b[:, c, :], gw2[:, c, :], start=c == 0, stop=False)
                T_.matmul(PL[:, 0, :], ones[0:1, :], b2r[:], start=False, stop=True)
                T_.matmul(PL[:, 1, 0:EX], ones[0:1, :], br1[:], start=True, stop=True).then_inc(s["prep_pe"], 1)
                pe.wait_ge(s["prep_dve"], 2)
                for l in range(2):
                    for q in range(2):
                        last = T_.transpose(PT[:, 0, (2 * l + q) * 16:(2 * l + q) * 16 + 16], prw[:, l, 2 + q, :],
                                            ident[0:2 * EX, 0:2 * EX])
                last.then_inc(s["prep_pe"], 1)

            upto = [0]

            def at(n):
                upto[0] = n
                return n

            def warm(bank):
                n = turn_at[sum(t <= upto[0] for t in turn_at)]
                if n - upto[0] < WARM_GAP:
                    return
                pe.wait_ge(s["sorted_step"], at(n - WARM_GAP + 2))
                for _ in range(WARM_N):
                    T_.matmul(bank[:, 0:P], ident[:], ones[:], start=True, stop=True)

            pe.wait_ge(s["diag"], 18)
            turn = iter(turn_at)
            cur = LOCAL_CUR
            for j in range(1, 8):
                warm(pa)
                for hf in range(2):
                    pe.wait_ge(s["sorted_step"], at(next(turn)))
                    for b in range(4 * hf, 4 * hf + 4):
                        last = T_.matmul(pa[:, b * P:(b + 1) * P], keyf[cur][:, b * P:(b + 1) * P], dsg[:, j - 1, :],
                                         start=True, stop=True)
                    last.then_inc(s["turned"], 1)
                if j == 5:
                    pe.wait_ge(s["sched_dve"], SCHED_B)
                    T_.matmul(PL[0:BINS, 0, 0:BINS], mb[:], ident[0:BINS, 0:BINS], start=True,
                              stop=True).then_inc(s["sched_pe"], 1)
                if j == 6:
                    pe.wait_ge(s["prep_act"], KH + 7)
                    pe.wait_ge(s["sched_dve"], SCHED_M)
                    for i in range(2):
                        T_.matmul(PT[:, i, 0:HE], bbc[:], Mm[0:BINS, i * HE:(i + 1) * HE], start=True, stop=True)
                        last = T_.matmul((PN, PL)[i][:].rearrange("p a d -> p (a d)")[:, 0:HE], dbc[:],
                                         Mm[0:BINS, i * HE:(i + 1) * HE], start=True, stop=True)
                    last.then_inc(s["sched_pe"], 1)
                if j == 7:
                    pe.wait_ge(s["sched_dve"], SCHED_T)
                    T_.matmul(PN[:, 0, 0:BINS], bbc[:], Rm[:], start=True, stop=True).then_inc(s["sched_pe"], 1)
                cur = (cur + j) % 2
                warm(pb)
                for hf in range(2):
                    pe.wait_ge(s["sorted_step"], at(next(turn)))
                    for b in range(4 * hf, 4 * hf + 4):
                        last = T_.transpose(pb[:, b * P:(b + 1) * P], keyf[cur][:, b * P:(b + 1) * P], ident[:])
                    last.then_inc(s["turned"], 1)
                if j == 2:
                    prep()
                if j == 4:
                    pe.wait_ge(s["b12_ready"], 1)
                    pe.wait_ge(s["counted"], BINS + 1)
                    T_.matmul(PL[0:BINS, 0, 0:1], cnt[:, 0:BINS], ones[:, 0:1], start=True, stop=True)
                    T_.matmul(PL[0:BINS, 0, 1:2], cnt[:, 1:BINS + 1], ones[:, 0:1], start=True,
                              stop=True).then_inc(s["sched_pe"], 1)
                if j == 5:
                    pe.wait_ge(s["sched_dve"], SCHED_B + 1)
                    T_.matmul(PL[0:BINS, 1, 0:2], Lm[:], sm[:, 3:5], start=True, stop=True).then_inc(s["sched_pe"], 1)
            pe.wait_ge(s["firsts"], NBLK)
            warm(pb)
            pe.wait_ge(s["sorted_step"], next(turn))
            for blk in range(NBLK):
                last = T_.matmul(PL[:, 1, 0:SLOTS], keyf[SORTED_IN][:, blk * P:(blk + 1) * P],
                                 PmA[:, blk * SLOTS:(blk + 1) * SLOTS], start=blk == 0, stop=blk == NBLK - 1)
            last.then_inc(s["sched_pe"], 1)
            for blk in range(NBLK):
                pe.wait_ge(s["select"], blk + 1)
                for i in range(2):
                    last = T_.matmul(PT[:, i, 0:RE], keyf[SORTED_IN][:, blk * P:(blk + 1) * P],
                                     Pm[blk % 2][:, i * RE:(i + 1) * RE], start=blk == 0, stop=blk == NBLK - 1)
                last.then_inc(s["sched_pe"], 1)

            def entries(c2, par, pair, banks=1):
                bank = PL if banks == 2 and pair % 2 else PN
                early = 2 if banks == 2 and pair else 0
                pe.wait_ge(s["oh_ready"], c2 * (2 * len(PAIRS)) + (len(PAIRS) * par + pair + 1))
                for m in PAIRS[pair]:
                    k = par * EPC + m
                    pe.wait_ge(gat[k], c2 * 16 + 16)
                    if m == PAIRS[pair][0] and not (isinstance(c2, int) and c2 * SLOTS + k - early <= 0):
                        pe.wait_ge(s["acc_done"], c2 * SLOTS + (k - early))
                    T_.matmul(bank[:, m % 2, :], onehot[:, par, m, :], gbuf[:, k, 0:D], start=True, stop=False)
                    T_.matmul(bank[:, m % 2, :], onehot[:, par, m, :], gbuf[:, k, D:2 * D], start=False,
                              stop=True).then_inc(s["ent_done"], 1)

            def chunk(c2, par, between=None):
                for pair in range(len(PAIRS)):
                    entries(c2, par, pair, 2)
                    if between and pair in between:
                        between[pair]()

            def rows_T(g, T):
                pe.wait_ge(s["hs_ready"], g * GT + T)
                if not first_group(g):
                    pe.wait_ge(s["bo_added"], g * 2)
                for i in range(T):
                    for k in range(KD):
                        last = T_.transpose(PT[:, k, i * P:(i + 1) * P], hs[:, i, k * P:(k + 1) * P], ident[:])
                last.then_inc(s["hT_done"], 1)

            def linear(g, T):
                pe.wait_ge(s["hT_sb"], g * KD + KD)
                for i in range(T):
                    for k in range(KD):
                        last = T_.matmul(PT[:, i // 2, (i % 2) * D:(i % 2) * D + D], hT[:, k, i * P:(i + 1) * P],
                                         W12[:, k, :], start=k == 0, stop=k == KD - 1)
                last.then_inc(s["lin_done"], 1)

            def y_T(g, T):
                pe.wait_ge(s["y_ready"], g * GT + T)
                for i in range(T):
                    for k in range(KD):
                        last = T_.transpose(PT[:, k, i * P:(i + 1) * P], hs[:, i, k * P:(k + 1) * P], ident[:])
                last.then_inc(s["yT_done"], 1)

            def logits(g, T, par):
                pe.wait_ge(s["yhi_ready"], g * KD + KD)
                pe.wait_ge(s["ylo_ready"], g * KD + KD)
                for i in range(T):
                    n = 0
                    for k in range(KD):
                        for wp, yp in PASSES:
                            last = T_.matmul(PT[:, 0, i * EX:(i + 1) * EX], yT[:, par, yp, k, i * P:(i + 1) * P],
                                             wrs[:, k, wp, :], start=n == 0, stop=n == 5)
                            n += 1
                last.then_inc(s["lg_done"], 1)

            def weights_T(g, T):
                pe.wait_ge(s["w_ready"], g * 3 + 3)
                for i in range(T):
                    last = T_.transpose(PT[0:3 * EX, 0, i * P:(i + 1) * P], w3[:, i, :], ident[:])
                last.then_inc(s["wT_done"], 1)

            def biases(g, T):
                pe.wait_ge(s["wT_sb"], g + 1)
                for i in range(T):
                    last = T_.matmul(PT[:, i // 2, (i % 2) * D:(i % 2) * D + D], wT[:, i * P:(i + 1) * P], bo3[:],
                                     start=True, stop=True)
                last.then_inc(s["bo_done"], 1)

            def L1(g, e, T, par, h):
                w, x_ = T * P, g * EX + e
                if not (isinstance(x_, int) and x_ < 1):
                    pe.wait_ge(s["z1_ready"], 2 * x_ + (h - 1))
                n = 0
                for k in range(KD):
                    for wp, yp in PASSES:
                        last = T_.matmul(PA[:, h, 0:w], wsp[0][:, e, k, wp, h * P:(h + 1) * P], yT[:, par, yp, k, 0:w],
                                         start=n == 0, stop=n == 5)
                        n += 1
                last.then_inc(s["l1_done"], 1)

            def L2(g, e, T, h):
                w, x_ = T * P, g * EX + e
                if h == 0:
                    pe.wait_ge(s["z1_ready"], 2 * x_ + 2)
                    pe.wait_ge(s["lo1_ready"], 2 * x_ + 2)
                if not (isinstance(x_, int) and x_ < 1):
                    pe.wait_ge(s["z2_ready"], 2 * x_ + (h - 1))
                n = 0
                for k in range(KD):
                    for wp, yp in PASSES:
                        last = T_.matmul(PB[:, h, 0:w], wsp[1][:, e, k, wp, h * P:(h + 1) * P],
                                         h1[:, e % 2, yp, k, 0:w], start=n == 0, stop=n == 5)
                        n += 1
                last.then_inc(s["l2_done"], 1)

            def L3(g, e, T, half):
                if T < GT and half:
                    return
                pe.wait_ge(s["z2_ready"], g * (2 * EX) + (2 * e + 2))
                pe.wait_ge(s["lo2_ready"], g * (2 * EX) + (2 * e + 2))
                if not (isinstance(g, int) and g == 0 and e == 0 and half == 0):
                    pe.wait_ge(s["y3_added"], thirds(g, e, half) - 1)
                for i in range(2 * half, min(2 * half + 2, T)):
                    n = 0
                    for k in range(KD):
                        for wp, yp in PASSES:
                            last = T_.matmul(PL[:, i % 2, :], h2[:, e % 2, yp, k, i * P:(i + 1) * P],
                                             wsp[2][:, e, k, wp, :], start=n == 0, stop=n == 5)
                            n += 1
                last.then_inc(s["l3_done"], 1)

            chunk(0, 0)
            chunk(0, 1)
            with pe.Fori(1, PRO // 2 - 2) as c2:
                chunk(c2, 0)
                chunk(c2, 1)
            C2 = PRO // 2 - 2
            def first_logits():
                pe.wait_ge(s["wlo_ready"], NW)
                logits(0, GT, 0)

            chunk(C2, 0)
            chunk(C2, 1, {1: lambda: rows_T(0, GT), 3: lambda: linear(0, GT)})
            chunk(C2 + 1, 0, {3: lambda: y_T(0, GT)})
            chunk(C2 + 1, 1, {0: first_logits, 1: lambda: L1(0, 0, GT, 0, 0), 2: lambda: L1(0, 0, GT, 0, 1)})

            def group(g, T, par, after, chunks, prev):
                for e in range(EX):
                    c2, cp = PRO // 2 + g * (EX // 2) + e // 2, e % 2
                    has = e < chunks
                    n_g, n_e, n_T, n_par = (g, e + 1, T, par) if e + 1 < EX else (g + 1, 0, after, 1 - par)
                    l_g, l_e, l_T = (g, e - 1, T) if e else (g - 1, EX - 1, prev)
                    if n_T:
                        L1(n_g, n_e, n_T, n_par, 0)
                    if has:
                        entries(c2, cp, 0)
                    if after and e == 4:
                        rows_T(g + 1, after)
                    if n_T:
                        L1(n_g, n_e, n_T, n_par, 1)
                    if has:
                        entries(c2, cp, 1)
                    if e == 1:
                        weights_T(g, T)
                    if after and e == 6:
                        y_T(g + 1, after)
                    if e == 2:
                        biases(g, T)
                    if l_T:
                        L3(l_g, l_e, l_T, 0)
                    L2(g, e, T, 0)
                    if has:
                        entries(c2, cp, 2)
                    if after and e == 4:
                        linear(g + 1, after)
                    L2(g, e, T, 1)
                    if has:
                        entries(c2, cp, 3)
                    if l_T:
                        L3(l_g, l_e, l_T, 1)
                    if has:
                        entries(c2, cp, 4)
                    if after and e == 6:
                        logits(g + 1, after, 1 - par)

            group(0, GT, 0, GT, EX, 0)
            with pe.Fori(0, (GROUPS - 4) // 2) as q:
                group(2 * q + 1, GT, 1, GT, EX, GT)
                group(2 * q + 2, GT, 0, GT, EX, GT)
            group(GROUPS - 3, GT, 1, GT, EX, GT)
            group(GROUPS - 2, GT, 0, GT, 2, GT)
            group(GROUPS - 1, GT, 1, 1, 0, GT)
            group(GROUPS, 1, 0, 0, 0, GT)
            L3(GROUPS, EX - 1, 1, 0)


IN_RANGE = ("a bin is a sum of at most BINS - 1 ones of the schedule's masks, or the place of the one in a row "
            "of a permutation matrix, whatever the edges are")
PAIRS = [(0, 1), (2, 3), (4, 5), (6, 7), (8,)]
OWN = 4 * GT + 6
OWN_LAST = 4 + 6
SCHED_B = 11
SCHED_M = SCHED_B + 9
SCHED_T = SCHED_M + 5
W_FIRST = 12
WARM_GAP = 10
WARM_N = 10
LN_LAG = 3
PASSES = [(0, 0), (0, 1), (1, 0)]
LOCAL_CUR = 56 % 2
SORTED_IN = (56 + 28 + 70) % 2

def kernel(**inputs):
    import numpy as _np
    import concourse.bacc as _bacc
    from concourse import mybir as _mybir
    from concourse.bass_utils import run_bass_kernel_spmd as _run

    names = ["x", "src", "dst", "L0_gnn_W1", "L0_gnn_b1", "L0_gnn_W2", "L0_gnn_b2", "L0_ffn_Wr", "L0_ffn_br"]
    bn_names = ["L0_ffn_" + n for n in BN_NAMES]
    names += bn_names + ["L0_ffn_W1", "L0_ffn_W2", "L0_ffn_Wo", "L0_ffn_bo"]
    nc = _bacc.Bacc("TRN2", target_bir_lowering=False, num_devices=1)
    arrays, aps = {}, {}
    for name in names:
        a = _np.ascontiguousarray(inputs[name])
        arrays[f"in_{name}"] = a
        aps[name] = nc.dram_tensor(f"in_{name}", a.shape, _mybir.dt.from_np(a.dtype), kind="ExternalInput").ap()
    out = nc.dram_tensor("out_0", (NPAD, D), _mybir.dt.float32, kind="ExternalOutput").ap()
    build(nc, *[aps[n] for n in names[:9]], [aps[n] for n in bn_names], *[aps[n] for n in names[-4:]], out)
    r = _run(nc, [arrays], core_ids=[0])
    return r.results[0]["out_0"][:N]
```
